# Optimizing a Trainium2 kernel written in Bass

```python
import numpy as np
import jax
import jax.numpy as jnp

def _softmax(x, axis=-1):
    return jax.nn.softmax(x, axis=axis)

def _gelu(x):
    return jax.nn.gelu(x, approximate=True)

def _silu(x):
    return jax.nn.silu(x)

def _sigmoid(x):
    return jax.nn.sigmoid(x)

def _layernorm(x, axis=-1, eps=1e-05):
    m = jnp.mean(x, axis=axis, keepdims=True)
    v = jnp.var(x, axis=axis, keepdims=True)
    return (x - m) / jnp.sqrt(v + eps)

def _scatter_add(tgt, idx, src, axis=0):
    return tgt.at[idx].add(src)

def _segment_sum(src, seg, n):
    return jax.ops.segment_sum(src, seg, n)
kernel_name = 'mk_conv_attn_hybrid_d4_conv_nchw128_r4_3234c6'

def setup_inputs(seed: int=0):
    np.random.seed(seed)
    _w = jnp.asarray

    def _rec_inputs():
        import jax
        import jax.numpy as jnp
        _gk = jax.random.key(seed)
        x = -0.0002928 + 1 * jax.random.normal(jax.random.fold_in(_gk, 1), (8, 32, 16, 16), jnp.float32)
        return x
    x = _rec_inputs()

    def _L0_conv_setup():
        import jax, jax.numpy as jnp
        from jax import lax
        import numpy as np
        K = 3
        STRIDE = 1
        PAD = 1
        DIL = 1

        def _deform_conv(x, w_off, b_off, w_dcn):
            B, C, H, W = x.shape
            Ho = (H + 2 * PAD - DIL * (K - 1) - 1) // STRIDE + 1
            Wo = (W + 2 * PAD - DIL * (K - 1) - 1) // STRIDE + 1
            KK = K * K
            offset = lax.conv_general_dilated(x, w_off, window_strides=(STRIDE, STRIDE), padding=[(PAD, PAD), (PAD, PAD)], rhs_dilation=(DIL, DIL), dimension_numbers=('NCHW', 'OIHW', 'NCHW'))
            offset = offset + b_off[None, :, None, None]
            off = offset.reshape(B, KK, 2, Ho, Wo)
            dy, dx = (off[:, :, 0], off[:, :, 1])
            ky, kx = jnp.meshgrid(jnp.arange(K), jnp.arange(K), indexing='ij')
            ky = (ky.reshape(-1) * DIL).astype(x.dtype)
            kx = (kx.reshape(-1) * DIL).astype(x.dtype)
            base_y = (jnp.arange(Ho) * STRIDE - PAD).astype(x.dtype)[None, :, None] + ky[:, None, None]
            base_x = (jnp.arange(Wo) * STRIDE - PAD).astype(x.dtype)[None, None, :] + kx[:, None, None]
            y = base_y[None] + dy
            xc = base_x[None] + dx
            y0 = jnp.floor(y)
            x0 = jnp.floor(xc)
            wy = y - y0
            wx = xc - x0
            y0i = y0.astype(jnp.int32)
            x0i = x0.astype(jnp.int32)

            def sample_one(xb, y0i, x0i, wy, wx):
                xf = xb.reshape(C, H * W)

                def corner(iy, ix):
                    valid = (iy >= 0) & (iy < H) & (ix >= 0) & (ix < W)
                    idx = jnp.clip(iy, 0, H - 1) * W + jnp.clip(ix, 0, W - 1)
                    v = jnp.take(xf, idx.reshape(-1), axis=1).reshape(C, KK, Ho, Wo)
                    return v * valid[None].astype(xb.dtype)
                v00 = corner(y0i, x0i)
                v01 = corner(y0i, x0i + 1)
                v10 = corner(y0i + 1, x0i)
                v11 = corner(y0i + 1, x0i + 1)
                return v00 * (1 - wy) * (1 - wx) + v01 * (1 - wy) * wx + v10 * wy * (1 - wx) + v11 * wy * wx
            sampled = jax.vmap(sample_one)(x, y0i, x0i, wy, wx)
            w = w_dcn.reshape(w_dcn.shape[0], C, KK)
            return jnp.einsum('bckhw,ock->bohw', sampled, w)
        key = jax.random.key(seed)
        k1, k2, k3, k4 = jax.random.split(key, 4)
        B, C, H, W, Co = (8, 32, 16, 16, 32)
        x = jax.random.normal(k1, (B, C, H, W), jnp.float32)
        w_off = jax.random.normal(k2, (2 * K * K, C, K, K), jnp.float32) * 0.01
        b_off = jax.random.normal(k3, (2 * K * K,), jnp.float32) * 0.01
        w_dcn = jax.random.normal(k4, (Co, C, K, K), jnp.float32) * (1.0 / np.sqrt(C * K * K))
        return {'x': x, 'w_off': w_off, 'b_off': b_off, 'w_dcn': w_dcn}
    _L0_conv_all = _L0_conv_setup()
    _L0_conv_in = {k: v for k, v in _L0_conv_all.items() if k in ('w_off', 'b_off', 'w_dcn')}
    del _L0_conv_all

    def _L1_conv_setup():
        import jax, jax.numpy as jnp
        import numpy as np
        from functools import partial
        IN_DIM = 32
        NUM_HEADS = 8
        DOWN_DIM = IN_DIM // 2
        HEAD_DIM = DOWN_DIM // NUM_HEADS
        MID = max(1, DOWN_DIM // 16)
        DIL = 3
        BN_EPS = 1e-05

        def conv2d(x, w, padding=0, dilation=1):
            return jax.lax.conv_general_dilated(x, w, window_strides=(1, 1), padding=[(padding, padding), (padding, padding)], rhs_dilation=(dilation, dilation), dimension_numbers=('NCHW', 'OIHW', 'NCHW'))

        def batchnorm(x, gamma, beta, mean, var):
            scale = (gamma / jnp.sqrt(var + BN_EPS))[None, :, None, None]
            shift = (beta - mean * gamma / jnp.sqrt(var + BN_EPS))[None, :, None, None]
            return x * scale + shift

        def complex_l2_norm(z, eps=1e-06):
            denom = jnp.sqrt(jnp.sum(z.real ** 2 + z.imag ** 2, axis=-1, keepdims=True) + eps)
            return z / denom

        def complex_softmax(z):
            return jax.lax.complex(jax.nn.softmax(z.real, axis=-1), jax.nn.softmax(z.imag, axis=-1))
        key = jax.random.key(seed)
        ks = jax.random.split(key, 6)
        B, H, W = (8, 32, 32)
        inp = {}
        inp['x'] = jax.random.normal(ks[0], (B, IN_DIM, H, W), dtype=jnp.float32)
        inp['conv_w'] = jax.random.normal(ks[1], (DOWN_DIM, IN_DIM, 3, 3), dtype=jnp.float32) * 0.02
        inp['bn1_g'] = jnp.ones((DOWN_DIM,), jnp.float32)
        inp['bn1_b'] = jnp.zeros((DOWN_DIM,), jnp.float32)
        inp['bn1_m'] = jnp.zeros((DOWN_DIM,), jnp.float32)
        inp['bn1_v'] = jnp.ones((DOWN_DIM,), jnp.float32)
        inp['cg1_w'] = jax.random.normal(ks[2], (MID, DOWN_DIM, 1, 1), dtype=jnp.float32) * 0.1
        inp['cg1_b'] = jnp.zeros((MID,), jnp.float32)
        inp['cgbn_g'] = jnp.ones((MID,), jnp.float32)
        inp['cgbn_b'] = jnp.zeros((MID,), jnp.float32)
        inp['cgbn_m'] = jnp.zeros((MID,), jnp.float32)
        inp['cgbn_v'] = jnp.ones((MID,), jnp.float32)
        inp['cg2_w'] = jax.random.normal(ks[3], (DOWN_DIM, MID, 1, 1), dtype=jnp.float32) * 0.1
        inp['cg2_b'] = jnp.zeros((DOWN_DIM,), jnp.float32)
        inp['tau'] = jnp.ones((NUM_HEADS, 1, 1), jnp.float32) * HEAD_DIM ** (-0.5)
        return inp
    _L1_conv_all = _L1_conv_setup()
    _L1_conv_in = {k: v for k, v in _L1_conv_all.items() if k in ('conv_w', 'bn1_g', 'bn1_b', 'bn1_m', 'bn1_v', 'cg1_w', 'cg1_b', 'cgbn_g', 'cgbn_b', 'cgbn_m', 'cgbn_v', 'cg2_w', 'cg2_b', 'tau')}
    del _L1_conv_all

    def _L2_attn_setup():
        import jax, jax.numpy as jnp
        import numpy as np
        HEADS = 8
        DIM_HEAD = 16
        LANDMARKS = 16
        PINV_ITERS = 6
        KERNEL = 33
        EPS_LN = 1e-05

        def moore_penrose_pinv(x, iters=PINV_ITERS):
            abs_x = jnp.abs(x)
            col = abs_x.sum(-1).max()
            row = abs_x.sum(-2).max()
            z = jnp.swapaxes(x, -1, -2) / (col * row)
            I = jnp.eye(x.shape[-1], dtype=x.dtype)
            for _ in range(iters):
                xz = x @ z
                z = 0.25 * (z @ (13.0 * I - xz @ (15.0 * I - xz @ (7.0 * I - xz))))
            return z
        key = jax.random.key(seed)
        ks = jax.random.split(key, 5)
        B, N, D = (2, 8192, 32)
        x = jax.random.normal(ks[0], (B, N, D), dtype=jnp.float32)
        ln_w = jnp.ones((D,), jnp.float32)
        ln_b = jnp.zeros((D,), jnp.float32)
        w_qkv = jax.random.normal(ks[1], (D, 3 * HEADS * DIM_HEAD), dtype=jnp.float32) * 0.05
        w_out = jax.random.normal(ks[2], (HEADS * DIM_HEAD, D), dtype=jnp.float32) * 0.05
        b_out = jnp.zeros((D,), jnp.float32)
        res_w = jax.random.normal(ks[3], (HEADS, 1, KERNEL, 1), dtype=jnp.float32) * 0.05
        return {'x': x, 'ln_w': ln_w, 'ln_b': ln_b, 'w_qkv': w_qkv, 'w_out': w_out, 'b_out': b_out, 'res_w': res_w}
    _L2_attn_all = _L2_attn_setup()
    _L2_attn_in = {k: v for k, v in _L2_attn_all.items() if k in ('ln_w', 'ln_b', 'w_qkv', 'w_out', 'b_out', 'res_w')}
    del _L2_attn_all

    def _L2_ffn_setup():
        import jax, jax.numpy as jnp
        import numpy as np
        B, S, D, E, H, O, K = (128, 512, 32, 16, 128, 32, 8)
        key = jax.random.key(seed)
        k0, k1, k2, k3 = jax.random.split(key, 4)
        x = jax.random.normal(k0, (B, S, D), dtype=jnp.float32)
        gate_w = jax.random.normal(k1, (E, D), dtype=jnp.float32) * (1.0 / np.sqrt(D))
        gate_b = jnp.zeros((E,), dtype=jnp.float32)
        weight1 = jax.random.uniform(k2, (E, D + 1, H), dtype=jnp.float32, minval=-1.0, maxval=1.0) * (1.0 / np.sqrt(D + 1))
        weight2 = jax.random.uniform(k3, (E, H + 1, O), dtype=jnp.float32, minval=-1.0, maxval=1.0) * (1.0 / np.sqrt(H + 1))
        return {'x': x, 'gate_w': gate_w, 'gate_b': gate_b, 'weight1': weight1, 'weight2': weight2}
    _L2_ffn_all = _L2_ffn_setup()
    _L2_ffn_in = {k: v for k, v in _L2_ffn_all.items() if k in ('gate_w', 'gate_b', 'weight1', 'weight2')}
    del _L2_ffn_all

    def _L3_attn_setup():
        import jax, jax.numpy as jnp
        import numpy as np
        B, N, D = (8, 512, 32)
        N_LAYER, N_HEAD = (4, 8)
        PARAMS_STD = 0.05

        def _attention(V, Q, Z):
            n = Z.shape[1]
            Attn = jnp.einsum('bni,ij,bmj->bnm', Z, Q, Z)
            values = jnp.einsum('ij,bnj->bni', V, Z)
            return jnp.einsum('bnm,bmi->bni', Attn, values) / n
        key = jax.random.key(seed)
        kz, kv, kq = jax.random.split(key, 3)
        Z = jax.random.normal(kz, (B, N, D), dtype=jnp.float32)
        v_matrix = PARAMS_STD * jax.random.normal(kv, (N_LAYER, N_HEAD, 1, D, D), dtype=jnp.float32)
        q_matrix = PARAMS_STD * jax.random.normal(kq, (N_LAYER, N_HEAD, 1, D, D), dtype=jnp.float32)
        return {'Z': Z, 'v_matrix': v_matrix, 'q_matrix': q_matrix}
    _L3_attn_all = _L3_attn_setup()
    _L3_attn_in = {k: v for k, v in _L3_attn_all.items() if k in ('v_matrix', 'q_matrix')}
    del _L3_attn_all

    def _L3_ffn_setup():
        import jax, jax.numpy as jnp
        import numpy as np
        NB, NOPS = (33, 19)
        D, H = (32, 128)
        B, S = (8, 256)
        CARRY_OPS = [0, 1, 2, 10, 11, 12, 13]

        def _build_masks():
            am = np.zeros((NB, NOPS), dtype=bool)
            fm = np.zeros((NB, NOPS), dtype=bool)
            fm[0, :] = True
            for b in range(1, 8):
                am[b, CARRY_OPS] = True
                fm[b, CARRY_OPS] = True
            am[8, [14, 15, 8, 9]] = True
            fm[8, [14, 15, 8, 9]] = True
            for b in range(16, 32):
                fm[b, [3, 4]] = True
            am[32, [10, 11, 12, 13]] = True
            fm[32, [5, 6, 7, 2, 4, 10, 11, 12, 13]] = True
            return (jnp.asarray(am), jnp.asarray(fm))
        key = jax.random.key(seed)
        ks = jax.random.split(key, 9)
        sd = 1.0 / np.sqrt(D)
        sh = 1.0 / np.sqrt(H)
        am, fm = _build_masks()
        return {'x': jax.random.normal(ks[0], (B, S, D), jnp.float32), 'ffn_w1': jax.random.normal(ks[1], (NB, NOPS, D, H), jnp.float32) * sd, 'ffn_b1': jnp.zeros((NB, NOPS, H), jnp.float32), 'ffn_w2': jax.random.normal(ks[2], (NB, NOPS, H, D), jnp.float32) * sh, 'ffn_b2': jnp.zeros((NB, NOPS, D), jnp.float32), 'wq': jax.random.normal(ks[3], (NB, NOPS, D, D), jnp.float32) * sd, 'wk': jax.random.normal(ks[4], (NB, NOPS, D, D), jnp.float32) * sd, 'wv': jax.random.normal(ks[5], (NB, NOPS, D, D), jnp.float32) * sd, 'wo': jax.random.normal(ks[6], (NB, NOPS, D, D), jnp.float32) * sd, 'attn_mask': am, 'ffn_mask': fm}
    _L3_ffn_all = _L3_ffn_setup()
    _L3_ffn_in = {k: v for k, v in _L3_ffn_all.items() if k in ('ffn_w1', 'ffn_b1', 'ffn_w2', 'ffn_b2', 'wq', 'wk', 'wv', 'wo', 'attn_mask', 'ffn_mask')}
    del _L3_ffn_all
    return {'x': x, 'L0_conv_w_off': _L0_conv_in['w_off'], 'L0_conv_b_off': _L0_conv_in['b_off'], 'L0_conv_w_dcn': _L0_conv_in['w_dcn'], 'L1_conv_conv_w': _L1_conv_in['conv_w'], 'L1_conv_bn1_g': _L1_conv_in['bn1_g'], 'L1_conv_bn1_b': _L1_conv_in['bn1_b'], 'L1_conv_bn1_m': _L1_conv_in['bn1_m'], 'L1_conv_bn1_v': _L1_conv_in['bn1_v'], 'L1_conv_cg1_w': _L1_conv_in['cg1_w'], 'L1_conv_cg1_b': _L1_conv_in['cg1_b'], 'L1_conv_cgbn_g': _L1_conv_in['cgbn_g'], 'L1_conv_cgbn_b': _L1_conv_in['cgbn_b'], 'L1_conv_cgbn_m': _L1_conv_in['cgbn_m'], 'L1_conv_cgbn_v': _L1_conv_in['cgbn_v'], 'L1_conv_cg2_w': _L1_conv_in['cg2_w'], 'L1_conv_cg2_b': _L1_conv_in['cg2_b'], 'L1_conv_tau': _L1_conv_in['tau'], 'L2_attn_ln_w': _L2_attn_in['ln_w'], 'L2_attn_ln_b': _L2_attn_in['ln_b'], 'L2_attn_w_qkv': _L2_attn_in['w_qkv'], 'L2_attn_w_out': _L2_attn_in['w_out'], 'L2_attn_b_out': _L2_attn_in['b_out'], 'L2_attn_res_w': _L2_attn_in['res_w'], 'L2_ffn_gate_w': _L2_ffn_in['gate_w'], 'L2_ffn_gate_b': _L2_ffn_in['gate_b'], 'L2_ffn_weight1': _L2_ffn_in['weight1'], 'L2_ffn_weight2': _L2_ffn_in['weight2'], 'L3_attn_v_matrix': _L3_attn_in['v_matrix'], 'L3_attn_q_matrix': _L3_attn_in['q_matrix'], 'L3_ffn_ffn_w1': _L3_ffn_in['ffn_w1'], 'L3_ffn_ffn_b1': _L3_ffn_in['ffn_b1'], 'L3_ffn_ffn_w2': _L3_ffn_in['ffn_w2'], 'L3_ffn_ffn_b2': _L3_ffn_in['ffn_b2'], 'L3_ffn_wq': _L3_ffn_in['wq'], 'L3_ffn_wk': _L3_ffn_in['wk'], 'L3_ffn_wv': _L3_ffn_in['wv'], 'L3_ffn_wo': _L3_ffn_in['wo'], 'L3_ffn_attn_mask': _L3_ffn_in['attn_mask'], 'L3_ffn_ffn_mask': _L3_ffn_in['ffn_mask']}

def reference(x, L0_conv_w_off, L0_conv_b_off, L0_conv_w_dcn, L1_conv_conv_w, L1_conv_bn1_g, L1_conv_bn1_b, L1_conv_bn1_m, L1_conv_bn1_v, L1_conv_cg1_w, L1_conv_cg1_b, L1_conv_cgbn_g, L1_conv_cgbn_b, L1_conv_cgbn_m, L1_conv_cgbn_v, L1_conv_cg2_w, L1_conv_cg2_b, L1_conv_tau, L2_attn_ln_w, L2_attn_ln_b, L2_attn_w_qkv, L2_attn_w_out, L2_attn_b_out, L2_attn_res_w, L2_ffn_gate_w, L2_ffn_gate_b, L2_ffn_weight1, L2_ffn_weight2, L3_attn_v_matrix, L3_attn_q_matrix, L3_ffn_ffn_w1, L3_ffn_ffn_b1, L3_ffn_ffn_w2, L3_ffn_ffn_b2, L3_ffn_wq, L3_ffn_wk, L3_ffn_wv, L3_ffn_wo, L3_ffn_attn_mask, L3_ffn_ffn_mask):
    import jax
    import jax.numpy as jnp

    def _L0_conv_ref(x, w_off, b_off, w_dcn):
        import jax, jax.numpy as jnp
        from jax import lax
        import numpy as np
        K = 3
        STRIDE = 1
        PAD = 1
        DIL = 1

        def _deform_conv(x, w_off, b_off, w_dcn):
            B, C, H, W = x.shape
            Ho = (H + 2 * PAD - DIL * (K - 1) - 1) // STRIDE + 1
            Wo = (W + 2 * PAD - DIL * (K - 1) - 1) // STRIDE + 1
            KK = K * K
            offset = lax.conv_general_dilated(x, w_off, window_strides=(STRIDE, STRIDE), padding=[(PAD, PAD), (PAD, PAD)], rhs_dilation=(DIL, DIL), dimension_numbers=('NCHW', 'OIHW', 'NCHW'))
            offset = offset + b_off[None, :, None, None]
            off = offset.reshape(B, KK, 2, Ho, Wo)
            dy, dx = (off[:, :, 0], off[:, :, 1])
            ky, kx = jnp.meshgrid(jnp.arange(K), jnp.arange(K), indexing='ij')
            ky = (ky.reshape(-1) * DIL).astype(x.dtype)
            kx = (kx.reshape(-1) * DIL).astype(x.dtype)
            base_y = (jnp.arange(Ho) * STRIDE - PAD).astype(x.dtype)[None, :, None] + ky[:, None, None]
            base_x = (jnp.arange(Wo) * STRIDE - PAD).astype(x.dtype)[None, None, :] + kx[:, None, None]
            y = base_y[None] + dy
            xc = base_x[None] + dx
            y0 = jnp.floor(y)
            x0 = jnp.floor(xc)
            wy = y - y0
            wx = xc - x0
            y0i = y0.astype(jnp.int32)
            x0i = x0.astype(jnp.int32)

            def sample_one(xb, y0i, x0i, wy, wx):
                xf = xb.reshape(C, H * W)

                def corner(iy, ix):
                    valid = (iy >= 0) & (iy < H) & (ix >= 0) & (ix < W)
                    idx = jnp.clip(iy, 0, H - 1) * W + jnp.clip(ix, 0, W - 1)
                    v = jnp.take(xf, idx.reshape(-1), axis=1).reshape(C, KK, Ho, Wo)
                    return v * valid[None].astype(xb.dtype)
                v00 = corner(y0i, x0i)
                v01 = corner(y0i, x0i + 1)
                v10 = corner(y0i + 1, x0i)
                v11 = corner(y0i + 1, x0i + 1)
                return v00 * (1 - wy) * (1 - wx) + v01 * (1 - wy) * wx + v10 * wy * (1 - wx) + v11 * wy * wx
            sampled = jax.vmap(sample_one)(x, y0i, x0i, wy, wx)
            w = w_dcn.reshape(w_dcn.shape[0], C, KK)
            return jnp.einsum('bckhw,ock->bohw', sampled, w)
        return _deform_conv(x, w_off, b_off, w_dcn)

    def _L1_conv_ref(x, conv_w, bn1_g, bn1_b, bn1_m, bn1_v, cg1_w, cg1_b, cgbn_g, cgbn_b, cgbn_m, cgbn_v, cg2_w, cg2_b, tau):
        import jax, jax.numpy as jnp
        import numpy as np
        from functools import partial
        IN_DIM = 32
        NUM_HEADS = 8
        DOWN_DIM = IN_DIM // 2
        HEAD_DIM = DOWN_DIM // NUM_HEADS
        MID = max(1, DOWN_DIM // 16)
        DIL = 3
        BN_EPS = 1e-05

        def conv2d(x, w, padding=0, dilation=1):
            return jax.lax.conv_general_dilated(x, w, window_strides=(1, 1), padding=[(padding, padding), (padding, padding)], rhs_dilation=(dilation, dilation), dimension_numbers=('NCHW', 'OIHW', 'NCHW'))

        def batchnorm(x, gamma, beta, mean, var):
            scale = (gamma / jnp.sqrt(var + BN_EPS))[None, :, None, None]
            shift = (beta - mean * gamma / jnp.sqrt(var + BN_EPS))[None, :, None, None]
            return x * scale + shift

        def complex_l2_norm(z, eps=1e-06):
            denom = jnp.sqrt(jnp.sum(z.real ** 2 + z.imag ** 2, axis=-1, keepdims=True) + eps)
            return z / denom

        def complex_softmax(z):
            return jax.lax.complex(jax.nn.softmax(z.real, axis=-1), jax.nn.softmax(z.imag, axis=-1))
        B, C, H, W = x.shape
        feat = conv2d(x, conv_w, padding=DIL, dilation=DIL)
        feat = batchnorm(feat, bn1_g, bn1_b, bn1_m, bn1_v)
        feat = jax.nn.gelu(feat, approximate=False)
        F2 = jnp.fft.fft2(feat.astype(jnp.float32), axes=(-2, -1))
        N = H * W
        qkv = F2.reshape(B, NUM_HEADS, HEAD_DIM, N)
        q = complex_l2_norm(qkv)
        k = complex_l2_norm(qkv)
        v = qkv
        attn = jnp.einsum('bhdn,bhen->bhde', q, jnp.conj(k)) * tau
        attn = complex_softmax(attn)
        out_f = jnp.einsum('bhde,bhen->bhdn', attn, v)
        out_f = out_f.reshape(B, DOWN_DIM, H, W)
        out_f = jnp.abs(jnp.fft.ifft2(out_f, axes=(-2, -1)))
        gr = F2.real
        cg = conv2d(gr, cg1_w) + cg1_b[None, :, None, None]
        cg = batchnorm(cg, cgbn_g, cgbn_b, cgbn_m, cgbn_v)
        cg = jax.nn.gelu(cg, approximate=False)
        cg = conv2d(cg, cg2_w) + cg2_b[None, :, None, None]
        cg = jax.nn.sigmoid(cg)
        gate = cg * F2
        gate = jnp.abs(jnp.fft.ifft2(gate, axes=(-2, -1)))
        y = jnp.concatenate([out_f, gate], axis=1)
        return y + x

    def _L2_attn_ref(x, ln_w, ln_b, w_qkv, w_out, b_out, res_w):
        import jax, jax.numpy as jnp
        import numpy as np
        HEADS = 8
        DIM_HEAD = 16
        LANDMARKS = 16
        PINV_ITERS = 6
        KERNEL = 33
        EPS_LN = 1e-05

        def moore_penrose_pinv(x, iters=PINV_ITERS):
            abs_x = jnp.abs(x)
            col = abs_x.sum(-1).max()
            row = abs_x.sum(-2).max()
            z = jnp.swapaxes(x, -1, -2) / (col * row)
            I = jnp.eye(x.shape[-1], dtype=x.dtype)
            for _ in range(iters):
                xz = x @ z
                z = 0.25 * (z @ (13.0 * I - xz @ (15.0 * I - xz @ (7.0 * I - xz))))
            return z
        b, n, dim = x.shape
        h, dh, m = (HEADS, DIM_HEAD, LANDMARKS)
        mu = x.mean(-1, keepdims=True)
        var = jnp.mean(jnp.square(x - mu), axis=-1, keepdims=True)
        xn = (x - mu) * jax.lax.rsqrt(var + EPS_LN) * ln_w + ln_b
        qkv = xn @ w_qkv
        q, k, v = jnp.split(qkv, 3, axis=-1)
        resh = lambda t: t.reshape(b, n, h, dh).transpose(0, 2, 1, 3)
        q, k, v = (resh(q), resh(k), resh(v))
        q = q * dh ** (-0.5)
        l = n // m
        q_l = q.reshape(b, h, m, l, dh).mean(axis=3)
        k_l = k.reshape(b, h, m, l, dh).mean(axis=3)
        sim1 = jnp.einsum('bhid,bhjd->bhij', q, k_l)
        sim2 = jnp.einsum('bhid,bhjd->bhij', q_l, k_l)
        sim3 = jnp.einsum('bhid,bhjd->bhij', q_l, k)
        a1 = jax.nn.softmax(sim1, axis=-1)
        a2 = jax.nn.softmax(sim2, axis=-1)
        a3 = jax.nn.softmax(sim3, axis=-1)
        a2_inv = moore_penrose_pinv(a2)
        out = a1 @ a2_inv @ (a3 @ v)
        pad = KERNEL // 2
        res = jax.lax.conv_general_dilated(v, res_w, window_strides=(1, 1), padding=((pad, pad), (0, 0)), dimension_numbers=('NCHW', 'OIHW', 'NCHW'), feature_group_count=h)
        out = out + res
        out = out.transpose(0, 2, 1, 3).reshape(b, n, h * dh)
        out = out @ w_out + b_out
        return x + out

    def _L2_ffn_ref(x, gate_w, gate_b, weight1, weight2):
        import jax, jax.numpy as jnp
        import numpy as np
        B, S, D, E, H, O, K = (128, 512, 32, 16, 128, 32, 8)
        Bn, Sn, Dn = x.shape
        logits = jnp.einsum('bsd,ed->bse', x, gate_w) + gate_b
        probs = jax.nn.softmax(logits, axis=1)
        vals, idx = jax.lax.top_k(probs.transpose(0, 2, 1), K)
        topv = vals.transpose(0, 2, 1)
        topi = idx.transpose(0, 2, 1)
        flat_idx = topi.reshape(Bn, K * E)
        gathered = jnp.take_along_axis(x, flat_idx[:, :, None], axis=1)
        gathered = gathered.reshape(Bn, K, E, Dn)
        pooled = jnp.einsum('bked,bke->bed', gathered, topv)
        ones = jnp.ones((E, Bn, 1), dtype=x.dtype)
        h = jnp.concatenate([pooled.transpose(1, 0, 2), ones], axis=-1)
        h = jax.nn.gelu(jnp.einsum('ebd,edh->ebh', h, weight1), approximate=False)
        h = jnp.concatenate([h, ones], axis=-1)
        out = jnp.einsum('ebh,eho->ebo', h, weight2)
        out = out.transpose(1, 0, 2)
        weighted = jnp.einsum('beo,bke->bkeo', out, topv).reshape(Bn, K * E, O)
        outputs = jnp.zeros((Bn, Sn, O), dtype=x.dtype)
        outputs = outputs.at[jnp.arange(Bn)[:, None], flat_idx].add(weighted)
        return outputs

    def _L3_attn_ref(Z, v_matrix, q_matrix):
        import jax, jax.numpy as jnp
        import numpy as np
        B, N, D = (8, 512, 32)
        N_LAYER, N_HEAD = (4, 8)
        PARAMS_STD = 0.05

        def _attention(V, Q, Z):
            n = Z.shape[1]
            Attn = jnp.einsum('bni,ij,bmj->bnm', Z, Q, Z)
            values = jnp.einsum('ij,bnj->bni', V, Z)
            return jnp.einsum('bnm,bmi->bni', Attn, values) / n
        n_layer, n_head = (v_matrix.shape[0], v_matrix.shape[1])
        for i in range(n_layer):
            Zi = Z
            residues = jnp.zeros_like(Zi)
            for j in range(n_head):
                Vij = v_matrix[i, j, 0]
                Qij = q_matrix[i, j, 0]
                residues = residues + _attention(Vij, Qij, Zi)
            Z = Zi + residues / n_head
        return Z

    def _L3_ffn_ref(x, ffn_w1, ffn_b1, ffn_w2, ffn_b2, wq, wk, wv, wo, attn_mask, ffn_mask):
        import jax, jax.numpy as jnp
        import numpy as np
        NB, NOPS = (33, 19)
        D, H = (32, 128)
        B, S = (8, 256)
        CARRY_OPS = [0, 1, 2, 10, 11, 12, 13]

        def _build_masks():
            am = np.zeros((NB, NOPS), dtype=bool)
            fm = np.zeros((NB, NOPS), dtype=bool)
            fm[0, :] = True
            for b in range(1, 8):
                am[b, CARRY_OPS] = True
                fm[b, CARRY_OPS] = True
            am[8, [14, 15, 8, 9]] = True
            fm[8, [14, 15, 8, 9]] = True
            for b in range(16, 32):
                fm[b, [3, 4]] = True
            am[32, [10, 11, 12, 13]] = True
            fm[32, [5, 6, 7, 2, 4, 10, 11, 12, 13]] = True
            return (jnp.asarray(am), jnp.asarray(fm))
        scale = jnp.asarray(1.0 / np.sqrt(D), x.dtype)

        def step(h, p):
            op = jnp.argmax(h[0, 0, :NOPS])
            q = h @ p['wq'][op]
            k = h @ p['wk'][op]
            v = h @ p['wv'][op]
            attn = jax.nn.softmax(jnp.einsum('bqd,bkd->bqk', q, k) * scale, axis=-1)
            y = jnp.einsum('bqk,bkd->bqd', attn, v) @ p['wo'][op]
            h = jnp.where(p['am'][op], y, h)
            z = jax.nn.relu(h @ p['w1'][op] + p['b1'][op]) @ p['w2'][op] + p['b2'][op]
            h = jnp.where(p['fm'][op], z, h)
            return (h, None)
        xs = {'w1': ffn_w1, 'b1': ffn_b1, 'w2': ffn_w2, 'b2': ffn_b2, 'wq': wq, 'wk': wk, 'wv': wv, 'wo': wo, 'am': attn_mask, 'fm': ffn_mask}
        out, _ = jax.lax.scan(step, x, xs)
        return out

    def _gn(v, G=32, eps=1e-05):
        B_, C_, H_, W_ = v.shape
        g = v.reshape(B_, G, C_ // G, H_, W_)
        m = jnp.mean(g, axis=(2, 3, 4), keepdims=True)
        s = jnp.var(g, axis=(2, 3, 4), keepdims=True)
        return ((g - m) / jnp.sqrt(s + eps)).reshape(v.shape)

    def _ln_c(v, eps=1e-06):
        m = jnp.mean(v, axis=1, keepdims=True)
        s = jnp.var(v, axis=1, keepdims=True)
        return (v - m) / jnp.sqrt(s + eps)

    def _ln_t(v, eps=1e-05):
        m = jnp.mean(v, axis=-1, keepdims=True)
        s = jnp.var(v, axis=-1, keepdims=True)
        return (v - m) / jnp.sqrt(s + eps)

    def _to_tokens(v):
        B_, C_, H_, W_ = v.shape
        return v.reshape(B_, C_, H_ * W_).transpose(0, 2, 1)

    def _from_tokens(t, like):
        B_, C_, H_, W_ = like.shape
        return t.transpose(0, 2, 1).reshape(B_, C_, H_, W_)
    x = x + _L0_conv_ref(_gn(x), L0_conv_w_off, L0_conv_b_off, L0_conv_w_dcn)
    x = _L1_conv_ref(x, L1_conv_conv_w, L1_conv_bn1_g, L1_conv_bn1_b, L1_conv_bn1_m, L1_conv_bn1_v, L1_conv_cg1_w, L1_conv_cg1_b, L1_conv_cgbn_g, L1_conv_cgbn_b, L1_conv_cgbn_m, L1_conv_cgbn_v, L1_conv_cg2_w, L1_conv_cg2_b, L1_conv_tau)
    t = _to_tokens(x)
    t = t + _L2_attn_ref(_ln_t(t), L2_attn_ln_w, L2_attn_ln_b, L2_attn_w_qkv, L2_attn_w_out, L2_attn_b_out, L2_attn_res_w)
    t = t + _L2_ffn_ref(_ln_t(t), L2_ffn_gate_w, L2_ffn_gate_b, L2_ffn_weight1, L2_ffn_weight2)
    t = t + _L3_attn_ref(_ln_t(t), L3_attn_v_matrix, L3_attn_q_matrix)
    t = t + _L3_ffn_ref(_ln_t(t), L3_ffn_ffn_w1, L3_ffn_ffn_b1, L3_ffn_ffn_w2, L3_ffn_ffn_b2, L3_ffn_wq, L3_ffn_wk, L3_ffn_wv, L3_ffn_wo, L3_ffn_attn_mask, L3_ffn_ffn_mask)
    x = _from_tokens(t, x)
    return x

_drawn_inputs = setup_inputs


def setup_inputs(seed=0):
    import zlib

    import numpy as np

    out = dict(_drawn_inputs(seed))
    spreads = {'L1_conv_bn1_g': (1.0, 0.539),
     'L1_conv_bn1_b': (0.0, 0.364),
     'L1_conv_bn1_m': (0.0, 0.1),
     'L1_conv_bn1_v': (1.0, 0.6),
     'L1_conv_cg2_b': (0.0, 2.0),
     'L1_conv_tau': (0.7071067690849304, 0.6),
     'L2_attn_ln_w': (1.0, 0.6),
     'L2_attn_ln_b': (0.0, 0.8),
     'L2_attn_b_out': (0.0, 0.1),
     'L2_ffn_gate_b': (0.0, 2.0),
     'L3_ffn_ffn_b1': (0.0, 0.365),
     'L3_ffn_ffn_b2': (0.0, 0.273)}
    factors = {'L0_conv_b_off': 4.848,
     'L1_conv_cg1_w': 8.0,
     'L1_conv_cg2_w': 8.0,
     'L2_attn_w_out': 2.723,
     'L2_attn_res_w': 2.863,
     'L2_ffn_gate_w': 8.0,
     'L2_ffn_weight1': 8.0,
     'L2_ffn_weight2': 8.0,
     'L3_attn_v_matrix': 2.933,
     'L3_attn_q_matrix': 2.927,
     'L3_ffn_wk': 3.586}
    for name, (base, spread) in spreads.items():
        noise = np.random.default_rng([zlib.crc32(name.encode()), seed]).standard_normal(out[name].shape)
        drawn = base * np.exp(spread * noise) if base else spread * noise
        out[name] = jnp.asarray(drawn.astype(out[name].dtype))
    for name, factor in factors.items():
        out[name] = (out[name] * factor).astype(out[name].dtype)
    return out
```

```python
from contextlib import ExitStack

import numpy as np

import concourse.bass as bass
from concourse import mybir
from concourse.alu_op_type import AluOpType as ALU

F32 = mybir.dt.float32
I32 = mybir.dt.int32
U32 = mybir.dt.uint32
ACT = mybir.ActivationFunctionType
AX = mybir.AxisListType

B, C, HH, WW = 8, 32, 16, 16
N = HH * WW
P = 128
BI, BG, PT = 4, 2, 2
KK = 9
NOFF = 2 * KK
CH = 16
HEADS, DH, LM = 8, 16, 16
PINV = 6
KRES = 33
EXP, HID = 16, 128
LAYERS, LHEADS = 4, 8
NB, NOPS = 33, 19
SMALL = 16 * (B + 1)
LATE = 16 * (BI + 7)

W32 = {}
_at = 0
for _n, _k in (("off", KK * NOFF), ("dcn", KK * C), ("conv", KK * CH), ("qkv", 3 * P), ("gate", EXP),
               ("v", LAYERS * LHEADS * C), ("q", LAYERS * LHEADS * C)):
    W32[_n] = (_at, _at + _k)
    _at += _k
W32_COLS = _at
W32_EARLY = W32["conv"][1]

CST = {}
_at = 0
for _n, _k in (("ident", P), ("flip", P), ("mask4", BI), ("mask8", HEADS), ("base", PT * NOFF), ("iota", 16),
               ("mask16", P), ("swap", P), ("eye", 48), ("dft", 2 * 3 * N)):
    CST[_n] = (_at, _at + _k)
    _at += _k
CST_COLS = _at

PAR = ("bn_g", "bn_b", "bn_m", "bn_v", "cg2_w", "cg2_b", "cg1_w", "cg1_b", "cgbn_g", "cgbn_b", "cgbn_m",
       "cgbn_v", "tau", "gate_b")
ROWS = {"b_off": (0, NOFF), "ln_w": (NOFF, NOFF + C), "ln_b": (NOFF + C, NOFF + 2 * C),
        "b_out": (NOFF + 2 * C, NOFF + 3 * C)}
ROW_COLS = NOFF + 3 * C
TOEP_PAD = 512

REC_A = HID + 4 * C + 1
REC_B = C + 1

SEMS = (
    "x_in", "cst_in", "w32_in", "par_in", "late_in",
    "pool_zero", "pool_bd", "gn_var", "gn_std", "xn", "off_mm", "g_mm", "g_ev", "diff", "hat",
    "prod", "tr", "s_ev", "gst", "dcn_mm", "x1_ready",
    "conv_mm", "bn_var", "bn_std", "bn_ready", "feat", "featT_mm", "featT_ev", "f2_mm", "f2_ev", "swap_mm",
    "l2_sum", "l2_std", "sm2_in", "sm2_exp", "mix", "mix_abs", "cg_mm", "cg_act", "gated", "gT_mm",
    "gT_ev", "inv_mm", "inv_sq", "inv_add", "inv_abs", "toT_mm", 
    "ln_var", "ln_std", "ct_in", "ct_mm", "ct_ev",
    "qk_mm", "q_ev", "k_ev", "pool_in", "lk_mm", "lk_ev", "ql_bd", "kl_bd", "v_mm", "v_ev", "sim2_mm",
    "sim3_mm", "a3_max", "a3_exp", "a3T_mm", "a3T_ev", "w3_mm", "w3_ev", "sim1_mm", "a1_sub", "a1_exp",
    "a1_norm", "a1_sum", "a1T_mm", "a1T_ev", "res_mm", "res_ev", "a2_sub", "a2_exp", "x_bd", "xT_mm", 
    "cr_in", "cr_max", "z_new", "zT_bd", "xz_mm", "t_ready", "t_mm", "z_mm", "w2_mm", "w2_ev",
    "oT_mm", "oT_evA", "oT_evD", "ao_mm",
    "lg_mm", "lg_max", "lg_exp", "topk", "mT_mm", "mT_ev", "pl_mm", "pl_ev", "hid_mm", "hid_ev", "eo_mm",
    "eo_ev", "eoT_mm", "eo_bd", "moe_mm",
    "la_z", "la_g", "la_gev", "la_h", "la_hev", "la_qbd", "la_r", "la_rev", "la_zmm", 
    "rt_h", "op_mm", "op_read", "op_ev", "w_in", "w_bd", "rq_mm", "rq_ev", "rk_ev", "rv_mm", "rv_ev", "sc_mm",
    "sc_max", "sc_exp", "sc_norm", "pT_mm", "pT_ev", "ro_mm", "ro_ev", "ry_mm",
    "f1_mm", "f1_evA", "f1_evD", "f2mm", "h_new", "out_ready", "out_st",
    "dve_own", "act_own", "pool_own", "passed",
)


class Own:

    def __init__(self, eng, sem):
        self.eng, self.sem, self.n = eng, sem, 0

    def link(self, ins):
        self.n += 1
        ins.then_inc(self.sem, 1)
        self.eng.wait_ge(self.sem, self.n)

    def restart(self):
        self.eng.sem_clear(self.sem)
        self.n = 0


def build(nc, x, cst, w32, par, rows, toep, w_out, moe_w1, moe_w2, moe_b2, am, fm, rec_a, rec_b, out):
    ctx = ExitStack()
    with ctx:
        def sb(name, cols, dt=F32, parts=P):
            return ctx.enter_context(nc.sbuf_tensor(name, [parts, cols], dt))[:, :]

        S = {n: ctx.enter_context(nc.semaphore(n)) for n in SEMS}
        ps = [ctx.enter_context(nc.psum_tensor(f"ps{i}", [P, 512], F32))[:, :] for i in range(8)]

        xC = sb("xC", 512)
        cstb = sb("cstb", CST_COLS)
        w32b = sb("w32b", W32_COLS)
        parb = sb("parb", len(PAR))
        rowb = sb("rowb", ROW_COLS)
        woutb = sb("woutb", C)
        w1b = sb("w1b", EXP * HID, parts=C + 1)
        w2b = sb("w2b", EXP * C)
        b2b = sb("b2b", EXP * C, parts=1)
        maskb = sb("maskb", NB * NOPS, I32, parts=1)
        flagb = sb("flagb", NB * NOPS, I32, parts=1)

        def cst_(n):
            return cstb[:, CST[n][0]:CST[n][1]]

        def w32_(n):
            return w32b[:, W32[n][0]:W32[n][1]]

        def par_(n):
            return parb[:, PAR.index(n):PAR.index(n) + 1]

        def row_(n):
            return rowb[:, ROWS[n][0]:ROWS[n][1]]

        ident, mask4, mask8, iota = cst_("ident"), cst_("mask4"), cst_("mask8"), cst_("iota")
        eye7, eye15, eye13 = (cst_("eye")[:, 16 * i:16 * i + 16] for i in range(3))
        dft = cst_("dft").rearrange("p (t n) -> p t n", t=PT)

        arena = sb("arena", 20480)

        def ar(at, cols):
            return arena[:, at:at + cols]

        xn3 = arena[:, 18208:18208 + BG * 3 * 18 * 16].rearrange("p (g s n) -> p g s n", g=BG, s=3)
        xp = sb("xp", BG * 22 * 22).rearrange("p (g y x) -> p g y x", g=BG, y=22)
        off_bd = sb("off_bd", KK * BI * NOFF).rearrange("p (k b o) -> p k b o", k=KK, b=BI)
        conv_bd = sb("conv_bd", KK * BI * CH).rearrange("p (k b o) -> p k b o", k=KK, b=BI)
        gate_bd = sb("gate_bd", BI * EXP).rearrange("p (b o) -> p b o", b=BI)
        cgw = sb("cgw", P)
        base2 = sb("base2", PT * NOFF).rearrange("p (t o) -> p t o", t=PT)
        zeros = sb("zeros", P)
        x1C = sb("x1C", 512)
        small = sb("small", 512)
        T = sb("T", 512)
        t0 = sb("t0", 512)
        ln_a = sb("ln_a", 512)
        ln_b = sb("ln_b", 512)
        lnC = sb("lnC", 512)
        tC = sb("tC", 512)
        T4 = T.rearrange("p (t b c) -> p t b c", t=PT, b=B)

        GS = ar(0, 4608).rearrange("p (g t b k o) -> p g t b k o", g=BG, t=PT, b=BI, k=KK)
        hat = ar(4608, 4608).rearrange("p (t b k a q) -> p t b k a q", t=PT, b=B, k=KK, a=2)
        ST = ar(9216, 4096).rearrange("p (c t y x) -> p c t y x", c=B, t=PT, y=HH)
        SQ = ar(13312, 4096).rearrange("p (c q n) -> p c q n", c=B, q=PT)
        yx = ar(17408, 288).rearrange("p (t b o) -> p t b o", t=PT, b=B)
        Gst = ar(17696, 512).rearrange("p (g t b o) -> p g t b o", g=BG, t=PT, b=BI)

        feat = sb("feat", N)
        featT = sb("featT", PT * P).rearrange("p (t n) -> p t n", t=PT)
        F2 = ar(18432, 2 * N)
        mixed = ar(18944, 2 * N)
        outf = sb("outf", N)
        gatef = sb("gatef", N)
        scr = sb("scr", 512)
        gated = ar(19456, 512)
        gT = ar(19968, 512).rearrange("p (a t n) -> p a t n", a=2, t=PT)
        cg = sb("cg", N)

        qT, kT, V, a1, a1T, a3, a3T, res, oT = (ar(2048 * i, 2048) for i in range(9))
        toepb = sb("toepb", HEADS * 384).rearrange("p (h n) -> p h n", h=HEADS)
        ql_bd, kl_bd, bdXT, bdz, bdzT, w3_bd = (
            sb(n, 1024).rearrange("p (b h m) -> p b h m", b=B, h=HEADS)
            for n in ("ql_bd", "kl_bd", "bdXT", "bdz", "bdzT", "w3_bd"))
        bdxzT, bdt, w2_bd = (a.rearrange("p (b h m) -> p b h m", b=B, h=HEADS)
                             for a in (a3[:, 0:1024], a3[:, 1024:2048], kT[:, 0:1024]))
        ql, kl, XM, XT, z, zT, tt = (sb(n, P).rearrange("p (b m) -> p b m", b=B)
                                     for n in ("ql", "kl", "XM", "XT", "z", "zT", "tt"))
        xpool = sb("xpool", BG * LM)

        probs = sb("probs", N)
        probs_rest = sb("probs_rest", N)
        mT = sb("mT", N).rearrange("p (t e) -> p t e", t=PT)
        pooled = sb("pooled", P, parts=C + 1)
        hid = sb("hid", EXP * B).rearrange("p (e b) -> p e b", e=EXP)
        eo = sb("eo", P, parts=C)
        eo_bd = sb("eo_bd", B * C).rearrange("p (b o) -> p b o", b=B)
        ones1 = sb("ones1", B, parts=1)

        ZT_, ZC = sb("ZT_", 512), sb("ZC", 512)
        g_bd = ar(12288, BG * P)
        hs = ar(12544, BG * LHEADS * C).rearrange("p (g j o) -> p g j o", g=BG, j=LHEADS)
        q_bd = ar(13312, LHEADS * P).rearrange("p (j b o) -> p j b o", j=LHEADS, b=BI)
        r_bd = ar(14336, BG * P)

        hC = sb("hC", 512)
        recA = sb("recA", REC_A)
        recB = sb("recB", REC_B)
        top8 = sb("top8", 8, parts=1)
        op8 = sb("op8", 8, U32, parts=1)
        w_bd = ar(0, 512)
        rq, rk, rv, ro, roC = (ar(512 * (1 + i), 512) for i in range(5))
        f1 = ar(3072, 2048)
        pr = ar(5120, 4096)
        prT = ar(9216, 4096)
        rmax = sb("rmax", 16)
        rsum = sb("rsum", 16)
        outC = ln_a

        def expand16(compact):
            return compact.unsqueeze(2).to_broadcast([P, compact.shape[1], HEADS, 16])

        def mask8_for(nb):
            return mask8.unsqueeze(1).unsqueeze(3).to_broadcast([P, nb, HEADS, 16])

        def window(buf, g, y0, x0, rows):
            return buf[:, g, y0:y0 + rows, x0:x0 + WW]

        def arr3(a, k):
            return a.rearrange("p (j k) -> p j k", k=k)

        def settled(eng):
            eng.sem_inc(S["passed"], 1)

        block = ctx.enter_context(nc.Block())

        @block.sync
        def _(sp):
            sp.dma_start(xC.rearrange("p (g n) -> p g n", g=BG),
                         x.rearrange("(g b) c n -> (b c) g n", g=BG)).then_inc(S["x_in"], 16)
            sp.dma_start(cstb, cst).then_inc(S["cst_in"], 16)
            for bi in range(BI):
                sp.dma_start(w32b[32 * bi:32 * bi + 32, 0:W32_EARLY], w32[:, 0:W32_EARLY]).then_inc(S["w32_in"], 16)
            sp.dma_start(rowb, rows.partition_broadcast(P)).then_inc(S["par_in"], 16)
            for b in range(B):
                sp.dma_start(parb[16 * b:16 * b + 16, :], par).then_inc(S["par_in"], 16)
            for bi in range(BI):
                sp.dma_start(w32b[32 * bi:32 * bi + 32, W32_EARLY:W32_COLS],
                             w32[:, W32_EARLY:W32_COLS]).then_inc(S["late_in"], 16)
            sp.dma_start(toepb, bass.AP(tensor=toep.tensor, offset=0, ap=[[1, P], [TOEP_PAD, HEADS], [1, 384]])
                         ).then_inc(S["late_in"], 16)
            sp.dma_start(woutb, w_out).then_inc(S["late_in"], 16)
            sp.dma_start(w1b.rearrange("d (e h) -> d e h", e=EXP), moe_w1).then_inc(S["late_in"], 16)
            sp.dma_start(w2b.rearrange("h (e o) -> h e o", e=EXP), moe_w2).then_inc(S["late_in"], 16)
            sp.dma_start(b2b, moe_b2).then_inc(S["late_in"], 16)
            sp.dma_start(maskb, am).then_inc(S["late_in"], 16)
            sp.dma_start(flagb, fm).then_inc(S["late_in"], 16)

            sp.sem_inc(S["op_read"], 1)
            with sp.Fori(0, NB) as s:
                sp.wait_ge(S["op_ev"], s + 1)
                settled(sp)
                op = sp.value_load(op8[0:1, 0:1], min_val=0, max_val=NOPS - 1)
                fl = sp.value_load(flagb[0:1, bass.ds(s * NOPS + op, 1)], min_val=0, max_val=3)
                sp.sem_inc(S["op_read"], 1)
                with sp.If(fl != 0):
                    for bi in range(BI):
                        sp.dma_start(recA[32 * bi:32 * bi + 32, :],
                                     rec_a[bass.ds(s * NOPS + op, 1), :, :].rearrange("a c n -> (a c) n")
                                     ).then_inc(S["w_in"], 16)
                    sp.dma_start(recB, rec_b[bass.ds(s * NOPS + op, 1), :, :].rearrange("a c n -> (a c) n")
                                 ).then_inc(S["w_in"], 16)
                with sp.Else():
                    sp.sem_inc(S["w_in"], 5 * 16)
            sp.wait_ge(S["out_ready"], 1)
            sp.dma_start(out.rearrange("(g b) c n -> (b c) g n", g=BG),
                         outC.rearrange("p (g n) -> p g n", g=BG)).then_inc(S["out_st"], 16)
            sp.wait_ge(S["out_st"], 16)

        @block.gpsimd
        def _(pool):
            own = Own(pool, S["pool_own"])
            nc.gpsimd.memset(xn3, 0.0).then_inc(S["pool_zero"], 1)
            nc.gpsimd.memset(zeros, 0.0).then_inc(S["pool_zero"], 1)
            nc.gpsimd.memset(xp, 0.0).then_inc(S["pool_zero"], 1)
            pool.wait_ge(S["pool_zero"], 3)
            nc.gpsimd.memset(pooled[C:C + 1, :], 1.0).then_inc(S["pool_zero"], 1)
            pool.wait_ge(S["pool_zero"], 4)
            nc.gpsimd.memset(ones1, 1.0).then_inc(S["pool_zero"], 1)
            pool.wait_ge(S["cst_in"], 16)
            pool.wait_ge(S["w32_in"], 64)
            pool.wait_ge(S["par_in"], SMALL)

            def bd4(dst, src, k, o):
                m = mask4.unsqueeze(1).unsqueeze(3).to_broadcast([P, k, BI, o])
                s = src.rearrange("p (k o) -> p k o", k=k).unsqueeze(2).to_broadcast([P, k, BI, o])
                return nc.gpsimd.tensor_tensor(dst, s, m, ALU.mult)

            bd4(off_bd, w32_("off"), KK, NOFF).then_inc(S["pool_bd"], 1)
            nc.gpsimd.tensor_tensor(base2, cst_("base").rearrange("p (t o) -> p t o", t=PT),
                                    row_("b_off").unsqueeze(1).to_broadcast([P, PT, NOFF]),
                                    ALU.add).then_inc(S["pool_bd"], 1)
            bd4(conv_bd, w32_("conv"), KK, CH).then_inc(S["pool_bd"], 1)
            pool.wait_ge(S["par_in"], SMALL)
            nc.gpsimd.tensor_scalar(cgw, cst_("mask16"), par_("cg1_w"), None, ALU.mult).then_inc(S["pool_bd"], 1)
            pool.wait_ge(S["late_in"], LATE)
            nc.gpsimd.tensor_tensor(gate_bd, w32_("gate").unsqueeze(1).to_broadcast([P, BI, EXP]),
                                    mask4.unsqueeze(2).to_broadcast([P, BI, EXP]), ALU.mult
                                    ).then_inc(S["pool_bd"], 1)
            pool.wait_ge(S["g_ev"], BG * PT * BI)
            with pool.Fori(0, KK) as k:
                pool.wait_ge(S["dcn_mm"], k * B + 1)
                nc.gpsimd.tensor_copy(Gst.rearrange("p g t b o -> p (g t b) o"),
                                      GS.rearrange("p g t b k o -> p (g t b) k o")[:, :, bass.ds(k, 1), :]
                                      .rearrange("p a k o -> p a (k o)")).then_inc(S["gst"], 1)
            pool.wait_ge(S["lk_ev"], 1)
            nc.gpsimd.tensor_tensor(ql_bd, expand16(ql), mask8_for(B), ALU.mult).then_inc(S["ql_bd"], 1)
            for bi in range(BI):
                pool.wait_ge(S["a1_sum"], bi + 1)
                v = arr3(a1[:, 512 * bi:512 * bi + 512], 16)
                nc.gpsimd.tensor_tensor(v, v, small[:, 256 + 32 * bi:288 + 32 * bi].unsqueeze(2)
                                        .to_broadcast([P, 32, 16]), ALU.mult).then_inc(S["a1_norm"], 1)
            pool.wait_ge(S["cr_in"], 1)
            nc.gpsimd.partition_all_reduce(small[:, 32:34], small[:, 16:18], P, bass.bass_isa.ReduceOp.max
                                           ).then_inc(S["cr_max"], 1)
            with pool.Fori(0, PINV) as it:
                pool.wait_ge(S["z_new"], it * 2 + 2)
                nc.gpsimd.tensor_tensor(bdzT, expand16(zT), mask8_for(B), ALU.mult).then_inc(S["zT_bd"], 1)
            with pool.Fori(0, LAYERS) as l:
                pool.wait_ge(S["la_r"], l + 1)
                src = w32_("q").rearrange("p (l n) -> p l n", l=LAYERS)[:, bass.ds(l, 1), :]
                src = src.rearrange("p l (j o) -> p (l j) o", o=C).unsqueeze(2).to_broadcast([P, LHEADS, BI, C])
                nc.gpsimd.tensor_tensor(q_bd, src, mask4.unsqueeze(1).unsqueeze(3)
                                        .to_broadcast([P, LHEADS, BI, C]), ALU.mult).then_inc(S["la_qbd"], 1)

        @block.tensor
        def _(pe):
            mm = nc.tensor.matmul
            tr = nc.tensor.transpose

            def to_C(src, bank, n):
                for g in range(BG):
                    for t in range(PT):
                        c0 = (t * B + g * BI) * C
                        last = tr(ps[bank][:, (g * PT + t) * P:(g * PT + t + 1) * P], src[:, c0:c0 + P], ident)
                last.then_inc(n, 1)

            pe.wait_ge(S["xn"], 3 * BG)
            pe.wait_ge(S["cst_in"], 16)
            pe.wait_ge(S["w32_in"], 64)
            pe.wait_ge(S["pool_bd"], 1)
            for t in range(PT):
                for g in range(BG):
                    c0 = (t * BG + g) * BI * NOFF
                    for k in range(KK):
                        last = mm(ps[0][:, c0:c0 + BI * NOFF], xn3[:, g, k % 3, 16 * (t * 8 + k // 3):16 * (t * 8 + k // 3) + P],
                                  off_bd[:, k, :, :], start=(k == 0), stop=(k == KK - 1))
            last.then_inc(S["off_mm"], 1)
            for g in range(BG):
                for t in range(PT):
                    r = g * PT + t
                    if r:
                        pe.wait_ge(S["g_ev"], r * BI)
                    for bi in range(BI):
                        rr = slice(32 * bi, 32 * bi + 32)
                        last = mm(ps[4 + bi][:, 0:KK * C], xn3[rr, g, 1, 16 * (1 + t * 8):16 * (9 + t * 8)],
                                  w32_("dcn")[rr, :], start=True, stop=True)
                    last.then_inc(S["g_mm"], 1)
            pe.wait_ge(S["g_ev"], BG * PT * BI)
            pe.wait_ge(S["pool_zero"], 2)
            for g in range(BG):
                mm(ps[4 + g][:, 0:N], zeros, xn3[:, 0, 1, 0:N], start=True, stop=False)
            pe.sem_inc(S["dcn_mm"], 1)
            pe.sem_inc(S["tr"], 1)
            pe.sem_inc(S["la_r"], 1)
            with pe.Fori(0, KK) as k:
                pe.wait_ge(S["gst"], k + 1)
                for c in range(B + 1):
                    if c < B:
                        pe.wait_ge(S["prod"], k * B + c + 1)
                        if c < BI:
                            pe.wait_ge(S["s_ev"], k * B + c + 1)
                        else:
                            pe.wait_ge(S["s_ev"], k * B + c - BI + 2)
                        for q in range(PT):
                            for t in range(PT):
                                last = tr(ps[c % BI][:, (q * PT + t) * P:(q * PT + t + 1) * P],
                                          ST[:, c, t, q * 8:q * 8 + 8, :], ident)
                        last.then_inc(S["tr"], 1)
                    if c:
                        d = c - 1
                        g, bi = d // BI, d % BI
                        pe.wait_ge(S["s_ev"], k * B + d + 2)
                        for q in range(PT):
                            last = mm(ps[4 + g][32 * bi:32 * bi + 32, 0:N], Gst[:, g, q, bi, :], SQ[:, d, q, :],
                                      start=False, stop=False, skip_group_check=True)
                        last.then_inc(S["dcn_mm"], 1)
            for g in range(BG):
                mm(ps[4 + g][:, 0:N], zeros, xn3[:, 0, 1, 0:N], start=False, stop=True).then_inc(S["dcn_mm"], 1)
            pe.wait_ge(S["x1_ready"], BG)
            pe.wait_ge(S["pool_bd"], 3)
            for g in range(BG):
                for k in range(KK):
                    last = mm(ps[g][64 * g:64 * g + 64, 0:N], conv_bd[:, k, :, :],
                              window(xp, g, 3 * (k // 3), 3 * (k % 3), 16), start=(k == 0), stop=(k == KK - 1))
                last.then_inc(S["conv_mm"], 1)
            pe.wait_ge(S["feat"], BG)
            for t in range(PT):
                last = tr(ps[2][:, t * P:t * P + P], feat[:, t * P:t * P + P], ident)
            last.then_inc(S["featT_mm"], 1)
            pe.wait_ge(S["featT_ev"], 1)
            for t in range(PT):
                last = mm(ps[3], featT[:, t, :], dft[:, t, 0:2 * N], start=(t == 0), stop=(t == PT - 1))
            last.then_inc(S["f2_mm"], 1)
            pe.wait_ge(S["f2_ev"], 1)
            mm(ps[4], cst_("swap"), F2, start=True, stop=True).then_inc(S["swap_mm"], 1)
            pe.wait_ge(S["pool_bd"], 4)
            mm(ps[6][:, 0:N], cgw, F2[:, 0:N], start=True, stop=True).then_inc(S["cg_mm"], 1)
            mm(ps[5][:, 0:N], cst_("swap"), feat, start=True, stop=True).then_inc(S["swap_mm"], 1)
            pe.wait_ge(S["gated"], 2)
            for a in range(2):
                for t in range(PT):
                    last = tr(ps[7][:, (a * PT + t) * P:(a * PT + t + 1) * P],
                              gated[:, a * N + t * P:a * N + t * P + P], ident)
            last.then_inc(S["gT_mm"], 1)
            pe.wait_ge(S["gT_ev"], 1)
            for n, (a, t) in enumerate(((0, 0), (0, 1), (1, 0), (1, 1))):
                last = mm(ps[2], gT[:, a, t, :], dft[:, t, a * N:a * N + 2 * N], start=(n == 0), stop=(n == 3))
            last.then_inc(S["inv_mm"], 1)
            for g in range(BG):
                for t in range(PT):
                    last = tr(ps[0][:, (t * BG + g) * P:(t * BG + g + 1) * P],
                              x1C[:, g * N + t * P:g * N + t * P + P], ident)
            last.then_inc(S["toT_mm"], 1)
            pe.wait_ge(S["mix_abs"], 1)
            pe.wait_ge(S["inv_abs"], 1)
            for n, src in enumerate((outf, gatef)):
                for t in range(PT):
                    last = tr(ps[1][:, (n * PT + t) * P:(n * PT + t + 1) * P], src[:, t * P:t * P + P], ident)
            last.then_inc(S["toT_mm"], 1)

            pe.wait_ge(S["ct_in"], 1)
            to_C(ln_b, 0, S["ct_mm"])
            pe.wait_ge(S["ct_ev"], 1)
            pe.wait_ge(S["late_in"], LATE)
            wq, wk, wv = (w32_("qkv")[:, P * i:P * i + P] for i in range(3))
            for w, bank in ((wq, 0), (wk, 4)):
                for bi in range(BI):
                    rr = slice(32 * bi, 32 * bi + 32)
                    mm(ps[bank + bi], w[rr, :], lnC[rr, :], start=True, stop=True).then_inc(S["qk_mm"], 1)
            pe.wait_ge(S["pool_in"], 1)
            for bi in range(BI):
                rr = slice(32 * bi, 32 * bi + 32)
                pe.wait_ge(S["q_ev"], bi + 1)
                mm(ps[bi][:, 0:32], wq[rr, :], xpool[rr, :], start=True, stop=True)
                mm(ps[bi][:, 32:64], wk[rr, :], xpool[rr, :], start=True, stop=True).then_inc(S["lk_mm"], 1)
            for bi in range(BI):
                rr = slice(32 * bi, 32 * bi + 32)
                pe.wait_ge(S["k_ev"], bi + 1)
                for g in range(BG):
                    for t in range(PT):
                        last = mm(ps[4 + bi][:, (g * PT + t) * P:(g * PT + t + 1) * P],
                                  lnC[rr, g * N + t * P:g * N + t * P + P], wv[rr, :], start=True, stop=True)
                last.then_inc(S["v_mm"], 1)
            pe.wait_ge(S["ql_bd"], 1)
            for b in range(B):
                last = mm(ps[0][:, 16 * b:16 * b + 16], ql_bd[:, b, :, :], kl[:, b, :], start=True, stop=True)
            last.then_inc(S["sim2_mm"], 1)
            for bi in range(BI):
                pe.wait_ge(S["v_ev"], bi + 1)
                for g in range(BG):
                    last = mm(ps[4 + bi][:, g * N:g * N + N], ql_bd[:, 2 * bi + g, :, :],
                              kT[:, 512 * bi + N * g:512 * bi + N * g + N], start=True, stop=True)
                last.then_inc(S["sim3_mm"], 1)
            for bi in range(BI):
                pe.wait_ge(S["a3_exp"], bi + 1)
                for j in range(4):
                    last = tr(ps[4 + bi][:, j * P:j * P + P], a3[:, 512 * bi + j * P:512 * bi + j * P + P], ident)
                last.then_inc(S["a3T_mm"], 1)
            for bi in range(BI):
                pe.wait_ge(S["a3T_ev"], bi + 1)
                for g in range(BG):
                    b = 2 * bi + g
                    for t in range(PT):
                        c0 = 512 * bi + (g * PT + t) * P
                        last = mm(ps[2 + b // 4][:, (b % 4) * P:(b % 4) * P + P], a3T[:, c0:c0 + P],
                                  V[:, c0:c0 + P], start=(t == 0), stop=(t == PT - 1))
            last.then_inc(S["w3_mm"], 1)
            pe.wait_ge(S["kl_bd"], 1)
            for bi in range(BI):
                for g in range(BG):
                    for t in range(PT):
                        c0 = 512 * bi + g * N + t * P
                        last = mm(ps[4 + bi][:, (g * PT + t) * P:(g * PT + t + 1) * P], qT[:, c0:c0 + P],
                                  kl_bd[:, 2 * bi + g, :, :], start=True, stop=True)
                last.then_inc(S["sim1_mm"], 1)
            pe.wait_ge(S["late_in"], LATE)
            pe.wait_ge(S["w3_ev"], 1)
            pe.wait_ge(S["a2_sub"], 1)
            Vb = V.rearrange("p (b t n) -> p b t n", b=B, t=PT)
            for t in range(PT):
                for h in range(HEADS):
                    for s in range(PT):
                        col = (1 - t + s) * P
                        last = mm(ps[2 * t + h // 4][:, (h % 4) * P:(h % 4) * P + P], toepb[:, h, col:col + P],
                                  Vb[:, :, s, h * DH:h * DH + DH], start=(s == 0), stop=(s == PT - 1))
                    if h % 4 == 3:
                        last.then_inc(S["res_mm"], 1)
            for bi in range(BI):
                pe.wait_ge(S["a1_norm"], bi + 1)
                for j in range(4):
                    last = tr(ps[4 + bi][:, j * P:j * P + P], a1[:, 512 * bi + j * P:512 * bi + j * P + P], ident)
                last.then_inc(S["a1T_mm"], 1)
            pe.wait_ge(S["x_bd"], 1)
            pe.wait_ge(S["res_ev"], 4)
            for b in range(B):
                last = tr(ps[b // 4][:, (b % 4) * P:(b % 4) * P + P], bdz[:, b, :, :], ident)
            last.then_inc(S["xT_mm"], 1)
            with pe.Fori(0, PINV) as it:
                pe.wait_ge(S["t_ready"], it * 4 + 1)
                for b in range(B):
                    mm(ps[0][:, 16 * b:16 * b + 16], bdz[:, b, :, :], XT[:, b, :], start=True, stop=True)
                for b in range(B):
                    last = mm(ps[1][:, 16 * b:16 * b + 16], bdXT[:, b, :, :], z[:, b, :], start=True, stop=True)
                last.then_inc(S["xz_mm"], 1)
                for n in range(2):
                    pe.wait_ge(S["t_ready"], it * 4 + 2 + n)
                    for b in range(B):
                        last = mm(ps[2 + n][:, 16 * b:16 * b + 16], bdxzT[:, b, :, :], tt[:, b, :],
                                  start=True, stop=True)
                    last.then_inc(S["t_mm"], 1)
                pe.wait_ge(S["t_ready"], it * 4 + 4)
                pe.wait_ge(S["zT_bd"], it + 1)
                for b in range(B):
                    mm(ps[0][:, 16 * b:16 * b + 16], bdzT[:, b, :, :], tt[:, b, :], start=True, stop=True)
                for b in range(B):
                    last = mm(ps[1][:, 16 * b:16 * b + 16], bdt[:, b, :, :], zT[:, b, :], start=True, stop=True)
                last.then_inc(S["z_mm"], 1)
            pe.wait_ge(S["t_ready"], PINV * 4 + 1)
            for b in range(B):
                last = mm(ps[2 + b // 4][:, (b % 4) * P:(b % 4) * P + P], bdz[:, b, :, :], w3_bd[:, b, :, :],
                          start=True, stop=True)
            last.then_inc(S["w2_mm"], 1)
            pe.wait_ge(S["w2_ev"], 1)
            pe.wait_ge(S["a1T_ev"], BI)
            for bi in range(BI):
                for g in range(BG):
                    b = 2 * bi + g
                    mm(ps[4 + bi][:, g * N:g * N + N], w2_bd[:, b, :, :], a1T[:, N * b:N * b + N],
                       start=True, stop=False)
                    for t in range(PT):
                        last = mm(ps[4 + bi][:, g * N + t * P:g * N + t * P + P],
                                  res[:, (t * B + b) * P:(t * B + b + 1) * P], cst_("flip"),
                                  start=False, stop=(t == PT - 1))
                last.then_inc(S["oT_mm"], 1)
            pe.wait_ge(S["oT_evA"], 2)
            pe.wait_ge(S["oT_evD"], 2)
            pe.wait_ge(S["late_in"], LATE)
            for bi in range(BI):
                for g in range(BG):
                    for t in range(PT):
                        j = t * B + g * BI + bi
                        c0 = 512 * bi + g * N + t * P
                        last = mm(ps[0][:, j * C:j * C + C], oT[:, c0:c0 + P], woutb, start=True, stop=True)
            last.then_inc(S["ao_mm"], 1)

            pe.wait_ge(S["ct_in"], 2)
            to_C(t0, 1, S["ct_mm"])
            pe.wait_ge(S["ct_ev"], 2)
            pe.wait_ge(S["pool_bd"], 5)
            for g in range(BG):
                last = mm(ps[2][64 * g:64 * g + 64, 0:N], gate_bd, lnC[:, g * N:g * N + N], start=True, stop=True)
            last.then_inc(S["lg_mm"], 1)
            pe.wait_ge(S["topk"], 1)
            for t in range(PT):
                last = tr(ps[3][:, t * P:t * P + P], probs[:, t * P:t * P + P], ident)
            last.then_inc(S["mT_mm"], 1)
            pe.wait_ge(S["mT_ev"], 1)
            for b in range(B):
                for t in range(PT):
                    j = t * B + b
                    last = mm(ps[4][0:C, 16 * b:16 * b + 16], t0[:, j * C:j * C + C], mT[:, t, 16 * b:16 * b + 16],
                              start=(t == 0), stop=(t == PT - 1))
            last.then_inc(S["pl_mm"], 1)
            pe.wait_ge(S["pl_ev"], 1)
            pe.wait_ge(S["late_in"], LATE)
            pe.wait_ge(S["pool_zero"], 5)
            pool_e = pooled.rearrange("d (b e) -> d e b", b=B)
            for e in range(EXP):
                last = mm(ps[5][:, B * e:B * e + B], w1b[:, HID * e:HID * e + HID], pool_e[:, e, :],
                          start=True, stop=True)
            last.then_inc(S["hid_mm"], 1)
            pe.wait_ge(S["hid_ev"], 1)
            for e in range(EXP):
                mm(ps[6][0:C, B * e:B * e + B], w2b[:, C * e:C * e + C], hid[:, e, :], start=True, stop=False)
                last = mm(ps[6][0:C, B * e:B * e + B], b2b[:, C * e:C * e + C], ones1, start=False, stop=True)
            last.then_inc(S["eo_mm"], 1)
            pe.wait_ge(S["eo_ev"], 1)
            tr(ps[7][:, 0:C], eo, ident[0:C, 0:C]).then_inc(S["eoT_mm"], 1)
            pe.wait_ge(S["eo_bd"], 1)
            for t in range(PT):
                last = mm(ps[0][:, t * N:t * N + N], probs[:, t * P:t * P + P], eo_bd, start=True, stop=True)
            last.then_inc(S["moe_mm"], 1)

            pe.wait_ge(S["ct_in"], 3)
            to_C(ZT_, 1, S["ct_mm"])
            VT = w32_("v").rearrange("p (l n) -> p l n", l=LAYERS)
            with pe.Fori(0, LAYERS) as l:
                pe.wait_ge(S["la_z"], l * 2 + 2)
                for g in range(BG):
                    for t in range(PT):
                        c0 = (t * B + g * BI) * C
                        last = mm(ps[2][:, g * P:g * P + P], ZT_[:, c0:c0 + P], ZT_[:, c0:c0 + P],
                                  start=(t == 0), stop=(t == PT - 1))
                last.then_inc(S["la_g"], 1)
                pe.wait_ge(S["la_gev"], l + 1)
                for g in range(BG):
                    last = mm(ps[3][:, g * N:g * N + N], g_bd[:, g * P:g * P + P],
                              VT[:, bass.ds(l, 1), :], start=True, stop=True)
                last.then_inc(S["la_h"], 1)
                pe.wait_ge(S["la_hev"], l + 1)
                pe.wait_ge(S["la_qbd"], l + 1)
                for j in range(LHEADS):
                    last = mm(ps[4][:, 0:BG * C], q_bd[:, j, :, :], hs[:, :, j, :],
                              start=(j == 0), stop=(j == LHEADS - 1))
                last.then_inc(S["la_r"], 1)
                pe.wait_ge(S["la_rev"], l + 1)
                for g in range(BG):
                    mm(ps[5][:, g * N:g * N + N], r_bd[:, g * P:g * P + P], ZC[:, g * N:g * N + N],
                       start=True, stop=True)
                for g in range(BG):
                    for t in range(PT):
                        c0 = (t * B + g * BI) * C
                        last = mm(ps[6][:, c0:c0 + P], ZC[:, g * N + t * P:g * N + t * P + P],
                                  r_bd[:, g * P:g * P + P], start=True, stop=True)
                last.then_inc(S["la_zmm"], 1)

            pe.wait_ge(S["ct_in"], 4)
            to_C(T, 0, S["ct_mm"])
            to_C(ln_b, 1, S["ct_mm"])
            with pe.Fori(0, NB) as s:
                pe.wait_ge(S["h_new"], s + 1)
                settled(pe)
                tr(ps[0][0:1, 0:C], hC[0:C, 0:1], ident[0:C, 0:C]).then_inc(S["op_mm"], 1)
                pe.wait_ge(S["op_ev"], s + 1)
                settled(pe)
                op = pe.value_load(op8[0:1, 0:1], min_val=0, max_val=NOPS - 1)
                fl = pe.value_load(flagb[0:1, bass.ds(s * NOPS + op, 1)], min_val=0, max_val=3)
                ffn = pe.snap(fl % 2)
                pe.sem_inc(S["op_read"], 1)
                with pe.If(fl >= 2):
                    wq, wk, wv, wo = (w_bd[:, P * i:P * i + P] for i in range(4))
                    pe.wait_ge(S["w_bd"], s + 1)
                    mm(ps[1], wq, hC, start=True, stop=True).then_inc(S["rq_mm"], 1)
                    mm(ps[2], wk, hC, start=True, stop=True).then_inc(S["rq_mm"], 1)
                    for g in range(BG):
                        for t in range(PT):
                            last = mm(ps[3][:, (g * PT + t) * P:(g * PT + t + 1) * P],
                                      hC[:, g * N + t * P:g * N + t * P + P], wv, start=True, stop=True)
                    last.then_inc(S["rv_mm"], 1)
                    pe.wait_ge(S["rq_ev"], s + 1)
                    pe.wait_ge(S["rk_ev"], s + 1)
                    pe.wait_ge(S["rv_ev"], s + 1)
                    for g in range(BG):
                        for bi in range(BI):
                            rr = slice(32 * bi, 32 * bi + 32)
                            for t in range(PT):
                                last = mm(ps[g * BI + bi][:, t * N:t * N + N],
                                          rq[rr, g * N + t * P:g * N + t * P + P], rk[rr, g * N:g * N + N],
                                          start=True, stop=True)
                            last.then_inc(S["sc_mm"], 1)
                    for b in range(B):
                        pe.wait_ge(S["sc_norm"], s * B + b + 1)
                        for t in range(PT):
                            for u in range(PT):
                                last = tr(ps[b][:, (u * PT + t) * P:(u * PT + t + 1) * P],
                                          pr[:, b * 512 + t * N + u * P:b * 512 + t * N + u * P + P], ident)
                        last.then_inc(S["pT_mm"], 1)
                    pe.wait_ge(S["pT_ev"], s * B + B)
                    for g in range(BG):
                        for bi in range(BI):
                            for u in range(PT):
                                last = mm(ps[g][32 * bi:32 * bi + 32, 0:N],
                                          rv[:, (g * PT + u) * P + 32 * bi:(g * PT + u) * P + 32 * bi + 32],
                                          prT[:, (g * BI + bi) * 512 + u * N:(g * BI + bi) * 512 + u * N + N],
                                          start=(u == 0), stop=(u == PT - 1))
                    last.then_inc(S["ro_mm"], 1)
                    pe.wait_ge(S["ro_ev"], s + 1)
                    mm(ps[2], wo, roC, start=True, stop=True).then_inc(S["ry_mm"], 1)
                with pe.Else():
                    pe.sem_inc(S["rq_mm"], 2)
                    pe.sem_inc(S["rv_mm"], 1)
                    pe.sem_inc(S["sc_mm"], B)
                    pe.sem_inc(S["pT_mm"], B)
                    pe.sem_inc(S["ro_mm"], 1)
                    pe.sem_inc(S["ry_mm"], 1)
                with pe.If(ffn != 0):
                    pe.wait_ge(S["w_in"], (s + 1) * 80)
                    pe.wait_ge(S["rt_h"], s + 1)
                    for bi in range(BI):
                        rr = slice(32 * bi, 32 * bi + 32)
                        mm(ps[4 + bi], recA[rr, 0:HID], hC[rr, :], start=True, stop=True).then_inc(S["f1_mm"], 1)
                    for bi in range(BI):
                        if bi < 2:
                            pe.wait_ge(S["f1_evA"], s * 2 + bi + 1)
                        else:
                            pe.wait_ge(S["f1_evD"], s * 2 + bi - 1)
                        last = mm(ps[1][32 * bi:32 * bi + 32, :], recB[:, 0:C], f1[:, 512 * bi:512 * bi + 512],
                                  start=True, stop=True)
                    last.then_inc(S["f2mm"], 1)
                with pe.Else():
                    pe.sem_inc(S["f1_mm"], BI)
                    pe.sem_inc(S["f2mm"], 1)

        @block.scalar
        def _(act):
            own = Own(act, S["act_own"])
            af = nc.scalar.activation

            def ln_std(n):
                act.wait_ge(S["ln_var"], n)
                af(small[:, 64:80], small[:, 48:64], ACT.Sqrt).then_inc(S["ln_std"], 1)

            def evac_C(bank, dst, n):
                act.wait_ge(S["ct_mm"], n)
                af(dst, ps[bank], ACT.Copy).then_inc(S["ct_ev"], 1)

            act.wait_ge(S["gn_var"], 1)
            af(small[:, 4:6], small[:, 2:4], ACT.Sqrt).then_inc(S["gn_std"], 1)
            act.wait_ge(S["bn_var"], 1)
            af(small[:, 10:12], small[:, 8:10], ACT.Sqrt).then_inc(S["bn_std"], 1)
            for t in range(PT):
                act.wait_ge(S["diff"], t + 1)
                v = hat[:, t].rearrange("p b k a q -> p (b k a q)")
                own.link(af(v, v, ACT.Abs))
                af(v, v, ACT.Relu, bias=1.0, scale=-1.0).then_inc(S["hat"], 1)
            for r in range(BG * PT):
                act.wait_ge(S["g_mm"], r + 1)
                for bi in range(BI):
                    af(GS[:, r // PT, r % PT, bi].rearrange("p k o -> p (k o)"), ps[4 + bi][:, 0:KK * C],
                       ACT.Copy).then_inc(S["g_ev"], 1)
            act.sem_inc(S["s_ev"], 1)
            with act.Fori(0, KK) as k:
                for c in range(B):
                    act.wait_ge(S["tr"], k * B + c + 2)
                    act.wait_ge(S["dcn_mm"], k * B + 1)
                    af(SQ[:, c].rearrange("p q n -> p (q n)"), ps[c % BI], ACT.Copy).then_inc(S["s_ev"], 1)
            act.wait_ge(S["bn_ready"], 1)
            for g in range(BG):
                act.wait_ge(S["conv_mm"], g + 1)
                hh = slice(64 * g, 64 * g + 64)
                af(feat[hh, :], ps[g][hh, 0:N], ACT.Gelu, bias=small[hh, 13:14], scale=small[hh, 12:13]
                   ).then_inc(S["feat"], 1)
            act.wait_ge(S["featT_mm"], 1)
            af(featT.rearrange("p t n -> p (t n)"), ps[2][:, 0:PT * P], ACT.Copy).then_inc(S["featT_ev"], 1)
            act.wait_ge(S["f2_mm"], 1)
            af(F2, ps[3], ACT.Copy).then_inc(S["f2_ev"], 1)
            act.wait_ge(S["cg_mm"], 1)
            own.link(af(cg, ps[6][:, 0:N], ACT.Gelu, bias=small[:, 15:16], scale=small[:, 14:15]))
            af(cg, cg, ACT.Sigmoid, bias=par_("cg2_b"), scale=par_("cg2_w")).then_inc(S["cg_act"], 1)
            act.wait_ge(S["l2_sum"], 1)
            af(small[:, 18:20], small[:, 16:18], ACT.Sqrt).then_inc(S["l2_std"], 1)
            act.wait_ge(S["sm2_in"], 1)
            af(small[:, 28:32], small[:, 28:32], ACT.Exp).then_inc(S["sm2_exp"], 1)
            act.wait_ge(S["gT_mm"], 1)
            af(gT.rearrange("p a t n -> p (a t n)"), ps[7], ACT.Copy).then_inc(S["gT_ev"], 1)
            act.wait_ge(S["mix"], 1)
            af(outf, outf, ACT.Sqrt).then_inc(S["mix_abs"], 1)
            act.wait_ge(S["inv_mm"], 1)
            af(gated, ps[2], ACT.Square).then_inc(S["inv_sq"], 1)
            act.wait_ge(S["inv_add"], 1)
            af(gatef, gatef, ACT.Sqrt, scale=1.0 / (N * N)).then_inc(S["inv_abs"], 1)

            ln_std(1)
            ln_std(2)
            evac_C(0, lnC, 1)
            for bi in range(BI):
                act.wait_ge(S["qk_mm"], bi + 1)
                af(qT[:, 512 * bi:512 * bi + 512], ps[bi], ACT.Copy, scale=DH ** -0.5).then_inc(S["q_ev"], 1)
            for bi in range(BI):
                act.wait_ge(S["v_mm"], bi + 1)
                af(V[:, 512 * bi:512 * bi + 512], ps[4 + bi], ACT.Copy).then_inc(S["v_ev"], 1)
            for bi in range(BI):
                act.wait_ge(S["a3_max"], bi + 1)
                for g in range(BG):
                    b = 2 * bi + g
                    last = af(a3[:, N * b:N * b + N], ps[4 + bi][:, g * N:g * N + N], ACT.Exp,
                              bias=small[:, 80 + b:81 + b], accum_out=small[:, 88 + b:89 + b])
                last.then_inc(S["a3_exp"], 1)
            act.wait_ge(S["a2_sub"], 1)
            af(XM, XM, ACT.Exp).then_inc(S["a2_exp"], 1)
            for bi in range(BI):
                act.wait_ge(S["a1_sub"], bi + 1)
                v = a1[:, 512 * bi:512 * bi + 512]
                af(v, v, ACT.Exp).then_inc(S["a1_exp"], 1)
            rr4 = res.rearrange("p (t b h e) -> p t h b e", t=PT, b=B, h=HEADS)
            for n in range(4):
                act.wait_ge(S["res_mm"], n + 1)
                af(rr4[:, n // 2, 4 * (n % 2):4 * (n % 2) + 4],
                   ps[n].rearrange("p (h b e) -> p h b e", h=4, b=B), ACT.Copy).then_inc(S["res_ev"], 1)
            for bi in range(BI):
                act.wait_ge(S["a1T_mm"], bi + 1)
                af(a1T[:, 512 * bi:512 * bi + 512], ps[4 + bi], ACT.Copy).then_inc(S["a1T_ev"], 1)
            for bi in range(2):
                act.wait_ge(S["oT_mm"], bi + 1)
                af(oT[:, 512 * bi:512 * bi + 512], ps[4 + bi], ACT.Copy).then_inc(S["oT_evA"], 1)

            ln_std(3)
            evac_C(1, lnC, 2)
            act.wait_ge(S["lg_max"], 1)
            af(probs, probs, ACT.Exp, bias=small[:, 105:106], accum_out=small[:, 106:107]).then_inc(S["lg_exp"], 1)
            act.wait_ge(S["hid_mm"], 1)
            af(hid.rearrange("p e b -> p (e b)"), ps[5][:, 0:P], ACT.Gelu).then_inc(S["hid_ev"], 1)

            ln_std(4)
            act.wait_ge(S["ct_mm"], 3)
            af(ZC, ps[1], ACT.Copy).then_inc(S["la_z"], 1)
            with act.Fori(0, LAYERS) as l:
                act.wait_ge(S["la_h"], l + 1)
                af(hs.rearrange("p g j o -> p (g j o)"), ps[3], ACT.Copy).then_inc(S["la_hev"], 1)
            ln_std(5)
            evac_C(0, tC, 4)
            act.wait_ge(S["ct_mm"], 5)
            af(hC, ps[1], ACT.Copy).then_inc(S["h_new"], 1)

            with act.Fori(0, NB) as s:
                act.wait_ge(S["op_ev"], s + 1)
                settled(act)
                op = act.value_load(op8[0:1, 0:1], min_val=0, max_val=NOPS - 1)
                fl = act.value_load(flagb[0:1, bass.ds(s * NOPS + op, 1)], min_val=0, max_val=3)
                ffn = act.snap(fl % 2)
                act.sem_inc(S["op_read"], 1)
                with act.If(fl >= 2):
                    act.wait_ge(S["rq_mm"], s * 2 + 1)
                    af(rq, ps[1], ACT.Copy, scale=C ** -0.5).then_inc(S["rq_ev"], 1)
                    act.wait_ge(S["rv_mm"], s + 1)
                    af(rv, ps[3], ACT.Copy).then_inc(S["rv_ev"], 1)
                    for b in range(B):
                        act.wait_ge(S["sc_max"], s * B + b + 1)
                        for t in range(PT):
                            last = af(pr[:, b * 512 + t * N:b * 512 + t * N + N], ps[b][:, t * N:t * N + N], ACT.Exp,
                                      bias=rmax[:, 2 * b + t:2 * b + t + 1],
                                      accum_out=rsum[:, 2 * b + t:2 * b + t + 1])
                        last.then_inc(S["sc_exp"], 1)
                    for b in range(B):
                        act.wait_ge(S["pT_mm"], s * B + b + 1)
                        af(prT[:, b * 512:b * 512 + 512], ps[b], ACT.Copy).then_inc(S["pT_ev"], 1)
                with act.Else():
                    act.sem_inc(S["rq_ev"], 1)
                    act.sem_inc(S["rv_ev"], 1)
                    act.sem_inc(S["sc_exp"], B)
                    act.sem_inc(S["pT_ev"], B)
                with act.If(ffn != 0):
                    act.wait_ge(S["w_in"], (s + 1) * 80)
                    for bi in range(2):
                        act.wait_ge(S["f1_mm"], s * BI + bi + 1)
                        af(f1[:, 512 * bi:512 * bi + 512], ps[4 + bi], ACT.Relu, bias=recB[:, C:C + 1]
                           ).then_inc(S["f1_evA"], 1)
                with act.Else():
                    act.sem_inc(S["f1_evA"], 2)

        @block.vector
        def _(dve):
            own = Own(dve, S["dve_own"])
            link = own.link
            v_ = nc.vector
            tt_, ts_, stt = v_.tensor_tensor, v_.tensor_scalar, v_.scalar_tensor_tensor

            def layernorm(src, dst, eps, n):
                s3, d3, c3 = arr3(src, C), arr3(dst, C), arr3(ln_a, C)
                bc = lambda a: a.unsqueeze(2).to_broadcast([P, 16, C])
                mean, var, std = small[:, 32:48], small[:, 48:64], small[:, 64:80]
                link(v_.tensor_reduce(mean, s3, AX.X, ALU.add))
                link(ts_(mean, mean, 1.0 / C, None, ALU.mult))
                link(tt_(c3, s3, bc(mean), ALU.subtract))
                link(tt_(d3, c3, c3, ALU.mult))
                link(v_.tensor_reduce(var, d3, AX.X, ALU.add))
                ts_(var, var, 1.0 / C, eps, ALU.mult, ALU.add).then_inc(S["ln_var"], 1)
                dve.wait_ge(S["ln_std"], n)
                link(v_.reciprocal(std, std))
                return tt_(d3, c3, bc(std), ALU.mult)

            dve.wait_ge(S["x_in"], 16)
            stats = scr[:, 0:12].rearrange("p (g s) -> p g s", g=BG)
            mv = scr[:, 16:20].rearrange("p (g s) -> p g s", g=BG)
            for g in range(BG):
                link(v_.bn_stats(stats[:, g, :], xC[:, g * N:g * N + N]))
            for g in range(BG):
                link(v_.bn_aggr(mv[:, g, :], stats[:, g, :]))
            ts_(small[:, 2:4], mv[:, :, 1], 1e-5, None, ALU.add).then_inc(S["gn_var"], 1)
            dve.wait_ge(S["gn_std"], 1)
            link(v_.reciprocal(small[:, 4:6], small[:, 4:6]))
            dve.wait_ge(S["pool_zero"], 1)
            for g in range(BG):
                src = xC[:, g * N:g * N + N].rearrange("p (y x) -> p y x", y=HH)
                for s, (d0, s0, n) in enumerate(((1, 0, 15), (0, 0, 16), (0, 1, 15))):
                    dst = xn3[:, g, s, 16:16 + N].rearrange("p (y x) -> p y x", y=HH)
                    ts_(dst[:, :, d0:d0 + n], src[:, :, s0:s0 + n], mv[:, g, 0:1], small[:, 4 + g:5 + g],
                        ALU.subtract, ALU.mult).then_inc(S["xn"], 1)
            dve.wait_ge(S["par_in"], SMALL)
            link(ts_(small[:, 8:9], par_("bn_v"), 1e-5, None, ALU.add))
            ts_(small[:, 9:10], par_("cgbn_v"), 1e-5, None, ALU.add).then_inc(S["bn_var"], 1)
            dve.wait_ge(S["off_mm"], 1)
            dve.wait_ge(S["pool_bd"], 2)
            link(tt_(yx, ps[0][:, 0:288].rearrange("p (t b o) -> p t b o", t=PT, b=B),
                     base2.unsqueeze(2).to_broadcast([P, PT, B, NOFF]), ALU.add))
            for t in range(PT):
                tt_(hat[:, t].rearrange("p b k a q -> p (b k a) q"),
                    yx[:, t].rearrange("p b o -> p (b o)").unsqueeze(2).to_broadcast([P, B * NOFF, 16]),
                    iota.unsqueeze(1).to_broadcast([P, B * NOFF, 16]), ALU.subtract).then_inc(S["diff"], 1)
            dve.wait_ge(S["bn_std"], 1)
            link(v_.reciprocal(small[:, 10:12], small[:, 10:12]))
            link(tt_(small[:, 12:13], par_("bn_g"), small[:, 10:11], ALU.mult))
            link(tt_(small[:, 14:15], par_("cgbn_g"), small[:, 11:12], ALU.mult))
            link(tt_(small[:, 6:7], par_("bn_m"), small[:, 12:13], ALU.mult))
            link(tt_(small[:, 13:14], par_("bn_b"), small[:, 6:7], ALU.subtract))
            link(tt_(small[:, 7:8], par_("cg1_b"), par_("cgbn_m"), ALU.subtract))
            link(tt_(small[:, 7:8], small[:, 7:8], small[:, 14:15], ALU.mult))
            tt_(small[:, 15:16], small[:, 7:8], par_("cgbn_b"), ALU.add).then_inc(S["bn_ready"], 1)
            dve.wait_ge(S["hat"], PT)
            with dve.Fori(0, KK) as k:
                for c in range(B):
                    if c == 0:
                        dve.wait_ge(S["tr"], k * B + 1)
                    hy = hat[:, :, c, bass.ds(k, 1), 0, :].rearrange("p t k q -> p t (k q)")
                    hx = hat[:, :, c, bass.ds(k, 1), 1, :].rearrange("p t k q -> p t (k q)")
                    tt_(ST[:, c], hy.unsqueeze(3).to_broadcast([P, PT, 16, 16]),
                        hx.unsqueeze(2).to_broadcast([P, PT, 16, 16]), ALU.mult).then_inc(S["prod"], 1)
            dve.wait_ge(S["dcn_mm"], KK * B + BG + 1)
            for g in range(BG):
                link(tt_(x1C[:, g * N:g * N + N], xC[:, g * N:g * N + N], ps[4 + g][:, 0:N], ALU.add))
                dve.wait_ge(S["pool_zero"], 3)
                v_.tensor_copy(xp[:, g, 3:19, 3:19], x1C[:, g * N:g * N + N].rearrange("p (y x) -> p y x", y=HH)
                               ).then_inc(S["x1_ready"], 1)

            Fp, fp = ps[4], ps[5][:, 0:N]
            dve.wait_ge(S["swap_mm"], 2)
            sm = small
            link(v_.tensor_tensor_reduce(scr, F2, F2, 1.0, 0.0, ALU.mult, ALU.add, sm[:, 16:17]))
            link(v_.tensor_copy(mixed, Fp))
            link(v_.tensor_tensor_reduce(scr, mixed, mixed, 1.0, 0.0, ALU.mult, ALU.add, sm[:, 17:18]))
            link(ts_(sm[:, 20:21], sm[:, 16:17], 1.0, None, ALU.mult))
            link(v_.tensor_tensor_reduce(scr, F2, mixed, 1.0, 0.0, ALU.mult, ALU.add, sm[:, 21:22]))
            link(v_.tensor_tensor_reduce(scr[:, 0:N], F2[:, N:2 * N], mixed[:, 0:N], 1.0, 0.0, ALU.mult, ALU.add,
                                         sm[:, 22:23]))
            link(v_.tensor_tensor_reduce(scr[:, 0:N], F2[:, 0:N], mixed[:, N:2 * N], 1.0, 0.0, ALU.mult, ALU.add,
                                         sm[:, 23:24]))
            link(tt_(sm[:, 23:24], sm[:, 22:23], sm[:, 23:24], ALU.subtract))
            link(v_.memset(sm[:, 22:23], 0.0))
            ts_(sm[:, 16:18], sm[:, 16:18], 1e-6, None, ALU.add).then_inc(S["l2_sum"], 1)
            dve.wait_ge(S["l2_std"], 1)
            link(v_.reciprocal(sm[:, 18:20], sm[:, 18:20]))
            link(ts_(sm[:, 24:28], sm[:, 20:24], sm[:, 18:19], par_("tau"), ALU.mult, ALU.mult))
            pairs = sm[:, 24:28].rearrange("p (r s) -> p r s", r=2)
            link(tt_(pairs, pairs, sm[:, 18:20].unsqueeze(1).to_broadcast([P, 2, 2]), ALU.mult))
            link(v_.tensor_reduce(sm[:, 20:22], pairs, AX.X, ALU.max))
            ex = sm[:, 28:32].rearrange("p (r s) -> p r s", r=2)
            tt_(ex, pairs, sm[:, 20:22].unsqueeze(2).to_broadcast([P, 2, 2]), ALU.subtract).then_inc(S["sm2_in"], 1)
            dve.wait_ge(S["cg_act"], 1)
            for a in range(2):
                tt_(gated[:, a * N:a * N + N], F2[:, a * N:a * N + N], cg, ALU.mult).then_inc(S["gated"], 1)
            dve.wait_ge(S["sm2_exp"], 1)
            link(v_.tensor_reduce(sm[:, 20:22], ex, AX.X, ALU.add))
            link(v_.reciprocal(sm[:, 20:22], sm[:, 20:22]))
            link(tt_(ex, ex, sm[:, 20:22].unsqueeze(2).to_broadcast([P, 2, 2]), ALU.mult))
            for a in range(2):
                m = mixed[:, a * N:a * N + N]
                link(ts_(m, fp, sm[:, 29 + 2 * a:30 + 2 * a], None, ALU.mult))
                link(stt(m, feat, sm[:, 28 + 2 * a:29 + 2 * a], m, ALU.mult, ALU.add))
            link(tt_(mixed, mixed, mixed, ALU.mult))
            tt_(outf, mixed[:, 0:N], mixed[:, N:2 * N], ALU.add).then_inc(S["mix"], 1)
            dve.wait_ge(S["inv_sq"], 1)
            tt_(gatef, gated[:, 0:N], gated[:, N:2 * N], ALU.add).then_inc(S["inv_add"], 1)
            dve.wait_ge(S["toT_mm"], 2)
            link(v_.tensor_copy(T, ps[0]))
            for n in range(2):
                dst = T4[:, :, :, n * CH:n * CH + CH]
                link(tt_(dst, dst, ps[1][:, n * N:n * N + N].rearrange("p (t b c) -> p t b c", t=PT, b=B), ALU.add))

            link(layernorm(T, t0, 1e-5, 1))
            link(layernorm(t0, ln_b, 1e-5, 2))
            bcrow = lambda n: row_(n).unsqueeze(1).to_broadcast([P, 16, C])
            dve.wait_ge(S["par_in"], SMALL)
            link(tt_(arr3(ln_b, C), arr3(ln_b, C), bcrow("ln_w"), ALU.mult))
            tt_(arr3(ln_b, C), arr3(ln_b, C), bcrow("ln_b"), ALU.add).then_inc(S["ct_in"], 1)
            dve.wait_ge(S["ct_ev"], 1)
            link(v_.tensor_reduce(xpool, arr3(lnC, 16), AX.X, ALU.add))
            ts_(xpool, xpool, 1.0 / LM, None, ALU.mult).then_inc(S["pool_in"], 1)
            for bi in range(BI):
                dve.wait_ge(S["qk_mm"], BI + bi + 1)
                v_.tensor_copy(kT[:, 512 * bi:512 * bi + 512], ps[4 + bi]).then_inc(S["k_ev"], 1)
            for bi in range(BI):
                dve.wait_ge(S["lk_mm"], bi + 1)
                link(ts_(ql[:, 2 * bi:2 * bi + 2, :], ps[bi][:, 0:32].rearrange("p (b m) -> p b m", b=2),
                         DH ** -0.5, None, ALU.mult))
                link(v_.tensor_copy(kl[:, 2 * bi:2 * bi + 2, :],
                                    ps[bi][:, 32:64].rearrange("p (b m) -> p b m", b=2)))
            v_.tensor_copy(small[:, 200:201], small[:, 4:5]).then_inc(S["lk_ev"], 1)
            tt_(kl_bd, expand16(kl), mask8_for(B), ALU.mult).then_inc(S["kl_bd"], 1)
            dve.wait_ge(S["sim2_mm"], 1)
            s2 = ps[0][:, 0:P].rearrange("p (b m) -> p b m", b=B)
            mx, sm8 = small[:, 108:116], small[:, 116:124]
            bc8 = lambda a: a.unsqueeze(2).to_broadcast([P, B, LM])
            link(v_.tensor_reduce(mx, s2, AX.X, ALU.max))
            tt_(XM, s2, bc8(mx), ALU.subtract).then_inc(S["a2_sub"], 1)
            for bi in range(BI):
                dve.wait_ge(S["sim3_mm"], bi + 1)
                v_.tensor_reduce(small[:, 80 + 2 * bi:82 + 2 * bi], arr3(ps[4 + bi], N), AX.X, ALU.max,
                                 negate=True).then_inc(S["a3_max"], 1)
            dve.wait_ge(S["a2_exp"], 1)
            link(v_.tensor_reduce(sm8, XM, AX.X, ALU.add))
            link(v_.reciprocal(sm8, sm8))
            link(tt_(XM, XM, bc8(sm8), ALU.mult))
            tt_(bdz, expand16(XM), mask8_for(B), ALU.mult).then_inc(S["x_bd"], 1)
            for bi in range(BI):
                dve.wait_ge(S["a3T_mm"], bi + 1)
                v_.tensor_copy(a3T[:, 512 * bi:512 * bi + 512], ps[4 + bi]).then_inc(S["a3T_ev"], 1)
            dve.wait_ge(S["w3_mm"], 1)
            link(v_.reciprocal(small[:, 96:104], small[:, 88:96]))
            mr = small[:, 128:192].rearrange("p (b h) -> p b h", b=B)
            link(tt_(mr, mask8.unsqueeze(1).to_broadcast([P, B, HEADS]),
                     small[:, 96:104].unsqueeze(2).to_broadcast([P, B, HEADS]), ALU.mult))
            for n in range(2):
                ins = tt_(w3_bd[:, 4 * n:4 * n + 4], ps[2 + n].rearrange("p (b h e) -> p b h e", b=4, h=HEADS),
                          mr[:, 4 * n:4 * n + 4].unsqueeze(3).to_broadcast([P, 4, HEADS, DH]), ALU.mult)
                if n:
                    ins.then_inc(S["w3_ev"], 1)
                else:
                    link(ins)
            mx1 = small[:, 384:512]
            for bi in range(BI):
                dve.wait_ge(S["sim1_mm"], bi + 1)
                m = mx1[:, 32 * bi:32 * bi + 32]
                link(v_.tensor_reduce(m, arr3(ps[4 + bi], 16), AX.X, ALU.max))
                tt_(arr3(a1[:, 512 * bi:512 * bi + 512], 16), arr3(ps[4 + bi], 16),
                    m.unsqueeze(2).to_broadcast([P, 32, 16]), ALU.subtract).then_inc(S["a1_sub"], 1)
            for bi in range(BI):
                dve.wait_ge(S["a1_exp"], bi + 1)
                r = small[:, 256 + 32 * bi:288 + 32 * bi]
                link(v_.tensor_reduce(r, arr3(a1[:, 512 * bi:512 * bi + 512], 16), AX.X, ALU.add))
                v_.reciprocal(r, r).then_inc(S["a1_sum"], 1)
            dve.wait_ge(S["xT_mm"], 1)
            for n in range(2):
                link(v_.tensor_copy(bdXT[:, 4 * n:4 * n + 4],
                                    ps[n].rearrange("p (b h e) -> p b h e", b=4, h=HEADS)))
            link(v_.tensor_reduce(XT, bdXT.rearrange("p b h m -> p b m h"), AX.X, ALU.add))
            link(v_.tensor_reduce(mx, XM, AX.X, ALU.add, apply_absolute_value=True))
            link(v_.tensor_reduce(sm8, XT, AX.X, ALU.add, apply_absolute_value=True))
            v_.tensor_reduce(small[:, 16:18], small[:, 108:124].rearrange("p (a b) -> p a b", a=2), AX.X, ALU.max
                             ).then_inc(S["cr_in"], 1)
            dve.wait_ge(S["cr_max"], 1)
            link(tt_(small[:, 34:35], small[:, 32:33], small[:, 33:34], ALU.mult))
            link(v_.reciprocal(small[:, 34:35], small[:, 34:35]))
            ts_(z, XT, small[:, 34:35], None, ALU.mult).then_inc(S["z_new"], 1)
            ts_(zT, XM, small[:, 34:35], None, ALU.mult).then_inc(S["z_new"], 1)
            ebc = lambda e: e.unsqueeze(1).to_broadcast([P, B, 16])
            pb = [ps[i][:, 0:P].rearrange("p (b m) -> p b m", b=B) for i in range(4)]
            dve.wait_ge(S["z_new"], 2)
            own.restart()
            with dve.Fori(0, PINV) as it:
                tt_(bdz, expand16(z), mask8_for(B), ALU.mult).then_inc(S["t_ready"], 1)
                dve.wait_ge(S["xz_mm"], it + 1)
                link(tt_(bdxzT, expand16(pb[0]), mask8_for(B), ALU.mult))
                stt(tt, pb[1], -1.0, ebc(eye7), ALU.mult, ALU.add).then_inc(S["t_ready"], 1)
                dve.wait_ge(S["t_mm"], it * 2 + 1)
                stt(tt, pb[2], -1.0, ebc(eye15), ALU.mult, ALU.add).then_inc(S["t_ready"], 1)
                dve.wait_ge(S["t_mm"], it * 2 + 2)
                link(stt(tt, pb[3], -0.25, ebc(eye13), ALU.mult, ALU.add))
                tt_(bdt, expand16(tt), mask8_for(B), ALU.mult).then_inc(S["t_ready"], 1)
                dve.wait_ge(S["z_mm"], it + 1)
                v_.tensor_copy(z, pb[0]).then_inc(S["z_new"], 1)
                v_.tensor_copy(zT, pb[1]).then_inc(S["z_new"], 1)
                dve.wait_ge(S["z_new"], it * 2 + 4)
                settled(dve)
                own.restart()
            tt_(bdz, expand16(zT), mask8_for(B), ALU.mult).then_inc(S["t_ready"], 1)
            dve.wait_ge(S["w2_mm"], 1)
            link(v_.tensor_copy(w2_bd[:, 0:4], ps[2].rearrange("p (b h e) -> p b h e", b=4, h=HEADS)))
            v_.tensor_copy(w2_bd[:, 4:8], ps[3].rearrange("p (b h e) -> p b h e", b=4, h=HEADS)
                           ).then_inc(S["w2_ev"], 1)
            for bi in range(2, 4):
                dve.wait_ge(S["oT_mm"], bi + 1)
                v_.tensor_copy(oT[:, 512 * bi:512 * bi + 512], ps[4 + bi]).then_inc(S["oT_evD"], 1)
            link(tt_(T, T, t0, ALU.add))
            link(tt_(arr3(T, C), arr3(T, C), bcrow("b_out"), ALU.add))
            dve.wait_ge(S["ao_mm"], 1)
            link(tt_(T, T, ps[0], ALU.add))

            layernorm(T, t0, 1e-5, 3).then_inc(S["ct_in"], 1)
            dve.wait_ge(S["lg_mm"], 1)
            link(ts_(probs, ps[2][:, 0:N], par_("gate_b"), None, ALU.add))
            v_.tensor_reduce(small[:, 105:106], probs, AX.X, ALU.max, negate=True).then_inc(S["lg_max"], 1)
            dve.wait_ge(S["lg_exp"], 1)
            link(v_.reciprocal(small[:, 107:108], small[:, 106:107]))
            link(ts_(probs, probs, small[:, 107:108], None, ALU.mult))
            link(v_.max(small[:, 192:200], probs))
            link(v_.match_replace(probs_rest, small[:, 192:200], probs, 0.0))
            tt_(probs, probs, probs_rest, ALU.subtract).then_inc(S["topk"], 1)
            dve.wait_ge(S["mT_mm"], 1)
            v_.tensor_copy(mT.rearrange("p t e -> p (t e)"), ps[3][:, 0:N]).then_inc(S["mT_ev"], 1)
            dve.wait_ge(S["pl_mm"], 1)
            v_.tensor_copy(pooled[0:C, :], ps[4][0:C, 0:P]).then_inc(S["pl_ev"], 1)
            dve.wait_ge(S["eo_mm"], 1)
            v_.tensor_copy(eo.rearrange("o (b e) -> o e b", b=B),
                           ps[6][0:C, 0:P].rearrange("o (e b) -> o e b", e=EXP)).then_inc(S["eo_ev"], 1)
            dve.wait_ge(S["eoT_mm"], 1)
            tt_(eo_bd, ps[7][:, 0:C].unsqueeze(1).to_broadcast([P, B, C]),
                mask8.unsqueeze(2).to_broadcast([P, B, C]), ALU.mult).then_inc(S["eo_bd"], 1)
            dve.wait_ge(S["moe_mm"], 1)
            link(tt_(T, T, ps[0], ALU.add))

            link(layernorm(T, ZT_, 1e-5, 4))
            v_.tensor_copy(small[:, 201:202], small[:, 4:5]).then_inc(S["ct_in"], 1)
            v_.tensor_copy(small[:, 202:203], small[:, 4:5]).then_inc(S["la_z"], 1)
            m4 = mask4.unsqueeze(1).unsqueeze(3)
            dve.wait_ge(S["la_z"], 2)
            own.restart()
            with dve.Fori(0, LAYERS) as l:
                dve.wait_ge(S["la_g"], l + 1)
                tt_(g_bd.rearrange("p (g b o) -> p g b o", g=BG, b=BI),
                    ps[2][:, 0:BG * P].rearrange("p (g b o) -> p g b o", g=BG, b=BI),
                    m4.to_broadcast([P, BG, BI, C]), ALU.mult).then_inc(S["la_gev"], 1)
                dve.wait_ge(S["la_r"], l + 2)
                link(tt_(r_bd.rearrange("p (g b o) -> p g b o", g=BG, b=BI),
                         ps[4][:, 0:BG * C].rearrange("p (g o) -> p g o", g=BG).unsqueeze(2)
                         .to_broadcast([P, BG, BI, C]), m4.to_broadcast([P, BG, BI, C]), ALU.mult))
                ts_(r_bd, r_bd, 1.0 / (N * LHEADS), None, ALU.mult).then_inc(S["la_rev"], 1)
                dve.wait_ge(S["la_zmm"], l + 1)
                tt_(ZC, ZC, ps[5], ALU.add).then_inc(S["la_z"], 1)
                tt_(ZT_, ZT_, ps[6], ALU.add).then_inc(S["la_z"], 1)
                dve.wait_ge(S["la_z"], 2 * l + 4)
                settled(dve)
                own.restart()
            link(tt_(T, T, ZT_, ALU.add))

            link(layernorm(T, ln_b, 1e-5, 5))
            v_.tensor_copy(small[:, 201:202], small[:, 4:5]).then_inc(S["ct_in"], 1)
            stt(flagb, maskb, 2.0, flagb, ALU.mult, ALU.add).then_inc(S["ct_in"], 1)
            dve.wait_ge(S["ct_in"], 5)
            own.restart()
            with dve.Fori(0, NB) as s:
                dve.wait_ge(S["op_mm"], s + 1)
                settled(dve)
                link(v_.max(top8, ps[0][0:1, 0:NOPS]))
                dve.wait_ge(S["op_read"], 3 * s + 1)
                settled(dve)
                v_.max_index(op8, top8, ps[0][0:1, 0:NOPS]).then_inc(S["op_ev"], 1)
                dve.wait_ge(S["op_ev"], s + 1)
                settled(dve)
                own.restart()
                op = dve.value_load(op8[0:1, 0:1], min_val=0, max_val=NOPS - 1)
                fl = dve.value_load(flagb[0:1, bass.ds(s * NOPS + op, 1)], min_val=0, max_val=3)
                ffn = dve.snap(fl % 2)
                with dve.If(fl >= 2):
                    dve.wait_ge(S["w_in"], (s + 1) * 80)
                    tt_(w_bd.rearrange("p (w b o) -> p w b o", w=4, b=BI),
                        recA[:, HID:HID + 4 * C].rearrange("p (w o) -> p w o", w=4).unsqueeze(2)
                        .to_broadcast([P, 4, BI, C]), m4.to_broadcast([P, 4, BI, C]), ALU.mult
                        ).then_inc(S["w_bd"], 1)
                    dve.wait_ge(S["rq_mm"], 2 * s + 2)
                    v_.tensor_copy(rk, ps[2]).then_inc(S["rk_ev"], 1)
                    for b in range(B):
                        dve.wait_ge(S["sc_mm"], s * B + b + 1)
                        v_.tensor_reduce(rmax[:, 2 * b:2 * b + 2], arr3(ps[b], N), AX.X, ALU.max,
                                         negate=True).then_inc(S["sc_max"], 1)
                    for b in range(B):
                        dve.wait_ge(S["sc_exp"], s * B + b + 1)
                        r = rsum[:, 2 * b:2 * b + 2]
                        link(v_.reciprocal(r, r))
                        pb3 = arr3(pr[:, b * 512:b * 512 + 512], N)
                        tt_(pb3, pb3, r.unsqueeze(2).to_broadcast([P, 2, N]), ALU.mult).then_inc(S["sc_norm"], 1)
                    dve.wait_ge(S["ro_mm"], s + 1)
                    link(v_.tensor_copy(roC[:, 0:N], ps[0][:, 0:N]))
                    v_.tensor_copy(roC[:, N:2 * N], ps[1][:, 0:N]).then_inc(S["ro_ev"], 1)
                    dve.wait_ge(S["ry_mm"], s + 1)
                    v_.tensor_copy(hC, ps[2]).then_inc(S["rt_h"], 1)
                    dve.wait_ge(S["rt_h"], s + 1)
                    settled(dve)
                    own.restart()
                with dve.Else():
                    dve.sem_inc(S["w_bd"], 1)
                    dve.sem_inc(S["rk_ev"], 1)
                    dve.sem_inc(S["sc_max"], B)
                    dve.sem_inc(S["sc_norm"], B)
                    dve.sem_inc(S["ro_ev"], 1)
                    dve.sem_inc(S["rt_h"], 1)
                with dve.If(ffn != 0):
                    dve.wait_ge(S["w_in"], (s + 1) * 80)
                    for bi in range(2, 4):
                        dve.wait_ge(S["f1_mm"], s * BI + bi + 1)
                        ts_(f1[:, 512 * bi:512 * bi + 512], ps[4 + bi], recB[:, C:C + 1], 0.0, ALU.add, ALU.max
                            ).then_inc(S["f1_evD"], 1)
                    dve.wait_ge(S["f2mm"], s + 1)
                    ts_(hC, ps[1], recA[:, REC_A - 1:REC_A], None, ALU.add).then_inc(S["h_new"], 1)
                    dve.wait_ge(S["h_new"], s + 2)
                    settled(dve)
                with dve.Else():
                    dve.sem_inc(S["f1_evD"], 2)
                    dve.sem_inc(S["h_new"], 1)
            dve.wait_ge(S["ct_ev"], 3)
            tt_(outC, tC, hC, ALU.add).then_inc(S["out_ready"], 1)


def constants():
    c = np.zeros((P, CST_COLS), np.float32)
    p = np.arange(P)

    def put(n, a):
        c[:, CST[n][0]:CST[n][1]] = a.reshape(P, -1)

    put("ident", np.eye(P))
    put("flip", np.eye(P)[::-1])
    put("mask4", p[:, None] // 32 == np.arange(4))
    put("mask8", p[:, None] // 16 == np.arange(8))
    put("iota", np.broadcast_to(np.arange(16), (P, 16)))
    put("mask16", p[:, None] // 16 == p[None, :] // 16)
    put("swap", (p[:, None] ^ 1) == p[None, :])
    put("eye", np.stack([s * (p[:, None] % 16 == np.arange(16)) for s in (7.0, 15.0, 3.25)], 1))
    k = np.arange(KK)
    t = np.arange(PT)
    y = t[None, :, None] * 8 + p[:, None, None] // 16 + k // 3 - 1
    xx = p[:, None, None] % 16 + k % 3 - 1 + 0 * t[None, :, None]
    put("base", np.stack([y, xx], -1))
    n = np.arange(N)
    ang = (np.outer(n // 16, n // 16) + np.outer(n % 16, n % 16)) % 16 * (2 * np.pi / 16)
    co, si = np.cos(ang), np.sin(ang)
    d = np.concatenate([co, -si, -co], 1).reshape(PT, P, 3 * N).transpose(1, 0, 2)
    put("dft", d)
    return c


def kernel(x, **w):
    from concourse import bacc
    from concourse.bass_utils import run_bass_kernel_spmd

    w = {k: np.asarray(v) for k, v in w.items()}

    def taps(a):
        return a.transpose(1, 2, 3, 0).reshape(C, -1)

    def words(mask):
        return np.pad(mask.view(np.uint8).reshape(1, -1, 1), ((0, 0), (0, 0), (0, 3))).view(np.int32)[:, :, 0]

    arrays = {
        "x": np.ascontiguousarray(np.asarray(x).reshape(B, C, N)),
        "cst": constants(),
        "w32": np.concatenate([
            taps(w["L0_conv_w_off"]), taps(w["L0_conv_w_dcn"]), taps(w["L1_conv_conv_w"]), w["L2_attn_w_qkv"],
            w["L2_ffn_gate_w"].T, w["L3_attn_v_matrix"][:, :, 0].transpose(3, 0, 1, 2).reshape(C, -1),
            w["L3_attn_q_matrix"][:, :, 0].transpose(3, 0, 1, 2).reshape(C, -1)], 1),
        "par": np.stack([
            w["L1_conv_bn1_g"], w["L1_conv_bn1_b"], w["L1_conv_bn1_m"], w["L1_conv_bn1_v"],
            w["L1_conv_cg2_w"].reshape(CH), w["L1_conv_cg2_b"], w["L1_conv_cg1_w"].reshape(CH)]
            + [np.broadcast_to(w["L1_conv_" + n], (CH,)) for n in ("cg1_b", "cgbn_g", "cgbn_b", "cgbn_m", "cgbn_v")]
            + [np.repeat(w["L1_conv_tau"].reshape(-1), 2), w["L2_ffn_gate_b"]], 1),
        "rows": np.concatenate([w["L0_conv_b_off"], w["L2_attn_ln_w"], w["L2_attn_ln_b"], w["L2_attn_b_out"]]),
        "toep": np.pad(w["L2_attn_res_w"].reshape(HEADS, KRES),
                       ((0, 0), (2 * P - KRES // 2 - 1, TOEP_PAD - 2 * P + 1 - KRES + KRES // 2))),
        "w_out": w["L2_attn_w_out"],
        "moe_w1": np.ascontiguousarray(w["L2_ffn_weight1"].transpose(1, 0, 2)),
        "moe_w2": np.ascontiguousarray(w["L2_ffn_weight2"][:, :HID].transpose(1, 0, 2)),
        "moe_b2": w["L2_ffn_weight2"][:, HID].reshape(1, -1),
        "am": words(w["L3_ffn_attn_mask"]),
        "fm": words(w["L3_ffn_ffn_mask"]),
        "rec_a": np.concatenate([w["L3_ffn_ffn_w1"], w["L3_ffn_wq"], w["L3_ffn_wk"], w["L3_ffn_wv"], w["L3_ffn_wo"],
                                 w["L3_ffn_ffn_b2"][..., None]], -1).reshape(NB * NOPS, C, REC_A),
        "rec_b": np.concatenate([w["L3_ffn_ffn_w2"], w["L3_ffn_ffn_b1"][..., None]], -1
                                ).reshape(NB * NOPS, HID, REC_B),
    }
    arrays = {k: np.ascontiguousarray(a) for k, a in arrays.items()}
    nc = bacc.Bacc("TRN2", target_bir_lowering=False, num_devices=1)
    args = [nc.dram_tensor(k, a.shape, mybir.dt.from_np(a.dtype), kind="ExternalInput").ap()
            for k, a in arrays.items()]
    out = nc.dram_tensor("out", (B, C, N), F32, kind="ExternalOutput").ap()
    build(nc, *args, out)
    r = run_bass_kernel_spmd(nc, [arrays], core_ids=[0])
    return r.results[0]["out"].reshape(B, C, HH, WW)
```

```python
from contextlib import ExitStack

import numpy as np

import concourse.bass as bass
from concourse import mybir
from concourse.alu_op_type import AluOpType as ALU

F32 = mybir.dt.float32
I32 = mybir.dt.int32
U32 = mybir.dt.uint32
ACT = mybir.ActivationFunctionType
AX = mybir.AxisListType

B, C, HH, WW = 8, 32, 16, 16
N = HH * WW
P = 128
BI, BG, PT = 4, 2, 2
KK = 9
NOFF = 2 * KK
CH = 16
HEADS, DH, LM = 8, 16, 16
PINV = 6
KRES = 33
EXP, HID = 16, 128
LAYERS, LHEADS = 4, 8
LAG = 3
NB, NOPS = 33, 19
RUNS, RUN = 5, 7
NONE = 4096
SMALL = 16 * (B + 1)
LATE = 16 * (BI + 8)

W32 = {}
_at = 0
for _n, _k in (("off", KK * NOFF), ("dcn", KK * C), ("conv", KK * CH), ("qkv", 3 * P), ("gate", EXP),
               ("v", LAYERS * LHEADS * C), ("q", LAYERS * LHEADS * C)):
    W32[_n] = (_at, _at + _k)
    _at += _k
W32_COLS = _at
W32_EARLY = W32["conv"][1]

CST = {}
_at = 0
for _n, _k in (("ident", P), ("flip", P), ("mask4", BI), ("mask8", HEADS), ("base", PT * NOFF), ("iota", 16),
               ("mask16", P), ("swap", P), ("eye", 48), ("dft", 2 * 3 * N)):
    CST[_n] = (_at, _at + _k)
    _at += _k
CST_COLS = _at

PAR = ("bn_g", "bn_b", "bn_m", "bn_v", "cg2_w", "cg2_b", "cg1_w", "cg1_b", "cgbn_g", "cgbn_b", "cgbn_m",
       "cgbn_v", "tau", "gate_b")
ROWS = {"b_off": (0, NOFF), "ln_w": (NOFF, NOFF + C), "ln_b": (NOFF + C, NOFF + 2 * C),
        "b_out": (NOFF + 2 * C, NOFF + 3 * C)}
ROW_COLS = NOFF + 3 * C
TOEP_PAD = 512

REC_A = HID + 4 * C + 1
REC_B = C + 1

SEMS = (
    "x_in", "cst_in", "w32_in", "par_in", "late_in",
    "pool_zero", "pool_bd", "gn_var", "gn_std", "xn", "off_mm", "off_ev", "g_mm", "g_ev", "diff", "hat",
    "prod", "tr", "s_ev", "gst", "dcn_mm", "x1_ready",
    "conv_mm", "bn_var", "bn_std", "bn_ready", "feat", "featT_mm", "featT_ev", "f2_mm", "f2_ev", "swap_mm",
    "l2_sum", "l2_std", "sm2_in", "sm2_exp", "mix", "mix_abs", "cg_mm", "cg_act", "gated", "gT_mm",
    "gT_ev", "inv_mm", "inv_sq", "inv_add", "inv_abs", "toT_mm", 
    "ln_var", "ln_std", "ct_in", "ct_mm", "ct_ev",
    "qk_mm", "q_ev", "k_ev", "pool_in", "lk_mm", "lk_ev", "ql_bd", "kl_bd", "v_mm", "v_ev", "sim2_mm",
    "sim3_mm", "a3_max", "a3_exp", "a3T_mm", "a3T_ev", "w3_mm", "w3_ev", "sim1_mm", "a1_sub", "a1_exp",
    "a1_norm", "a1_sum", "a1T_mm", "a1T_ev", "res_mm", "res_ev", "a2_sub", "a2_exp", "x_bd", "xT_mm", 
    "cr_in", "cr_max", "z_new", "zT_bd", "xz_mm", "x_ev", "tt_new", "t_ready", "t_mm", "w2_mm", "w2_ev",
    "oT_mm", "oT_evA", "oT_evD", "ao_mm",
    "lg_mm", "lg_max", "lg_exp", "topk", "mT_mm", "mT_ev", "pl_mm", "pl_ev", "hid_mm", "hid_ev", "eo_mm",
    "eo_ev", "eoT_mm", "eo_bd", "moe_mm",
    "la_z", "la_g", "la_gev", "la_h", "la_hev", "la_qbd", "la_r", "la_rev", "la_zmm", 
    "rt_h", "op_mm", "op_read", "op_ev", "w_in", "w_bd", "w1_bd", "w_used", "tok_mm", "tok_ev", "rq_mm", "rq_ev", "rk_ev", "rv_mm", "rv_ev", "sc_mm",
    "sc_max", "sc_exp", "sc_norm", "pT_mm", "pT_ev", "ro_mm", "ro_ev", "ry_mm",
    "f1_mm", "f1_ev", "f2mm", "h_new", "out_ready", "out_st",
    "dve_own", "act_own", "pool_own", "passed",
)


class Own:

    def __init__(self, eng, sem):
        self.eng, self.sem, self.n = eng, sem, 0

    def link(self, ins):
        self.n += 1
        ins.then_inc(self.sem, 1)
        self.eng.wait_ge(self.sem, self.n)

    def restart(self):
        self.eng.sem_clear(self.sem)
        self.n = 0


def build(nc, x, cst, w32, par, rows, toep, w_out, moe_w1, moe_w2, moe_b2, am, fm, keys, rec_a, rec_b, out):
    ctx = ExitStack()
    with ctx:
        def sb(name, cols, dt=F32, parts=P):
            return ctx.enter_context(nc.sbuf_tensor(name, [parts, cols], dt))[:, :]

        S = {n: ctx.enter_context(nc.semaphore(n)) for n in SEMS}
        ps = [ctx.enter_context(nc.psum_tensor(f"ps{i}", [P, 512], F32))[:, :] for i in range(8)]

        xC = sb("xC", 512)
        cstb = sb("cstb", CST_COLS)
        w32b = sb("w32b", W32_COLS)
        parb = sb("parb", len(PAR))
        rowb = sb("rowb", ROW_COLS)
        woutb = sb("woutb", C)
        w1b = sb("w1b", EXP * HID, parts=C + 1)
        w2b = sb("w2b", EXP * C)
        b2b = sb("b2b", EXP * C, parts=1)
        maskb = sb("maskb", NB * NOPS, I32, parts=1)
        flagb = sb("flagb", NB * NOPS, I32, parts=1)

        def cst_(n):
            return cstb[:, CST[n][0]:CST[n][1]]

        def w32_(n):
            return w32b[:, W32[n][0]:W32[n][1]]

        def par_(n):
            return parb[:, PAR.index(n):PAR.index(n) + 1]

        def row_(n):
            return rowb[:, ROWS[n][0]:ROWS[n][1]]

        ident, mask4, mask8, iota = cst_("ident"), cst_("mask4"), cst_("mask8"), cst_("iota")
        eye7, eye15, eye13 = (cst_("eye")[:, 16 * i:16 * i + 16] for i in range(3))
        dft = cst_("dft").rearrange("p (t n) -> p t n", t=PT)

        arena = sb("arena", 20480)

        def ar(at, cols):
            return arena[:, at:at + cols]

        xnp = ar(18208, BG * 18 * 18).rearrange("p (g y x) -> p g y x", g=BG, y=18)
        xn = ar(18856, BG * N)
        offC = ar(19368, BG * N)
        dcn_bd = ar(13312, BI * KK * C).rearrange("p (b n) -> p b n", b=BI)
        xp = sb("xp", BG * 22 * 22).rearrange("p (g y x) -> p g y x", g=BG, y=22)
        off_bd = sb("off_bd", KK * BI * NOFF).rearrange("p (k b o) -> p k b o", k=KK, b=BI)
        conv_bd = sb("conv_bd", KK * BI * CH).rearrange("p (k b o) -> p k b o", k=KK, b=BI)
        gate_bd = sb("gate_bd", BI * EXP).rearrange("p (b o) -> p b o", b=BI)
        cgw = sb("cgw", P)
        base2 = sb("base2", PT * NOFF).rearrange("p (t o) -> p t o", t=PT)
        zeros = sb("zeros", P)
        x1C = sb("x1C", 512)
        small = sb("small", 512)
        T = sb("T", 512)
        t0 = sb("t0", 512)
        ln_a = sb("ln_a", 512)
        ln_b = sb("ln_b", 512)
        lnC = sb("lnC", 512)
        tC = sb("tC", 512)
        T4 = T.rearrange("p (t b c) -> p t b c", t=PT, b=B)

        GS = ar(0, 4608).rearrange("p (g t b k o) -> p g t b k o", g=BG, t=PT, b=BI, k=KK)
        hat = ar(4608, 4608).rearrange("p (t b k a q) -> p t b k a q", t=PT, b=B, k=KK, a=2)
        ST = ar(9216, 4096).rearrange("p (c t y x) -> p c t y x", c=B, t=PT, y=HH)
        SQ = ar(13312, 4096).rearrange("p (c q n) -> p c q n", c=B, q=PT)
        yx = ar(17408, 288).rearrange("p (t b o) -> p t b o", t=PT, b=B)
        Gst = ar(17696, 512).rearrange("p (g t b o) -> p g t b o", g=BG, t=PT, b=BI)

        feat = sb("feat", N)
        featT = sb("featT", PT * P).rearrange("p (t n) -> p t n", t=PT)
        F2 = ar(18432, 2 * N)
        mixed = ar(18944, 2 * N)
        outf = sb("outf", N)
        gatef = sb("gatef", N)
        scr = sb("scr", 512)
        gated = ar(19456, 512)
        gT = ar(19968, 512).rearrange("p (a t n) -> p a t n", a=2, t=PT)
        cg = sb("cg", N)

        qT, kT, V, a1, a1T, a3, a3T, res, oT = (ar(2048 * i, 2048) for i in range(9))
        toepb = sb("toepb", HEADS * 384).rearrange("p (h n) -> p h n", h=HEADS)
        ql_bd, kl_bd, bdXT, bdz, bdzT, w3_bd = (
            sb(n, 1024).rearrange("p (b h m) -> p b h m", b=B, h=HEADS)
            for n in ("ql_bd", "kl_bd", "bdXT", "bdz", "bdzT", "w3_bd"))
        bdxzT, bdt, w2_bd = (a.rearrange("p (b h m) -> p b h m", b=B, h=HEADS)
                             for a in (a3[:, 0:1024], a3[:, 1024:2048], kT[:, 0:1024]))
        ql, kl, XM, XT, z, zT, tt = (sb(n, P).rearrange("p (b m) -> p b m", b=B)
                                     for n in ("ql", "kl", "XM", "XT", "z", "zT", "tt"))
        xpool = sb("xpool", BG * LM)
        pX, pY = xC[:, 0:2 * P], xC[:, 2 * P:4 * P]

        probs = sb("probs", N)
        probs_rest = sb("probs_rest", N)
        mT = sb("mT", N).rearrange("p (t e) -> p t e", t=PT)
        pooled = sb("pooled", P, parts=C + 1)
        hid = sb("hid", EXP * B).rearrange("p (e b) -> p e b", e=EXP)
        eo = sb("eo", P, parts=C)
        eo_bd = sb("eo_bd", B * C).rearrange("p (b o) -> p b o", b=B)
        ones1 = sb("ones1", B, parts=1)

        ZT_, ZC = sb("ZT_", 512), sb("ZC", 512)
        g_bd = ar(12288, BG * P)
        hs = ar(12544, BG * LHEADS * C).rearrange("p (g j o) -> p g j o", g=BG, j=LHEADS)
        q_bd = ar(13312, LHEADS * P).rearrange("p (j b o) -> p j b o", j=LHEADS, b=BI)
        r_bd = ar(14336, BG * P)

        hC = sb("hC", 512)
        recA = sb("recA", REC_A)
        recB = sb("recB", REC_B)
        top8 = sb("top8", 8, parts=1)
        op8 = sb("op8", 8, U32, parts=1)
        w_bd = ar(0, 512)
        rk, rv, roC = (ar(512 * (1 + i), 512) for i in range(3))
        f1 = ar(3072, 2048)
        rq_bd = f1.rearrange("p (b n) -> p b n", b=BI)
        pr = ar(5120, 4096)
        prT = ar(9216, 4096)
        rmax = sb("rmax", 16)
        rsum = sb("rsum", 16)
        keyb = off_bd.rearrange("p k b o -> p (k b o)")[0:1, 0:NB * NOPS]
        stepb, passed, cand, key = (sb(n, k, parts=1) for n, k in
                                    (("stepb", NB), ("passed_", NB), ("cand", NB), ("key", 1)))
        keyi = sb("keyi", 1, I32, parts=1)
        keyf = ar(15360, NB * NOPS)[0:1, :]
        w2c, b2c, f1t = sb("w2c", REC_B), sb("b2c", 1), sb("f1t", 1)
        w1_bd = ar(13312, BI * HID)
        outC = ln_a

        def expand16(compact):
            return compact.unsqueeze(2).to_broadcast([P, compact.shape[1], HEADS, 16])

        def mask8_for(nb):
            return mask8.unsqueeze(1).unsqueeze(3).to_broadcast([P, nb, HEADS, 16])

        def window(buf, g, y0, x0, rows):
            return buf[:, g, y0:y0 + rows, x0:x0 + WW]

        def arr3(a, k):
            return a.rearrange("p (j k) -> p j k", k=k)

        def settled(eng):
            eng.sem_inc(S["passed"], 1)

        def routed(eng, body):
            with eng.Fori(0, RUNS) as i:
                more = eng.value_load(keyi[0:1, 0:1], min_val=0, max_val=2 * NONE)
                with eng.If(more < NONE):
                    with eng.Fori(0, RUN) as j:
                        k = eng.value_load(keyi[0:1, 0:1], min_val=0, max_val=2 * NONE)
                        with eng.If(k < NONE):
                            body(eng.snap(i * RUN + j), k)

        block = ctx.enter_context(nc.Block())

        @block.sync
        def _(sp):
            sp.dma_start(xC.rearrange("p (g n) -> p g n", g=BG),
                         x.rearrange("(g b) c n -> (b c) g n", g=BG)).then_inc(S["x_in"], 16)
            sp.dma_start(cstb, cst).then_inc(S["cst_in"], 16)
            for bi in range(BI):
                sp.dma_start(w32b[32 * bi:32 * bi + 32, 0:W32_EARLY], w32[:, 0:W32_EARLY]).then_inc(S["w32_in"], 16)
            sp.dma_start(rowb, rows.partition_broadcast(P)).then_inc(S["par_in"], 16)
            for b in range(B):
                sp.dma_start(parb[16 * b:16 * b + 16, :], par).then_inc(S["par_in"], 16)
            for bi in range(BI):
                sp.dma_start(w32b[32 * bi:32 * bi + 32, W32_EARLY:W32_COLS],
                             w32[:, W32_EARLY:W32_COLS]).then_inc(S["late_in"], 16)
            sp.dma_start(toepb, bass.AP(tensor=toep.tensor, offset=0, ap=[[1, P], [TOEP_PAD, HEADS], [1, 384]])
                         ).then_inc(S["late_in"], 16)
            sp.dma_start(woutb, w_out).then_inc(S["late_in"], 16)
            sp.dma_start(w1b.rearrange("d (e h) -> d e h", e=EXP), moe_w1).then_inc(S["late_in"], 16)
            sp.dma_start(w2b.rearrange("h (e o) -> h e o", e=EXP), moe_w2).then_inc(S["late_in"], 16)
            sp.dma_start(b2b, moe_b2).then_inc(S["late_in"], 16)
            sp.dma_start(maskb, am).then_inc(S["late_in"], 16)
            sp.dma_start(flagb, fm).then_inc(S["late_in"], 16)
            sp.wait_ge(S["off_mm"], BG)
            sp.dma_start(keyb, keys).then_inc(S["late_in"], 16)

            sp.sem_inc(S["w_used"], 1)
            sp.wait_ge(S["op_ev"], 1)

            def load_record(n, k):
                rec = nc.s_assert_within(sp.snap(k // 4), 0, NB * NOPS - 1, skip_runtime_bounds_check_because=
                                         "a key below NONE is an active step's, so its record exists")
                sp.wait_ge(S["w_used"], n + 1)
                sp.dma_start(recA,
                             rec_a[bass.ds(rec, 1), :, :].to_broadcast([BI, C, REC_A])).then_inc(S["w_in"], 16)
                sp.dma_start(recB, rec_b[bass.ds(rec, 1), :, :].rearrange("a c n -> (a c) n")
                             ).then_inc(S["w_in"], 16)
                sp.sem_inc(S["op_read"], 1)
                sp.wait_ge(S["op_ev"], n + 2)
                settled(sp)

            routed(sp, load_record)
            sp.wait_ge(S["out_ready"], 1)
            sp.dma_start(out.rearrange("(g b) c n -> (b c) g n", g=BG),
                         outC.rearrange("p (g n) -> p g n", g=BG)).then_inc(S["out_st"], 16)
            sp.wait_ge(S["out_st"], 16)

        @block.gpsimd
        def _(pool):
            own = Own(pool, S["pool_own"])
            nc.gpsimd.memset(xnp, 0.0).then_inc(S["pool_zero"], 1)
            nc.gpsimd.memset(zeros, 0.0).then_inc(S["pool_zero"], 1)
            nc.gpsimd.memset(xp, 0.0).then_inc(S["pool_zero"], 1)
            pool.wait_ge(S["pool_zero"], 3)
            nc.gpsimd.memset(pooled[C:C + 1, :], 1.0).then_inc(S["pool_zero"], 1)
            pool.wait_ge(S["pool_zero"], 4)
            nc.gpsimd.memset(ones1, 1.0).then_inc(S["pool_zero"], 1)
            pool.wait_ge(S["cst_in"], 16)
            pool.wait_ge(S["w32_in"], 64)
            pool.wait_ge(S["par_in"], SMALL)

            def bd4(dst, src, k, o):
                m = mask4.unsqueeze(1).unsqueeze(3).to_broadcast([P, k, BI, o])
                s = src.rearrange("p (k o) -> p k o", k=k).unsqueeze(2).to_broadcast([P, k, BI, o])
                return nc.gpsimd.tensor_tensor(dst, s, m, ALU.mult)

            bd4(off_bd, w32_("off"), KK, NOFF).then_inc(S["pool_bd"], 1)
            nc.gpsimd.tensor_tensor(dcn_bd, w32_("dcn").unsqueeze(1).to_broadcast([P, BI, KK * C]),
                                    mask4.unsqueeze(2).to_broadcast([P, BI, KK * C]), ALU.mult
                                    ).then_inc(S["pool_bd"], 1)
            nc.gpsimd.tensor_tensor(base2, cst_("base").rearrange("p (t o) -> p t o", t=PT),
                                    row_("b_off").unsqueeze(1).to_broadcast([P, PT, NOFF]),
                                    ALU.add).then_inc(S["pool_bd"], 1)
            bd4(conv_bd, w32_("conv"), KK, CH).then_inc(S["pool_bd"], 1)
            pool.wait_ge(S["par_in"], SMALL)
            nc.gpsimd.tensor_scalar(cgw, cst_("mask16"), par_("cg1_w"), None, ALU.mult).then_inc(S["pool_bd"], 1)
            pool.wait_ge(S["late_in"], LATE)
            nc.gpsimd.tensor_tensor(gate_bd, w32_("gate").unsqueeze(1).to_broadcast([P, BI, EXP]),
                                    mask4.unsqueeze(2).to_broadcast([P, BI, EXP]), ALU.mult
                                    ).then_inc(S["pool_bd"], 1)
            pool.wait_ge(S["g_ev"], BG * PT * BI)
            with pool.Fori(0, KK) as k:
                pool.wait_ge(S["dcn_mm"], k * BG + BG)
                nc.gpsimd.tensor_copy(Gst.rearrange("p g t b o -> p (g t b) o"),
                                      GS.rearrange("p g t b k o -> p (g t b) k o")[:, :, bass.ds(k, 1), :]
                                      .rearrange("p a k o -> p a (k o)")).then_inc(S["gst"], 1)
            pool.wait_ge(S["lk_ev"], 1)
            nc.gpsimd.tensor_tensor(ql_bd, expand16(ql), mask8_for(B), ALU.mult).then_inc(S["ql_bd"], 1)
            for bi in range(BI):
                pool.wait_ge(S["a1_sum"], bi + 1)
                v = arr3(a1[:, 512 * bi:512 * bi + 512], 16)
                nc.gpsimd.tensor_tensor(v, v, small[:, 256 + 32 * bi:288 + 32 * bi].unsqueeze(2)
                                        .to_broadcast([P, 32, 16]), ALU.mult).then_inc(S["a1_norm"], 1)
            pool.wait_ge(S["cr_in"], 1)
            nc.gpsimd.partition_all_reduce(small[:, 32:34], small[:, 16:18], P, bass.bass_isa.ReduceOp.max
                                           ).then_inc(S["cr_max"], 1)
            with pool.Fori(0, PINV) as it:
                pool.wait_ge(S["z_new"], it * 2 + 2)
                nc.gpsimd.tensor_tensor(bdzT, expand16(zT), mask8_for(B), ALU.mult).then_inc(S["zT_bd"], 1)
            with pool.Fori(0, LAYERS) as l:
                pool.wait_ge(S["la_r"], l + 1)
                src = w32_("q").rearrange("p (l n) -> p l n", l=LAYERS)[:, bass.ds(l, 1), :]
                src = src.rearrange("p l (j o) -> p (l j) o", o=C).unsqueeze(2).to_broadcast([P, LHEADS, BI, C])
                nc.gpsimd.tensor_tensor(q_bd, src, mask4.unsqueeze(1).unsqueeze(3)
                                        .to_broadcast([P, LHEADS, BI, C]), ALU.mult).then_inc(S["la_qbd"], 1)

        @block.tensor
        def _(pe):
            mm = nc.tensor.matmul
            tr = nc.tensor.transpose

            def to_C(src, bank, n):
                for g in range(BG):
                    for t in range(PT):
                        c0 = (t * B + g * BI) * C
                        last = tr(ps[bank][:, (g * PT + t) * P:(g * PT + t + 1) * P], src[:, c0:c0 + P], ident)
                last.then_inc(n, 1)

            pe.wait_ge(S["xn"], 2 * BG)
            pe.wait_ge(S["pool_bd"], 1)
            for g in range(BG):
                for k in range(KK):
                    last = mm(ps[g][0:BI * NOFF, 0:N], off_bd[:, k, :, :], window(xnp, g, k // 3, k % 3, 16),
                              start=(k == 0), stop=(k == KK - 1))
                last.then_inc(S["off_mm"], 1)
            pe.wait_ge(S["pool_bd"], 2)
            for r in range(BG * PT):
                if r:
                    pe.wait_ge(S["g_ev"], r * BI)
                for bi in range(BI):
                    last = mm(ps[4 + bi][:, 0:KK * C], xn[:, r * P:r * P + P], dcn_bd[:, bi, :],
                              start=True, stop=True)
                last.then_inc(S["g_mm"], 1)
                if r == 0:
                    pe.wait_ge(S["off_ev"], BG)
                    for t in range(PT):
                        for g in range(BG):
                            c0 = (t * BG + g) * BI * NOFF
                            last = tr(ps[2][:, c0:c0 + BI * NOFF],
                                      offC[0:BI * NOFF, g * N + t * P:g * N + t * P + P],
                                      ident[0:BI * NOFF, 0:BI * NOFF])
                    last.then_inc(S["off_mm"], 1)
            pe.wait_ge(S["g_ev"], BG * PT * BI)
            pe.wait_ge(S["pool_zero"], 2)
            for g in range(BG):
                mm(ps[4 + g][:, 0:N], zeros, xn[:, 0:N], start=True, stop=False)
            pe.sem_inc(S["dcn_mm"], BG)
            pe.sem_inc(S["tr"], B)
            with pe.Fori(0, KK) as k:
                for c in range(B):
                    pe.wait_ge(S["prod"], k * B + c + 1)
                    pe.wait_ge(S["s_ev"], k * B + c + 1)
                    for q in range(PT):
                        for t in range(PT):
                            last = tr(ps[c % BI][:, (q * PT + t) * P:(q * PT + t + 1) * P],
                                      ST[:, c, t, q * 8:q * 8 + 8, :], ident)
                    last.then_inc(S["tr"], 1)
                pe.wait_ge(S["gst"], k + 1)
                for g in range(BG):
                    pe.wait_ge(S["s_ev"], k * B + (g + 2) * BI)
                    for q in range(PT):
                        for bi in range(BI):
                            last = mm(ps[4 + g][32 * bi:32 * bi + 32, 0:N], Gst[:, g, q, bi, :],
                                      SQ[:, g * BI + bi, q, :], start=False, stop=False, skip_group_check=True)
                    last.then_inc(S["dcn_mm"], 1)
            for g in range(BG):
                mm(ps[4 + g][:, 0:N], zeros, xn[:, 0:N], start=False, stop=True).then_inc(S["dcn_mm"], 1)
            pe.wait_ge(S["x1_ready"], BG)
            pe.wait_ge(S["pool_bd"], 4)
            for g in range(BG):
                for k in range(KK):
                    last = mm(ps[g][64 * g:64 * g + 64, 0:N], conv_bd[:, k, :, :],
                              window(xp, g, 3 * (k // 3), 3 * (k % 3), 16), start=(k == 0), stop=(k == KK - 1))
                last.then_inc(S["conv_mm"], 1)
            pe.wait_ge(S["feat"], BG)
            for t in range(PT):
                last = tr(ps[2][:, t * P:t * P + P], feat[:, t * P:t * P + P], ident)
            last.then_inc(S["featT_mm"], 1)
            pe.wait_ge(S["featT_ev"], 1)
            for t in range(PT):
                last = mm(ps[3], featT[:, t, :], dft[:, t, 0:2 * N], start=(t == 0), stop=(t == PT - 1))
            last.then_inc(S["f2_mm"], 1)
            pe.wait_ge(S["f2_ev"], 1)
            mm(ps[4], cst_("swap"), F2, start=True, stop=True).then_inc(S["swap_mm"], 1)
            pe.wait_ge(S["pool_bd"], 5)
            mm(ps[6][:, 0:N], cgw, F2[:, 0:N], start=True, stop=True).then_inc(S["cg_mm"], 1)
            mm(ps[5][:, 0:N], cst_("swap"), feat, start=True, stop=True).then_inc(S["swap_mm"], 1)
            pe.wait_ge(S["gated"], 2)
            for a in range(2):
                for t in range(PT):
                    last = tr(ps[7][:, (a * PT + t) * P:(a * PT + t + 1) * P],
                              gated[:, a * N + t * P:a * N + t * P + P], ident)
            last.then_inc(S["gT_mm"], 1)
            pe.wait_ge(S["gT_ev"], 1)
            for n, (a, t) in enumerate(((0, 0), (0, 1), (1, 0), (1, 1))):
                last = mm(ps[2], gT[:, a, t, :], dft[:, t, a * N:a * N + 2 * N], start=(n == 0), stop=(n == 3))
            last.then_inc(S["inv_mm"], 1)
            for g in range(BG):
                for t in range(PT):
                    last = tr(ps[0][:, (t * BG + g) * P:(t * BG + g + 1) * P],
                              x1C[:, g * N + t * P:g * N + t * P + P], ident)
            last.then_inc(S["toT_mm"], 1)
            pe.wait_ge(S["mix_abs"], 1)
            pe.wait_ge(S["inv_abs"], 1)
            for n, src in enumerate((outf, gatef)):
                for t in range(PT):
                    last = tr(ps[1][:, (n * PT + t) * P:(n * PT + t + 1) * P], src[:, t * P:t * P + P], ident)
            last.then_inc(S["toT_mm"], 1)

            pe.wait_ge(S["ct_in"], 1)
            to_C(ln_b, 0, S["ct_mm"])
            pe.wait_ge(S["ct_ev"], 1)
            pe.wait_ge(S["late_in"], LATE)
            wq, wk, wv = (w32_("qkv")[:, P * i:P * i + P] for i in range(3))
            for w, bank in ((wq, 0), (wk, 4)):
                for bi in range(BI):
                    rr = slice(32 * bi, 32 * bi + 32)
                    mm(ps[bank + bi], w[rr, :], lnC[rr, :], start=True, stop=True).then_inc(S["qk_mm"], 1)
            pe.wait_ge(S["pool_in"], 1)
            for bi in range(BI):
                rr = slice(32 * bi, 32 * bi + 32)
                pe.wait_ge(S["q_ev"], bi + 1)
                mm(ps[bi][:, 0:32], wq[rr, :], xpool[rr, :], start=True, stop=True)
                mm(ps[bi][:, 32:64], wk[rr, :], xpool[rr, :], start=True, stop=True).then_inc(S["lk_mm"], 1)
            for bi in range(BI):
                rr = slice(32 * bi, 32 * bi + 32)
                pe.wait_ge(S["k_ev"], bi + 1)
                for g in range(BG):
                    for t in range(PT):
                        last = mm(ps[4 + bi][:, (g * PT + t) * P:(g * PT + t + 1) * P],
                                  lnC[rr, g * N + t * P:g * N + t * P + P], wv[rr, :], start=True, stop=True)
                last.then_inc(S["v_mm"], 1)
            pe.wait_ge(S["ql_bd"], 1)
            for b in range(B):
                last = mm(ps[0][:, 16 * b:16 * b + 16], ql_bd[:, b, :, :], kl[:, b, :], start=True, stop=True)
            last.then_inc(S["sim2_mm"], 1)
            for bi in range(BI):
                pe.wait_ge(S["v_ev"], bi + 1)
                for g in range(BG):
                    last = mm(ps[4 + bi][:, g * N:g * N + N], ql_bd[:, 2 * bi + g, :, :],
                              kT[:, 512 * bi + N * g:512 * bi + N * g + N], start=True, stop=True)
                last.then_inc(S["sim3_mm"], 1)
            for bi in range(BI):
                pe.wait_ge(S["a3_exp"], bi + 1)
                for j in range(4):
                    last = tr(ps[4 + bi][:, j * P:j * P + P], a3[:, 512 * bi + j * P:512 * bi + j * P + P], ident)
                last.then_inc(S["a3T_mm"], 1)
            for bi in range(BI):
                pe.wait_ge(S["a3T_ev"], bi + 1)
                for g in range(BG):
                    b = 2 * bi + g
                    for t in range(PT):
                        c0 = 512 * bi + (g * PT + t) * P
                        last = mm(ps[2 + b // 4][:, (b % 4) * P:(b % 4) * P + P], a3T[:, c0:c0 + P],
                                  V[:, c0:c0 + P], start=(t == 0), stop=(t == PT - 1))
            last.then_inc(S["w3_mm"], 1)
            pe.wait_ge(S["kl_bd"], 1)
            for bi in range(BI):
                for g in range(BG):
                    for t in range(PT):
                        c0 = 512 * bi + g * N + t * P
                        last = mm(ps[4 + bi][:, (g * PT + t) * P:(g * PT + t + 1) * P], qT[:, c0:c0 + P],
                                  kl_bd[:, 2 * bi + g, :, :], start=True, stop=True)
                last.then_inc(S["sim1_mm"], 1)
            pe.wait_ge(S["late_in"], LATE)
            pe.wait_ge(S["w3_ev"], 1)
            pe.wait_ge(S["a2_sub"], 1)
            Vb = V.rearrange("p (b t n) -> p b t n", b=B, t=PT)
            for t in range(PT):
                for h in range(HEADS):
                    for s in range(PT):
                        col = (1 - t + s) * P
                        last = mm(ps[2 * t + h // 4][:, (h % 4) * P:(h % 4) * P + P], toepb[:, h, col:col + P],
                                  Vb[:, :, s, h * DH:h * DH + DH], start=(s == 0), stop=(s == PT - 1))
                    if h % 4 == 3:
                        last.then_inc(S["res_mm"], 1)
            for bi in range(BI):
                pe.wait_ge(S["a1_norm"], bi + 1)
                for j in range(4):
                    last = tr(ps[4 + bi][:, j * P:j * P + P], a1[:, 512 * bi + j * P:512 * bi + j * P + P], ident)
                last.then_inc(S["a1T_mm"], 1)
            pe.wait_ge(S["x_bd"], 1)
            pe.wait_ge(S["res_ev"], 4)
            for b in range(B):
                last = tr(ps[b // 4][:, (b % 4) * P:(b % 4) * P + P], bdz[:, b, :, :], ident)
            last.then_inc(S["xT_mm"], 1)
            def head_product(bank, a, b_bd):
                for g in range(BG):
                    for j in range(BI):
                        b = g * BI + j
                        last = mm(ps[bank][32 * j:32 * j + LM, g * P:g * P + P], a[:, b, :], b_bd[:, b, :, :],
                                  start=True, stop=True)
                last.then_inc(S["xz_mm"], 1)

            def turn(bank, src):
                for g in range(BG):
                    last = tr(ps[bank][:, g * P:g * P + P], src[:, g * P:g * P + P], ident)
                last.then_inc(S["t_mm"], 1)

            with pe.Fori(0, PINV) as it:
                pe.wait_ge(S["z_new"], it * 2 + 2)
                head_product(0, z, bdXT)
                pe.wait_ge(S["t_ready"], it * 4 + 1)
                head_product(1, XT, bdz)
                pe.wait_ge(S["x_ev"], it * 6 + 1)
                turn(2, pX)
                pe.wait_ge(S["x_ev"], it * 6 + 2)
                turn(3, pY)
                for n in range(2):
                    pe.wait_ge(S["t_ready"], it * 4 + 2 + n)
                    head_product(0, tt, bdxzT)
                    pe.wait_ge(S["x_ev"], it * 6 + 3 + n)
                    turn(2, pX)
                pe.wait_ge(S["tt_new"], it + 1)
                pe.wait_ge(S["zT_bd"], it + 1)
                head_product(0, tt, bdzT)
                pe.wait_ge(S["t_ready"], it * 4 + 4)
                head_product(1, zT, bdt)
                pe.wait_ge(S["x_ev"], it * 6 + 5)
                turn(2, pX)
                pe.wait_ge(S["x_ev"], it * 6 + 6)
                turn(3, pY)
            pe.wait_ge(S["t_ready"], PINV * 4 + 2)
            for b in range(B):
                last = mm(ps[2 + b // 4][:, (b % 4) * P:(b % 4) * P + P], bdz[:, b, :, :], w3_bd[:, b, :, :],
                          start=True, stop=True)
            last.then_inc(S["w2_mm"], 1)
            pe.wait_ge(S["w2_ev"], 1)
            pe.wait_ge(S["a1T_ev"], BI)
            for bi in range(BI):
                for g in range(BG):
                    b = 2 * bi + g
                    mm(ps[4 + bi][:, g * N:g * N + N], w2_bd[:, b, :, :], a1T[:, N * b:N * b + N],
                       start=True, stop=False)
                    for t in range(PT):
                        last = mm(ps[4 + bi][:, g * N + t * P:g * N + t * P + P],
                                  res[:, (t * B + b) * P:(t * B + b + 1) * P], cst_("flip"),
                                  start=False, stop=(t == PT - 1))
                last.then_inc(S["oT_mm"], 1)
            pe.wait_ge(S["oT_evA"], 2)
            pe.wait_ge(S["oT_evD"], 2)
            pe.wait_ge(S["late_in"], LATE)
            for bi in range(BI):
                for g in range(BG):
                    for t in range(PT):
                        j = t * B + g * BI + bi
                        c0 = 512 * bi + g * N + t * P
                        last = mm(ps[0][:, j * C:j * C + C], oT[:, c0:c0 + P], woutb, start=True, stop=True)
            last.then_inc(S["ao_mm"], 1)

            pe.wait_ge(S["ct_in"], 2)
            to_C(t0, 1, S["ct_mm"])
            pe.wait_ge(S["ct_ev"], 2)
            pe.wait_ge(S["pool_bd"], 6)
            for g in range(BG):
                last = mm(ps[2][64 * g:64 * g + 64, 0:N], gate_bd, lnC[:, g * N:g * N + N], start=True, stop=True)
            last.then_inc(S["lg_mm"], 1)
            pe.wait_ge(S["topk"], 1)
            for t in range(PT):
                last = tr(ps[3][:, t * P:t * P + P], probs[:, t * P:t * P + P], ident)
            last.then_inc(S["mT_mm"], 1)
            pe.wait_ge(S["mT_ev"], 1)
            for b in range(B):
                for t in range(PT):
                    j = t * B + b
                    last = mm(ps[4][0:C, 16 * b:16 * b + 16], t0[:, j * C:j * C + C], mT[:, t, 16 * b:16 * b + 16],
                              start=(t == 0), stop=(t == PT - 1))
            last.then_inc(S["pl_mm"], 1)
            pe.wait_ge(S["pl_ev"], 1)
            pe.wait_ge(S["late_in"], LATE)
            pe.wait_ge(S["pool_zero"], 5)
            pool_e = pooled.rearrange("d (b e) -> d e b", b=B)
            for e in range(EXP):
                last = mm(ps[5][:, B * e:B * e + B], w1b[:, HID * e:HID * e + HID], pool_e[:, e, :],
                          start=True, stop=True)
            last.then_inc(S["hid_mm"], 1)
            pe.wait_ge(S["hid_ev"], 1)
            for e in range(EXP):
                mm(ps[6][0:C, B * e:B * e + B], w2b[:, C * e:C * e + C], hid[:, e, :], start=True, stop=False)
                last = mm(ps[6][0:C, B * e:B * e + B], b2b[:, C * e:C * e + C], ones1, start=False, stop=True)
            last.then_inc(S["eo_mm"], 1)
            pe.wait_ge(S["eo_ev"], 1)
            tr(ps[7][:, 0:C], eo, ident[0:C, 0:C]).then_inc(S["eoT_mm"], 1)
            pe.wait_ge(S["eo_bd"], 1)
            for t in range(PT):
                last = mm(ps[0][:, t * N:t * N + N], probs[:, t * P:t * P + P], eo_bd, start=True, stop=True)
            last.then_inc(S["moe_mm"], 1)

            pe.wait_ge(S["ct_in"], 3)
            to_C(ZT_, 1, S["ct_mm"])
            VT = w32_("v").rearrange("p (l n) -> p l n", l=LAYERS)
            pe.sem_inc(S["la_r"], 1)
            with pe.Fori(0, LAYERS) as l:
                pe.wait_ge(S["la_z"], l * 2 + 2)
                for g in range(BG):
                    for t in range(PT):
                        c0 = (t * B + g * BI) * C
                        last = mm(ps[2][:, g * P:g * P + P], ZT_[:, c0:c0 + P], ZT_[:, c0:c0 + P],
                                  start=(t == 0), stop=(t == PT - 1))
                last.then_inc(S["la_g"], 1)
                pe.wait_ge(S["la_gev"], l + 1)
                for g in range(BG):
                    last = mm(ps[3][:, g * N:g * N + N], g_bd[:, g * P:g * P + P],
                              VT[:, bass.ds(l, 1), :], start=True, stop=True)
                last.then_inc(S["la_h"], 1)
                pe.wait_ge(S["la_hev"], l + 1)
                pe.wait_ge(S["la_qbd"], l + 1)
                for j in range(LHEADS):
                    last = mm(ps[4][:, 0:BG * C], q_bd[:, j, :, :], hs[:, :, j, :],
                              start=(j == 0), stop=(j == LHEADS - 1))
                last.then_inc(S["la_r"], 1)
                pe.wait_ge(S["la_rev"], l + 1)
                for g in range(BG):
                    mm(ps[5][:, g * N:g * N + N], r_bd[:, g * P:g * P + P], ZC[:, g * N:g * N + N],
                       start=True, stop=True)
                for g in range(BG):
                    for t in range(PT):
                        c0 = (t * B + g * BI) * C
                        last = mm(ps[6][:, c0:c0 + P], ZC[:, g * N + t * P:g * N + t * P + P],
                                  r_bd[:, g * P:g * P + P], start=True, stop=True)
                last.then_inc(S["la_zmm"], 1)

            pe.wait_ge(S["ct_in"], 4)
            to_C(T, 0, S["ct_mm"])
            to_C(ln_b, 1, S["ct_mm"])
            pe.wait_ge(S["h_new"], 1)
            tr(ps[0][0:1, 0:C], hC[0:C, 0:1], ident[0:C, 0:C]).then_inc(S["op_mm"], 1)
            pe.wait_ge(S["op_ev"], 1)

            def step(n, k):
                pe.sem_inc(S["op_read"], 1)
                fl = pe.snap(k % 4)
                ffn = pe.snap(k % 2)
                with pe.If(fl >= 2):
                    wq, wk, wv, wo = (w_bd[:, P * i:P * i + P] for i in range(4))
                    pe.wait_ge(S["h_new"], n + 1)
                    pe.wait_ge(S["w_bd"], n + 1)
                    mm(ps[7], wq, hC, start=True, stop=True).then_inc(S["rq_mm"], 1)
                    mm(ps[6], wk, hC, start=True, stop=True).then_inc(S["rq_mm"], 1)
                    for g in range(BG):
                        for t in range(PT):
                            last = mm(ps[5][:, (g * PT + t) * P:(g * PT + t + 1) * P],
                                      hC[:, g * N + t * P:g * N + t * P + P], wv, start=True, stop=True)
                    last.then_inc(S["rv_mm"], 1)
                    pe.wait_ge(S["rk_ev"], n + 1)
                    for b in range(B + LAG):
                        if b < B:
                            g, bi = divmod(b, BI)
                            if b < BI:
                                pe.wait_ge(S["rq_ev"], n * BI + b + 1)
                            elif b == 5:
                                pe.wait_ge(S["rv_ev"], n + 1)
                            for t in range(PT):
                                last = mm(ps[b][:, t * N:t * N + N], rq_bd[:, bi, g * N + t * P:g * N + t * P + P],
                                          rk[:, g * N:g * N + N], start=True, stop=True)
                            last.then_inc(S["sc_mm"], 1)
                        if b >= LAG:
                            a = b - LAG
                            pe.wait_ge(S["sc_norm"], n * B + a + 1)
                            for t in range(PT):
                                for u in range(PT):
                                    last = tr(ps[a][:, (u * PT + t) * P:(u * PT + t + 1) * P],
                                              pr[:, a * 512 + t * N + u * P:a * 512 + t * N + u * P + P], ident)
                            last.then_inc(S["pT_mm"], 1)
                    for g in range(BG):
                        pe.wait_ge(S["pT_ev"], n * B + (g + 1) * BI)
                        for u in range(PT):
                            for bi in range(BI):
                                last = mm(ps[g][32 * bi:32 * bi + 32, 0:N],
                                          rv[:, (g * PT + u) * P + 32 * bi:(g * PT + u) * P + 32 * bi + 32],
                                          prT[:, (g * BI + bi) * 512 + u * N:(g * BI + bi) * 512 + u * N + N],
                                          start=(u == 0), stop=(u == PT - 1), skip_group_check=True)
                    last.then_inc(S["ro_mm"], 1)
                    pe.wait_ge(S["ro_ev"], n + 1)
                    mm(ps[2], wo, roC, start=True, stop=True).then_inc(S["ry_mm"], 1)
                with pe.Else():
                    pe.sem_inc(S["rq_mm"], 2)
                    pe.sem_inc(S["rv_mm"], 1)
                    pe.sem_inc(S["sc_mm"], B)
                    pe.sem_inc(S["pT_mm"], B)
                    pe.sem_inc(S["ro_mm"], 1)
                    pe.sem_inc(S["ry_mm"], 1)
                with pe.If(ffn != 0):
                    pe.wait_ge(S["w1_bd"], n + 1)
                    pe.wait_ge(S["h_new"], n + 1)
                    pe.wait_ge(S["rt_h"], n + 1)
                    mm(ps[0][:, 0:1], w1_bd[:, 0:HID], hC[:, 0:1], start=True, stop=True).then_inc(S["tok_mm"], 1)
                    for bi in range(BI):
                        mm(ps[4 + bi], w1_bd[:, HID * bi:HID * bi + HID], hC, start=True, stop=True
                           ).then_inc(S["f1_mm"], 1)
                        if bi == 0:
                            pe.wait_ge(S["tok_ev"], n + 1)
                            mm(ps[0][0:1, 0:C], f1t, w2c[:, 0:C], start=True, stop=False)
                            mm(ps[0][0:1, 0:C], b2c[0:C, :], ident[0:C, 0:C], start=False, stop=True
                               ).then_inc(S["op_mm"], 1)
                    for bi in range(BI):
                        pe.wait_ge(S["f1_ev"], n * BI + bi + 1)
                        last = mm(ps[1][32 * bi:32 * bi + 32, :], w2c[:, 0:C], f1[:, 512 * bi:512 * bi + 512],
                                  start=True, stop=True)
                    last.then_inc(S["f2mm"], 1)
                with pe.Else():
                    pe.sem_inc(S["f1_mm"], BI)
                    pe.sem_inc(S["f2mm"], 1)
                    pe.sem_inc(S["tok_mm"], 1)
                    pe.wait_ge(S["rt_h"], n + 1)
                    settled(pe)
                    tr(ps[0][0:1, 0:C], hC[0:C, 0:1], ident[0:C, 0:C]).then_inc(S["op_mm"], 1)
                pe.wait_ge(S["op_ev"], n + 2)
                settled(pe)

            routed(pe, step)

        @block.scalar
        def _(act):
            own = Own(act, S["act_own"])
            af = nc.scalar.activation

            def ln_std(n):
                act.wait_ge(S["ln_var"], n)
                af(small[:, 64:80], small[:, 48:64], ACT.Sqrt).then_inc(S["ln_std"], 1)

            def evac_C(bank, dst, n):
                act.wait_ge(S["ct_mm"], n)
                af(dst, ps[bank], ACT.Copy).then_inc(S["ct_ev"], 1)

            act.wait_ge(S["gn_var"], 1)
            af(small[:, 4:6], small[:, 2:4], ACT.Sqrt).then_inc(S["gn_std"], 1)
            act.wait_ge(S["bn_var"], 1)
            af(small[:, 10:12], small[:, 8:10], ACT.Sqrt).then_inc(S["bn_std"], 1)
            for t in range(PT):
                act.wait_ge(S["diff"], t + 1)
                v = hat[:, t].rearrange("p b k a q -> p (b k a q)")
                own.link(af(v, v, ACT.Abs))
                af(v, v, ACT.Relu, bias=1.0, scale=-1.0).then_inc(S["hat"], 1)
            for r in range(BG * PT):
                act.wait_ge(S["g_mm"], r + 1)
                for bi in range(BI):
                    af(GS[:, r // PT, r % PT, bi].rearrange("p k o -> p (k o)"), ps[4 + bi][:, 0:KK * C],
                       ACT.Copy).then_inc(S["g_ev"], 1)
            act.sem_inc(S["s_ev"], BI)
            with act.Fori(0, KK) as k:
                for c in range(B):
                    act.wait_ge(S["tr"], k * B + B + c + 1)
                    act.wait_ge(S["dcn_mm"], k * BG + c // BI + 1)
                    af(SQ[:, c].rearrange("p q n -> p (q n)"), ps[c % BI], ACT.Copy).then_inc(S["s_ev"], 1)
            act.wait_ge(S["bn_ready"], 1)
            for g in range(BG):
                act.wait_ge(S["conv_mm"], g + 1)
                hh = slice(64 * g, 64 * g + 64)
                af(feat[hh, :], ps[g][hh, 0:N], ACT.Gelu, bias=small[hh, 13:14], scale=small[hh, 12:13]
                   ).then_inc(S["feat"], 1)
            act.wait_ge(S["featT_mm"], 1)
            af(featT.rearrange("p t n -> p (t n)"), ps[2][:, 0:PT * P], ACT.Copy).then_inc(S["featT_ev"], 1)
            act.wait_ge(S["f2_mm"], 1)
            af(F2, ps[3], ACT.Copy).then_inc(S["f2_ev"], 1)
            act.wait_ge(S["cg_mm"], 1)
            own.link(af(cg, ps[6][:, 0:N], ACT.Gelu, bias=small[:, 15:16], scale=small[:, 14:15]))
            af(cg, cg, ACT.Sigmoid, bias=par_("cg2_b"), scale=par_("cg2_w")).then_inc(S["cg_act"], 1)
            act.wait_ge(S["l2_sum"], 1)
            af(small[:, 18:20], small[:, 16:18], ACT.Sqrt).then_inc(S["l2_std"], 1)
            act.wait_ge(S["sm2_in"], 1)
            af(small[:, 28:32], small[:, 28:32], ACT.Exp).then_inc(S["sm2_exp"], 1)
            act.wait_ge(S["gT_mm"], 1)
            af(gT.rearrange("p a t n -> p (a t n)"), ps[7], ACT.Copy).then_inc(S["gT_ev"], 1)
            act.wait_ge(S["mix"], 1)
            af(outf, outf, ACT.Sqrt).then_inc(S["mix_abs"], 1)
            act.wait_ge(S["inv_mm"], 1)
            af(gated, ps[2], ACT.Square).then_inc(S["inv_sq"], 1)
            act.wait_ge(S["inv_add"], 1)
            af(gatef, gatef, ACT.Sqrt, scale=1.0 / (N * N)).then_inc(S["inv_abs"], 1)

            ln_std(1)
            ln_std(2)
            evac_C(0, lnC, 1)
            for bi in range(BI):
                act.wait_ge(S["qk_mm"], bi + 1)
                af(qT[:, 512 * bi:512 * bi + 512], ps[bi], ACT.Copy, scale=DH ** -0.5).then_inc(S["q_ev"], 1)
            for bi in range(BI):
                act.wait_ge(S["v_mm"], bi + 1)
                af(V[:, 512 * bi:512 * bi + 512], ps[4 + bi], ACT.Copy).then_inc(S["v_ev"], 1)
            for bi in range(BI):
                act.wait_ge(S["a3_max"], bi + 1)
                for g in range(BG):
                    b = 2 * bi + g
                    last = af(a3[:, N * b:N * b + N], ps[4 + bi][:, g * N:g * N + N], ACT.Exp,
                              bias=small[:, 80 + b:81 + b], accum_out=small[:, 88 + b:89 + b])
                last.then_inc(S["a3_exp"], 1)
            act.wait_ge(S["a2_sub"], 1)
            af(XM, XM, ACT.Exp).then_inc(S["a2_exp"], 1)
            for bi in range(BI):
                act.wait_ge(S["a1_sub"], bi + 1)
                v = a1[:, 512 * bi:512 * bi + 512]
                af(v, v, ACT.Exp).then_inc(S["a1_exp"], 1)
            rr4 = res.rearrange("p (t b h e) -> p t h b e", t=PT, b=B, h=HEADS)
            for n in range(4):
                act.wait_ge(S["res_mm"], n + 1)
                af(rr4[:, n // 2, 4 * (n % 2):4 * (n % 2) + 4],
                   ps[n].rearrange("p (h b e) -> p h b e", h=4, b=B), ACT.Copy).then_inc(S["res_ev"], 1)
            for bi in range(BI):
                act.wait_ge(S["a1T_mm"], bi + 1)
                af(a1T[:, 512 * bi:512 * bi + 512], ps[4 + bi], ACT.Copy).then_inc(S["a1T_ev"], 1)
            act.wait_ge(S["z_new"], 2)
            with act.Fori(0, PINV) as it:
                for n, (bank, dst) in enumerate(((0, pX), (1, pY), (0, pX), (0, pX), (0, pX), (1, pY))):
                    act.wait_ge(S["xz_mm"], it * 6 + n + 1)
                    af(dst, ps[bank][:, 0:2 * P], ACT.Copy).then_inc(S["x_ev"], 1)
            for bi in range(2):
                act.wait_ge(S["oT_mm"], bi + 1)
                af(oT[:, 512 * bi:512 * bi + 512], ps[4 + bi], ACT.Copy).then_inc(S["oT_evA"], 1)

            ln_std(3)
            evac_C(1, lnC, 2)
            act.wait_ge(S["lg_max"], 1)
            af(probs, probs, ACT.Exp, bias=small[:, 105:106], accum_out=small[:, 106:107]).then_inc(S["lg_exp"], 1)
            act.wait_ge(S["hid_mm"], 1)
            af(hid.rearrange("p e b -> p (e b)"), ps[5][:, 0:P], ACT.Gelu).then_inc(S["hid_ev"], 1)

            ln_std(4)
            act.wait_ge(S["ct_mm"], 3)
            af(ZC, ps[1], ACT.Copy).then_inc(S["la_z"], 1)
            with act.Fori(0, LAYERS) as l:
                act.wait_ge(S["la_h"], l + 1)
                af(hs.rearrange("p g j o -> p (g j o)"), ps[3], ACT.Copy).then_inc(S["la_hev"], 1)
            ln_std(5)
            evac_C(0, tC, 4)
            act.wait_ge(S["ct_mm"], 5)
            af(hC, ps[1], ACT.Copy).then_inc(S["h_new"], 1)

            act.wait_ge(S["op_ev"], 1)

            def step(n, k):
                act.sem_inc(S["op_read"], 1)
                fl = act.snap(k % 4)
                ffn = act.snap(k % 2)
                with act.If(fl >= 2):
                    act.wait_ge(S["rq_mm"], n * 2 + 2)
                    af(rk, ps[6], ACT.Copy).then_inc(S["rk_ev"], 1)
                    act.wait_ge(S["rv_mm"], n + 1)
                    af(rv, ps[5], ACT.Copy).then_inc(S["rv_ev"], 1)
                    for b in range(B + LAG):
                        if b < B:
                            act.wait_ge(S["sc_max"], n * B + b + 1)
                            for t in range(PT):
                                last = af(pr[:, b * 512 + t * N:b * 512 + t * N + N], ps[b][:, t * N:t * N + N],
                                          ACT.Exp, bias=rmax[:, 2 * b + t:2 * b + t + 1],
                                          accum_out=rsum[:, 2 * b + t:2 * b + t + 1])
                            last.then_inc(S["sc_exp"], 1)
                        if b >= LAG:
                            a = b - LAG
                            act.wait_ge(S["pT_mm"], n * B + a + 1)
                            af(prT[:, a * 512:a * 512 + 512], ps[a], ACT.Copy).then_inc(S["pT_ev"], 1)
                with act.Else():
                    act.sem_inc(S["rk_ev"], 1)
                    act.sem_inc(S["rv_ev"], 1)
                    act.sem_inc(S["sc_exp"], B)
                    act.sem_inc(S["pT_ev"], B)
                with act.If(ffn != 0):
                    act.wait_ge(S["w1_bd"], n + 1)
                    for bi in range(BI):
                        act.wait_ge(S["f1_mm"], n * BI + bi + 1)
                        af(f1[:, 512 * bi:512 * bi + 512], ps[4 + bi], ACT.Relu, bias=w2c[:, C:C + 1]
                           ).then_inc(S["f1_ev"], 1)
                with act.Else():
                    act.sem_inc(S["f1_ev"], BI)
                act.wait_ge(S["op_ev"], n + 2)
                settled(act)

            routed(act, step)

        @block.vector
        def _(dve):
            own = Own(dve, S["dve_own"])
            link = own.link
            v_ = nc.vector
            tt_, ts_, stt = v_.tensor_tensor, v_.tensor_scalar, v_.scalar_tensor_tensor

            def layernorm(src, dst, eps, n):
                s3, d3, c3 = arr3(src, C), arr3(dst, C), arr3(ln_a, C)
                bc = lambda a: a.unsqueeze(2).to_broadcast([P, 16, C])
                mean, var, std = small[:, 32:48], small[:, 48:64], small[:, 64:80]
                link(v_.tensor_reduce(mean, s3, AX.X, ALU.add))
                link(ts_(mean, mean, 1.0 / C, None, ALU.mult))
                link(tt_(c3, s3, bc(mean), ALU.subtract))
                link(tt_(d3, c3, c3, ALU.mult))
                link(v_.tensor_reduce(var, d3, AX.X, ALU.add))
                ts_(var, var, 1.0 / C, eps, ALU.mult, ALU.add).then_inc(S["ln_var"], 1)
                dve.wait_ge(S["ln_std"], n)
                link(v_.reciprocal(std, std))
                return tt_(d3, c3, bc(std), ALU.mult)

            dve.wait_ge(S["x_in"], 16)
            stats = scr[:, 0:12].rearrange("p (g s) -> p g s", g=BG)
            mv = scr[:, 16:20].rearrange("p (g s) -> p g s", g=BG)
            for g in range(BG):
                link(v_.bn_stats(stats[:, g, :], xC[:, g * N:g * N + N]))
            for g in range(BG):
                link(v_.bn_aggr(mv[:, g, :], stats[:, g, :]))
            ts_(small[:, 2:4], mv[:, :, 1], 1e-5, None, ALU.add).then_inc(S["gn_var"], 1)
            dve.wait_ge(S["gn_std"], 1)
            link(v_.reciprocal(small[:, 4:6], small[:, 4:6]))
            dve.wait_ge(S["pool_zero"], 1)
            for g in range(BG):
                src = xC[:, g * N:g * N + N]
                ts_(xnp[:, g, 1:17, 1:17], src.rearrange("p (y x) -> p y x", y=HH), mv[:, g, 0:1],
                    small[:, 4 + g:5 + g], ALU.subtract, ALU.mult).then_inc(S["xn"], 1)
                ts_(xn[:, g * N:g * N + N], src, mv[:, g, 0:1], small[:, 4 + g:5 + g], ALU.subtract, ALU.mult
                    ).then_inc(S["xn"], 1)
            dve.wait_ge(S["par_in"], SMALL)
            link(ts_(small[:, 8:9], par_("bn_v"), 1e-5, None, ALU.add))
            ts_(small[:, 9:10], par_("cgbn_v"), 1e-5, None, ALU.add).then_inc(S["bn_var"], 1)
            for g in range(BG):
                dve.wait_ge(S["off_mm"], g + 1)
                v_.tensor_copy(offC[0:BI * NOFF, g * N:g * N + N], ps[g][0:BI * NOFF, 0:N]
                               ).then_inc(S["off_ev"], 1)
            dve.wait_ge(S["off_mm"], BG + 1)
            dve.wait_ge(S["pool_bd"], 3)
            link(tt_(yx, ps[2][:, 0:288].rearrange("p (t b o) -> p t b o", t=PT, b=B),
                     base2.unsqueeze(2).to_broadcast([P, PT, B, NOFF]), ALU.add))
            for t in range(PT):
                tt_(hat[:, t].rearrange("p b k a q -> p (b k a) q"),
                    yx[:, t].rearrange("p b o -> p (b o)").unsqueeze(2).to_broadcast([P, B * NOFF, 16]),
                    iota.unsqueeze(1).to_broadcast([P, B * NOFF, 16]), ALU.subtract).then_inc(S["diff"], 1)
            dve.wait_ge(S["bn_std"], 1)
            link(v_.reciprocal(small[:, 10:12], small[:, 10:12]))
            link(tt_(small[:, 12:13], par_("bn_g"), small[:, 10:11], ALU.mult))
            link(tt_(small[:, 14:15], par_("cgbn_g"), small[:, 11:12], ALU.mult))
            link(tt_(small[:, 6:7], par_("bn_m"), small[:, 12:13], ALU.mult))
            link(tt_(small[:, 13:14], par_("bn_b"), small[:, 6:7], ALU.subtract))
            link(tt_(small[:, 7:8], par_("cg1_b"), par_("cgbn_m"), ALU.subtract))
            link(tt_(small[:, 7:8], small[:, 7:8], small[:, 14:15], ALU.mult))
            tt_(small[:, 15:16], small[:, 7:8], par_("cgbn_b"), ALU.add).then_inc(S["bn_ready"], 1)
            dve.wait_ge(S["hat"], PT)
            with dve.Fori(0, KK) as k:
                for c in range(B):
                    dve.wait_ge(S["tr"], k * B + c + 1)
                    hy = hat[:, :, c, bass.ds(k, 1), 0, :].rearrange("p t k q -> p t (k q)")
                    hx = hat[:, :, c, bass.ds(k, 1), 1, :].rearrange("p t k q -> p t (k q)")
                    tt_(ST[:, c], hy.unsqueeze(3).to_broadcast([P, PT, 16, 16]),
                        hx.unsqueeze(2).to_broadcast([P, PT, 16, 16]), ALU.mult).then_inc(S["prod"], 1)
            dve.wait_ge(S["dcn_mm"], (KK + 2) * BG)
            for g in range(BG):
                link(tt_(x1C[:, g * N:g * N + N], xC[:, g * N:g * N + N], ps[4 + g][:, 0:N], ALU.add))
                dve.wait_ge(S["pool_zero"], 3)
                v_.tensor_copy(xp[:, g, 3:19, 3:19], x1C[:, g * N:g * N + N].rearrange("p (y x) -> p y x", y=HH)
                               ).then_inc(S["x1_ready"], 1)

            Fp, fp = ps[4], ps[5][:, 0:N]
            dve.wait_ge(S["swap_mm"], 2)
            sm = small
            link(v_.tensor_tensor_reduce(scr, F2, F2, 1.0, 0.0, ALU.mult, ALU.add, sm[:, 16:17]))
            link(v_.tensor_copy(mixed, Fp))
            link(v_.tensor_tensor_reduce(scr, mixed, mixed, 1.0, 0.0, ALU.mult, ALU.add, sm[:, 17:18]))
            link(ts_(sm[:, 20:21], sm[:, 16:17], 1.0, None, ALU.mult))
            link(v_.tensor_tensor_reduce(scr, F2, mixed, 1.0, 0.0, ALU.mult, ALU.add, sm[:, 21:22]))
            link(v_.tensor_tensor_reduce(scr[:, 0:N], F2[:, N:2 * N], mixed[:, 0:N], 1.0, 0.0, ALU.mult, ALU.add,
                                         sm[:, 22:23]))
            link(v_.tensor_tensor_reduce(scr[:, 0:N], F2[:, 0:N], mixed[:, N:2 * N], 1.0, 0.0, ALU.mult, ALU.add,
                                         sm[:, 23:24]))
            link(tt_(sm[:, 23:24], sm[:, 22:23], sm[:, 23:24], ALU.subtract))
            link(v_.memset(sm[:, 22:23], 0.0))
            ts_(sm[:, 16:18], sm[:, 16:18], 1e-6, None, ALU.add).then_inc(S["l2_sum"], 1)
            dve.wait_ge(S["l2_std"], 1)
            link(v_.reciprocal(sm[:, 18:20], sm[:, 18:20]))
            link(ts_(sm[:, 24:28], sm[:, 20:24], sm[:, 18:19], par_("tau"), ALU.mult, ALU.mult))
            pairs = sm[:, 24:28].rearrange("p (r s) -> p r s", r=2)
            link(tt_(pairs, pairs, sm[:, 18:20].unsqueeze(1).to_broadcast([P, 2, 2]), ALU.mult))
            link(v_.tensor_reduce(sm[:, 20:22], pairs, AX.X, ALU.max))
            ex = sm[:, 28:32].rearrange("p (r s) -> p r s", r=2)
            tt_(ex, pairs, sm[:, 20:22].unsqueeze(2).to_broadcast([P, 2, 2]), ALU.subtract).then_inc(S["sm2_in"], 1)
            dve.wait_ge(S["cg_act"], 1)
            for a in range(2):
                tt_(gated[:, a * N:a * N + N], F2[:, a * N:a * N + N], cg, ALU.mult).then_inc(S["gated"], 1)
            dve.wait_ge(S["sm2_exp"], 1)
            link(v_.tensor_reduce(sm[:, 20:22], ex, AX.X, ALU.add))
            link(v_.reciprocal(sm[:, 20:22], sm[:, 20:22]))
            link(tt_(ex, ex, sm[:, 20:22].unsqueeze(2).to_broadcast([P, 2, 2]), ALU.mult))
            for a in range(2):
                m = mixed[:, a * N:a * N + N]
                link(ts_(m, fp, sm[:, 29 + 2 * a:30 + 2 * a], None, ALU.mult))
                link(stt(m, feat, sm[:, 28 + 2 * a:29 + 2 * a], m, ALU.mult, ALU.add))
            link(tt_(mixed, mixed, mixed, ALU.mult))
            tt_(outf, mixed[:, 0:N], mixed[:, N:2 * N], ALU.add).then_inc(S["mix"], 1)
            dve.wait_ge(S["inv_sq"], 1)
            tt_(gatef, gated[:, 0:N], gated[:, N:2 * N], ALU.add).then_inc(S["inv_add"], 1)
            dve.wait_ge(S["toT_mm"], 2)
            link(v_.tensor_copy(T, ps[0]))
            for n in range(2):
                dst = T4[:, :, :, n * CH:n * CH + CH]
                link(tt_(dst, dst, ps[1][:, n * N:n * N + N].rearrange("p (t b c) -> p t b c", t=PT, b=B), ALU.add))

            link(layernorm(T, t0, 1e-5, 1))
            link(layernorm(t0, ln_b, 1e-5, 2))
            bcrow = lambda n: row_(n).unsqueeze(1).to_broadcast([P, 16, C])
            dve.wait_ge(S["par_in"], SMALL)
            link(tt_(arr3(ln_b, C), arr3(ln_b, C), bcrow("ln_w"), ALU.mult))
            tt_(arr3(ln_b, C), arr3(ln_b, C), bcrow("ln_b"), ALU.add).then_inc(S["ct_in"], 1)
            dve.wait_ge(S["ct_ev"], 1)
            link(v_.tensor_reduce(xpool, arr3(lnC, 16), AX.X, ALU.add))
            ts_(xpool, xpool, 1.0 / LM, None, ALU.mult).then_inc(S["pool_in"], 1)
            for bi in range(BI):
                dve.wait_ge(S["qk_mm"], BI + bi + 1)
                v_.tensor_copy(kT[:, 512 * bi:512 * bi + 512], ps[4 + bi]).then_inc(S["k_ev"], 1)
            for bi in range(BI):
                dve.wait_ge(S["lk_mm"], bi + 1)
                link(ts_(ql[:, 2 * bi:2 * bi + 2, :], ps[bi][:, 0:32].rearrange("p (b m) -> p b m", b=2),
                         DH ** -0.5, None, ALU.mult))
                link(v_.tensor_copy(kl[:, 2 * bi:2 * bi + 2, :],
                                    ps[bi][:, 32:64].rearrange("p (b m) -> p b m", b=2)))
            v_.tensor_copy(small[:, 200:201], small[:, 4:5]).then_inc(S["lk_ev"], 1)
            tt_(kl_bd, expand16(kl), mask8_for(B), ALU.mult).then_inc(S["kl_bd"], 1)
            dve.wait_ge(S["sim2_mm"], 1)
            s2 = ps[0][:, 0:P].rearrange("p (b m) -> p b m", b=B)
            mx, sm8 = small[:, 108:116], small[:, 116:124]
            bc8 = lambda a: a.unsqueeze(2).to_broadcast([P, B, LM])
            link(v_.tensor_reduce(mx, s2, AX.X, ALU.max))
            tt_(XM, s2, bc8(mx), ALU.subtract).then_inc(S["a2_sub"], 1)
            for bi in range(BI):
                dve.wait_ge(S["sim3_mm"], bi + 1)
                v_.tensor_reduce(small[:, 80 + 2 * bi:82 + 2 * bi], arr3(ps[4 + bi], N), AX.X, ALU.max,
                                 negate=True).then_inc(S["a3_max"], 1)
            dve.wait_ge(S["a2_exp"], 1)
            link(v_.tensor_reduce(sm8, XM, AX.X, ALU.add))
            link(v_.reciprocal(sm8, sm8))
            link(tt_(XM, XM, bc8(sm8), ALU.mult))
            tt_(bdz, expand16(XM), mask8_for(B), ALU.mult).then_inc(S["x_bd"], 1)
            for bi in range(BI):
                dve.wait_ge(S["a3T_mm"], bi + 1)
                v_.tensor_copy(a3T[:, 512 * bi:512 * bi + 512], ps[4 + bi]).then_inc(S["a3T_ev"], 1)
            dve.wait_ge(S["w3_mm"], 1)
            link(v_.reciprocal(small[:, 96:104], small[:, 88:96]))
            mr = small[:, 128:192].rearrange("p (b h) -> p b h", b=B)
            link(tt_(mr, mask8.unsqueeze(1).to_broadcast([P, B, HEADS]),
                     small[:, 96:104].unsqueeze(2).to_broadcast([P, B, HEADS]), ALU.mult))
            for n in range(2):
                ins = tt_(w3_bd[:, 4 * n:4 * n + 4], ps[2 + n].rearrange("p (b h e) -> p b h e", b=4, h=HEADS),
                          mr[:, 4 * n:4 * n + 4].unsqueeze(3).to_broadcast([P, 4, HEADS, DH]), ALU.mult)
                if n:
                    ins.then_inc(S["w3_ev"], 1)
                else:
                    link(ins)
            mx1 = small[:, 384:512]
            for bi in range(BI):
                dve.wait_ge(S["sim1_mm"], bi + 1)
                m = mx1[:, 32 * bi:32 * bi + 32]
                link(v_.tensor_reduce(m, arr3(ps[4 + bi], 16), AX.X, ALU.max))
                tt_(arr3(a1[:, 512 * bi:512 * bi + 512], 16), arr3(ps[4 + bi], 16),
                    m.unsqueeze(2).to_broadcast([P, 32, 16]), ALU.subtract).then_inc(S["a1_sub"], 1)
            for bi in range(BI):
                dve.wait_ge(S["a1_exp"], bi + 1)
                r = small[:, 256 + 32 * bi:288 + 32 * bi]
                link(v_.tensor_reduce(r, arr3(a1[:, 512 * bi:512 * bi + 512], 16), AX.X, ALU.add))
                v_.reciprocal(r, r).then_inc(S["a1_sum"], 1)
            dve.wait_ge(S["xT_mm"], 1)
            for n in range(2):
                link(v_.tensor_copy(bdXT[:, 4 * n:4 * n + 4],
                                    ps[n].rearrange("p (b h e) -> p b h e", b=4, h=HEADS)))
            link(v_.tensor_reduce(XT, bdXT.rearrange("p b h m -> p b m h"), AX.X, ALU.add))
            link(v_.tensor_reduce(mx, XM, AX.X, ALU.add, apply_absolute_value=True))
            link(v_.tensor_reduce(sm8, XT, AX.X, ALU.add, apply_absolute_value=True))
            v_.tensor_reduce(small[:, 16:18], small[:, 108:124].rearrange("p (a b) -> p a b", a=2), AX.X, ALU.max
                             ).then_inc(S["cr_in"], 1)
            dve.wait_ge(S["cr_max"], 1)
            link(tt_(small[:, 34:35], small[:, 32:33], small[:, 33:34], ALU.mult))
            link(v_.reciprocal(small[:, 34:35], small[:, 34:35]))
            ebc = lambda e: e.unsqueeze(1).to_broadcast([P, B, 16])
            pb = [ps[i][:, 0:2 * P].rearrange("p (b m) -> p b m", b=B)[:, :, 0:LM] for i in range(4)]
            link(v_.memset(ps[0][:, 0:2 * P], 0.0))
            link(v_.memset(ps[1][:, 0:2 * P], 0.0))
            ts_(z, XT, small[:, 34:35], None, ALU.mult).then_inc(S["z_new"], 1)
            ts_(zT, XM, small[:, 34:35], None, ALU.mult).then_inc(S["z_new"], 1)
            dve.wait_ge(S["z_new"], 2)
            tt_(bdz, expand16(z), mask8_for(B), ALU.mult).then_inc(S["t_ready"], 1)
            own.restart()
            with dve.Fori(0, PINV) as it:
                dve.wait_ge(S["t_mm"], it * 6 + 1)
                link(stt(tt, pb[2], -1.0, ebc(eye7), ALU.mult, ALU.add))
                dve.wait_ge(S["t_mm"], it * 6 + 2)
                tt_(bdxzT, expand16(pb[3]), mask8_for(B), ALU.mult).then_inc(S["t_ready"], 1)
                dve.wait_ge(S["t_mm"], it * 6 + 3)
                stt(tt, pb[2], -1.0, ebc(eye15), ALU.mult, ALU.add).then_inc(S["t_ready"], 1)
                dve.wait_ge(S["t_mm"], it * 6 + 4)
                stt(tt, pb[2], -0.25, ebc(eye13), ALU.mult, ALU.add).then_inc(S["tt_new"], 1)
                dve.wait_ge(S["tt_new"], it + 1)
                tt_(bdt, expand16(tt), mask8_for(B), ALU.mult).then_inc(S["t_ready"], 1)
                dve.wait_ge(S["t_mm"], it * 6 + 5)
                v_.tensor_copy(z, pb[2]).then_inc(S["z_new"], 1)
                dve.wait_ge(S["t_mm"], it * 6 + 6)
                v_.tensor_copy(zT, pb[3]).then_inc(S["z_new"], 1)
                dve.wait_ge(S["z_new"], it * 2 + 4)
                tt_(bdz, expand16(z), mask8_for(B), ALU.mult).then_inc(S["t_ready"], 1)
                dve.wait_ge(S["t_ready"], it * 4 + 5)
                settled(dve)
                own.restart()
            link(v_.tensor_copy(small[:, 200:201], small[:, 4:5]))
            tt_(bdz, expand16(zT), mask8_for(B), ALU.mult).then_inc(S["t_ready"], 1)
            dve.wait_ge(S["w2_mm"], 1)
            link(v_.tensor_copy(w2_bd[:, 0:4], ps[2].rearrange("p (b h e) -> p b h e", b=4, h=HEADS)))
            v_.tensor_copy(w2_bd[:, 4:8], ps[3].rearrange("p (b h e) -> p b h e", b=4, h=HEADS)
                           ).then_inc(S["w2_ev"], 1)
            for bi in range(2, 4):
                dve.wait_ge(S["oT_mm"], bi + 1)
                v_.tensor_copy(oT[:, 512 * bi:512 * bi + 512], ps[4 + bi]).then_inc(S["oT_evD"], 1)
            link(tt_(T, T, t0, ALU.add))
            link(tt_(arr3(T, C), arr3(T, C), bcrow("b_out"), ALU.add))
            dve.wait_ge(S["ao_mm"], 1)
            link(tt_(T, T, ps[0], ALU.add))

            layernorm(T, t0, 1e-5, 3).then_inc(S["ct_in"], 1)
            dve.wait_ge(S["lg_mm"], 1)
            link(ts_(probs, ps[2][:, 0:N], par_("gate_b"), None, ALU.add))
            v_.tensor_reduce(small[:, 105:106], probs, AX.X, ALU.max, negate=True).then_inc(S["lg_max"], 1)
            dve.wait_ge(S["lg_exp"], 1)
            link(v_.reciprocal(small[:, 107:108], small[:, 106:107]))
            link(ts_(probs, probs, small[:, 107:108], None, ALU.mult))
            link(v_.max(small[:, 192:200], probs))
            link(v_.match_replace(probs_rest, small[:, 192:200], probs, 0.0))
            tt_(probs, probs, probs_rest, ALU.subtract).then_inc(S["topk"], 1)
            dve.wait_ge(S["mT_mm"], 1)
            v_.tensor_copy(mT.rearrange("p t e -> p (t e)"), ps[3][:, 0:N]).then_inc(S["mT_ev"], 1)
            dve.wait_ge(S["pl_mm"], 1)
            v_.tensor_copy(pooled[0:C, :], ps[4][0:C, 0:P]).then_inc(S["pl_ev"], 1)
            dve.wait_ge(S["eo_mm"], 1)
            v_.tensor_copy(eo.rearrange("o (b e) -> o e b", b=B),
                           ps[6][0:C, 0:P].rearrange("o (e b) -> o e b", e=EXP)).then_inc(S["eo_ev"], 1)
            dve.wait_ge(S["eoT_mm"], 1)
            tt_(eo_bd, ps[7][:, 0:C].unsqueeze(1).to_broadcast([P, B, C]),
                mask8.unsqueeze(2).to_broadcast([P, B, C]), ALU.mult).then_inc(S["eo_bd"], 1)
            dve.wait_ge(S["moe_mm"], 1)
            link(tt_(T, T, ps[0], ALU.add))

            link(layernorm(T, ZT_, 1e-5, 4))
            v_.tensor_copy(small[:, 201:202], small[:, 4:5]).then_inc(S["ct_in"], 1)
            v_.tensor_copy(small[:, 202:203], small[:, 4:5]).then_inc(S["la_z"], 1)
            m4 = mask4.unsqueeze(1).unsqueeze(3)
            dve.wait_ge(S["la_z"], 2)
            own.restart()
            with dve.Fori(0, LAYERS) as l:
                dve.wait_ge(S["la_g"], l + 1)
                tt_(g_bd.rearrange("p (g b o) -> p g b o", g=BG, b=BI),
                    ps[2][:, 0:BG * P].rearrange("p (g b o) -> p g b o", g=BG, b=BI),
                    m4.to_broadcast([P, BG, BI, C]), ALU.mult).then_inc(S["la_gev"], 1)
                dve.wait_ge(S["la_r"], l + 2)
                link(tt_(r_bd.rearrange("p (g b o) -> p g b o", g=BG, b=BI),
                         ps[4][:, 0:BG * C].rearrange("p (g o) -> p g o", g=BG).unsqueeze(2)
                         .to_broadcast([P, BG, BI, C]), m4.to_broadcast([P, BG, BI, C]), ALU.mult))
                ts_(r_bd, r_bd, 1.0 / (N * LHEADS), None, ALU.mult).then_inc(S["la_rev"], 1)
                dve.wait_ge(S["la_zmm"], l + 1)
                tt_(ZC, ZC, ps[5], ALU.add).then_inc(S["la_z"], 1)
                tt_(ZT_, ZT_, ps[6], ALU.add).then_inc(S["la_z"], 1)
                dve.wait_ge(S["la_z"], 2 * l + 4)
                settled(dve)
                own.restart()
            link(tt_(T, T, ZT_, ALU.add))

            link(layernorm(T, ln_b, 1e-5, 5))
            v_.tensor_copy(small[:, 201:202], small[:, 4:5]).then_inc(S["ct_in"], 1)
            link(v_.tensor_copy(stepb, keyb.rearrange("p (s o) -> p s o", o=NOPS)[:, :, 0]))
            link(stt(keyf, maskb, 2.0, flagb, ALU.mult, ALU.add))
            link(tt_(keyb, keyb, keyf, ALU.add))
            link(ts_(keyf, keyf, 0.0, float(NONE), ALU.is_equal, ALU.mult))
            link(tt_(keyb, keyb, keyf, ALU.add))
            link(v_.memset(passed, 0.0))

            def next_op():
                link(v_.max_index(op8, top8, ps[0][0:1, 0:NOPS]))
                op = dve.value_load(op8[0:1, 0:1], min_val=0, max_val=NOPS - 1)
                link(tt_(cand, keyb.rearrange("p (s o) -> p s o", o=NOPS)[:, :, bass.ds(op, 1)]
                         .rearrange("p s o -> p (s o)"), passed, ALU.add))
                link(v_.tensor_reduce(key, cand, AX.X, ALU.min))
                link(v_.tensor_copy(keyi, key))
                own.restart()
                dve.sem_inc(S["op_ev"], 1)

            dve.wait_ge(S["op_mm"], 1)
            link(v_.max(top8, ps[0][0:1, 0:NOPS]))
            next_op()

            def step(n, k):
                fl = dve.snap(k % 4)
                ffn = dve.snap(k % 2)
                dve.wait_ge(S["w_in"], (n + 1) * 32)
                with dve.If(fl >= 2):
                    tt_(w_bd.rearrange("p (w b o) -> p w b o", w=4, b=BI),
                        recA[:, HID:HID + 4 * C].rearrange("p (w o) -> p w o", w=4).unsqueeze(2)
                        .to_broadcast([P, 4, BI, C]), m4.to_broadcast([P, 4, BI, C]), ALU.mult
                        ).then_inc(S["w_bd"], 1)
                with dve.Else():
                    dve.sem_inc(S["w_bd"], 1)
                link(v_.tensor_copy(w2c, recB))
                link(v_.tensor_copy(b2c, recA[:, REC_A - 1:REC_A]))
                tt_(w1_bd.rearrange("p (b h) -> p b h", b=BI),
                    recA[:, 0:HID].unsqueeze(1).to_broadcast([P, BI, HID]),
                    mask4.unsqueeze(2).to_broadcast([P, BI, HID]), ALU.mult).then_inc(S["w1_bd"], 1)
                link(ts_(passed, stepb, key, float(NONE), ALU.is_le, ALU.mult))
                dve.wait_ge(S["w1_bd"], n + 1)
                dve.sem_inc(S["w_used"], 1)
                with dve.If(fl >= 2):
                    dve.wait_ge(S["rq_mm"], 2 * n + 1)
                    for bi in range(BI):
                        ts_(rq_bd[:, bi, :], ps[7], mask4[:, bi:bi + 1], C ** -0.5, ALU.mult, ALU.mult
                            ).then_inc(S["rq_ev"], 1)
                    for b in range(B + 1):
                        if b < B:
                            dve.wait_ge(S["sc_mm"], n * B + b + 1)
                            v_.tensor_reduce(rmax[:, 2 * b:2 * b + 2], arr3(ps[b], N), AX.X, ALU.max,
                                             negate=True).then_inc(S["sc_max"], 1)
                        if b:
                            a = b - 1
                            dve.wait_ge(S["sc_exp"], n * B + a + 1)
                            r = rsum[:, 2 * a:2 * a + 2]
                            link(v_.reciprocal(r, r))
                            pb3 = arr3(pr[:, a * 512:a * 512 + 512], N)
                            tt_(pb3, pb3, r.unsqueeze(2).to_broadcast([P, 2, N]), ALU.mult).then_inc(S["sc_norm"], 1)
                    dve.wait_ge(S["ro_mm"], n + 1)
                    link(v_.tensor_copy(roC[:, 0:N], ps[0][:, 0:N]))
                    v_.tensor_copy(roC[:, N:2 * N], ps[1][:, 0:N]).then_inc(S["ro_ev"], 1)
                    dve.wait_ge(S["ry_mm"], n + 1)
                    v_.tensor_copy(hC, ps[2]).then_inc(S["rt_h"], 1)
                    dve.wait_ge(S["rt_h"], n + 1)
                    settled(dve)
                    own.restart()
                with dve.Else():
                    dve.sem_inc(S["rq_ev"], BI)
                    dve.sem_inc(S["sc_max"], B)
                    dve.sem_inc(S["sc_norm"], B)
                    dve.sem_inc(S["ro_ev"], 1)
                    dve.sem_inc(S["rt_h"], 1)
                    own.restart()
                with dve.If(ffn != 0):
                    dve.wait_ge(S["tok_mm"], n + 1)
                    ts_(f1t, ps[0][:, 0:1], w2c[:, C:C + 1], 0.0, ALU.add, ALU.max).then_inc(S["tok_ev"], 1)
                with dve.Else():
                    dve.sem_inc(S["tok_ev"], 1)
                dve.wait_ge(S["op_mm"], n + 2)
                settled(dve)
                link(v_.max(top8, ps[0][0:1, 0:NOPS]))
                dve.wait_ge(S["op_read"], 3 * n + 3)
                settled(dve)
                next_op()
                with dve.If(ffn != 0):
                    dve.wait_ge(S["f2mm"], n + 1)
                    ts_(hC, ps[1], b2c, None, ALU.add).then_inc(S["h_new"], 1)
                    dve.wait_ge(S["h_new"], n + 2)
                    settled(dve)
                with dve.Else():
                    dve.sem_inc(S["h_new"], 1)

            routed(dve, step)
            dve.wait_ge(S["ct_ev"], 3)
            tt_(outC, tC, hC, ALU.add).then_inc(S["out_ready"], 1)


def constants():
    c = np.zeros((P, CST_COLS), np.float32)
    p = np.arange(P)

    def put(n, a):
        c[:, CST[n][0]:CST[n][1]] = a.reshape(P, -1)

    put("ident", np.eye(P))
    put("flip", np.eye(P)[::-1])
    put("mask4", p[:, None] // 32 == np.arange(4))
    put("mask8", p[:, None] // 16 == np.arange(8))
    put("iota", np.broadcast_to(np.arange(16), (P, 16)))
    put("mask16", p[:, None] // 16 == p[None, :] // 16)
    put("swap", (p[:, None] ^ 1) == p[None, :])
    put("eye", np.stack([s * (p[:, None] % 16 == np.arange(16)) for s in (7.0, 15.0, 3.25)], 1))
    k = np.arange(KK)
    t = np.arange(PT)
    y = t[None, :, None] * 8 + p[:, None, None] // 16 + k // 3 - 1
    xx = p[:, None, None] % 16 + k % 3 - 1 + 0 * t[None, :, None]
    put("base", np.stack([y, xx], -1))
    n = np.arange(N)
    ang = (np.outer(n // 16, n // 16) + np.outer(n % 16, n % 16)) % 16 * (2 * np.pi / 16)
    co, si = np.cos(ang), np.sin(ang)
    d = np.concatenate([co, -si, -co], 1).reshape(PT, P, 3 * N).transpose(1, 0, 2)
    put("dft", d)
    return c


def kernel(x, **w):
    from concourse import bacc
    from concourse.bass_utils import run_bass_kernel_spmd

    w = {k: np.asarray(v) for k, v in w.items()}

    def taps(a):
        return a.transpose(1, 2, 3, 0).reshape(C, -1)

    def words(mask):
        return np.pad(mask.view(np.uint8).reshape(1, -1, 1), ((0, 0), (0, 0), (0, 3))).view(np.int32)[:, :, 0]

    arrays = {
        "x": np.ascontiguousarray(np.asarray(x).reshape(B, C, N)),
        "cst": constants(),
        "w32": np.concatenate([
            taps(w["L0_conv_w_off"]), taps(w["L0_conv_w_dcn"]), taps(w["L1_conv_conv_w"]), w["L2_attn_w_qkv"],
            w["L2_ffn_gate_w"].T, w["L3_attn_v_matrix"][:, :, 0].transpose(3, 0, 1, 2).reshape(C, -1),
            w["L3_attn_q_matrix"][:, :, 0].transpose(3, 0, 1, 2).reshape(C, -1)], 1),
        "par": np.stack([
            w["L1_conv_bn1_g"], w["L1_conv_bn1_b"], w["L1_conv_bn1_m"], w["L1_conv_bn1_v"],
            w["L1_conv_cg2_w"].reshape(CH), w["L1_conv_cg2_b"], w["L1_conv_cg1_w"].reshape(CH)]
            + [np.broadcast_to(w["L1_conv_" + n], (CH,)) for n in ("cg1_b", "cgbn_g", "cgbn_b", "cgbn_m", "cgbn_v")]
            + [np.repeat(w["L1_conv_tau"].reshape(-1), 2), w["L2_ffn_gate_b"]], 1),
        "rows": np.concatenate([w["L0_conv_b_off"], w["L2_attn_ln_w"], w["L2_attn_ln_b"], w["L2_attn_b_out"]]),
        "toep": np.pad(w["L2_attn_res_w"].reshape(HEADS, KRES),
                       ((0, 0), (2 * P - KRES // 2 - 1, TOEP_PAD - 2 * P + 1 - KRES + KRES // 2))),
        "w_out": w["L2_attn_w_out"],
        "moe_w1": np.ascontiguousarray(w["L2_ffn_weight1"].transpose(1, 0, 2)),
        "moe_w2": np.ascontiguousarray(w["L2_ffn_weight2"][:, :HID].transpose(1, 0, 2)),
        "moe_b2": w["L2_ffn_weight2"][:, HID].reshape(1, -1),
        "am": words(w["L3_ffn_attn_mask"]),
        "fm": words(w["L3_ffn_ffn_mask"]),
        "keys": 4 * np.arange(NB * NOPS, dtype=np.float32).reshape(1, -1),
        "rec_a": np.concatenate([w["L3_ffn_ffn_w1"], w["L3_ffn_wq"], w["L3_ffn_wk"], w["L3_ffn_wv"], w["L3_ffn_wo"],
                                 w["L3_ffn_ffn_b2"][..., None]], -1).reshape(NB * NOPS, C, REC_A),
        "rec_b": np.concatenate([w["L3_ffn_ffn_w2"], w["L3_ffn_ffn_b1"][..., None]], -1
                                ).reshape(NB * NOPS, HID, REC_B),
    }
    arrays = {k: np.ascontiguousarray(a) for k, a in arrays.items()}
    nc = bacc.Bacc("TRN2", target_bir_lowering=False, num_devices=1)
    args = [nc.dram_tensor(k, a.shape, mybir.dt.from_np(a.dtype), kind="ExternalInput").ap()
            for k, a in arrays.items()]
    out = nc.dram_tensor("out", (B, C, N), F32, kind="ExternalOutput").ap()
    build(nc, *args, out)
    r = run_bass_kernel_spmd(nc, [arrays], core_ids=[0])
    return r.results[0]["out"].reshape(B, C, HH, WW)
```

```python
from contextlib import ExitStack

import numpy as np

import concourse.bass as bass
from concourse import mybir
from concourse.alu_op_type import AluOpType as ALU

F32 = mybir.dt.float32
I32 = mybir.dt.int32
U32 = mybir.dt.uint32
ACT = mybir.ActivationFunctionType
AX = mybir.AxisListType

B, C, HH, WW = 8, 32, 16, 16
N = HH * WW
P = 128
BI, BG, PT = 4, 2, 2
KK = 9
NOFF = 2 * KK
CH = 16
HEADS, DH, LM = 8, 16, 16
PINV = 6
KRES = 33
EXP, HID = 16, 128
LAYERS, LHEADS = 4, 8
LAG = 4
NB, NOPS = 33, 19
PLACES = (3, 3, 4)
NONE = 4096
SMALL = 16 * 2
LATE = 16 * 10

W32 = {}
_at = 0
for _n, _k in (("off", KK * NOFF), ("dcn", KK * C), ("conv", KK * CH), ("qkv", 3 * P), ("gate", EXP), ("ln", 2),
               ("v", LAYERS * LHEADS * C), ("q", LAYERS * LHEADS * C)):
    W32[_n] = (_at, _at + _k)
    _at += _k
W32_COLS = _at
W32_EARLY = W32["conv"][1]

CST = {}
_at = 0
for _n, _k in (("ident", P), ("flip", P), ("mask4", BI), ("mask8", HEADS), ("base", PT * NOFF),
               ("eye32", C), ("iota", 16), ("rep16", P), ("mask16", P), ("swap", P), ("dft", 2 * 3 * N)):
    CST[_n] = (_at, _at + _k)
    _at += _k
CST_COLS = _at
CST_EARLY = CST["dft"][0]

PAR = ("bn_g", "bn_b", "bn_m", "bn_v", "cg2_w", "cg2_b", "cg1_w", "cg1_b", "cgbn_g", "cgbn_b", "cgbn_m",
       "cgbn_v", "tau", "gate_b")
ROWS = {"b_off": (0, NOFF), "b_out": (NOFF, NOFF + C)}
ROW_COLS = NOFF + C
TOEP_PAD = 512

REC_A = HID + 4 * C + 1
REC_B = C + 1

SEMS = (
    "x_in", "cst_in", "w32_in", "par_in", "late_in",
    "pool_zero", "pool_bd", "var", "std", "xn", "off_mm", "off_ev", "g_mm", "g_ev", "g_evD", "diff", "hat",
    "prod", "tr", "s_ev", "gst", "dcn_mm", "x1_ready",
    "conv_mm", "bn_ready", "feat", "featT_mm", "featT_ev", "f2_mm", "f2_ev", "swap_mm",
    "l2_sum", "l2_std", "sm2_in", "sm2_exp", "sum_sq", "abs", "cg_mm", "cg_act", "gated", "gT_mm",
    "gT_ev", "inv_mm", "inv_sq", "toT_mm",
    "ct_in", "ct_mm", "ct_ev",
    "qk_mm", "q_ev", "k_ev", "pool_in", "lk_mm", "lk_ev", "ql_bd", "kl_bd", "v_mm", "v_ev", "sim2_mm",
    "sim3_mm", "a3_max", "a3_exp", "a3T_mm", "a3T_ev", "w3_mm", "w3_ev", "sim1_mm", "a1_sub", "a1_exp",
    "a1_norm", "a1_sum", "a1T_mm", "a1T_ev", "res_mm", "res_ev", "a2_sub", "a2_exp", "x_bd", "xT_mm", "xT_ev",
    "cr_in", "cr_max", "z_new", "zT_new", "pi_mm", "y_ev", "t_ready", "w2_mm", "w2_ev", "w2_evD",
    "oT_mm", "oT_ev", "ao_mm", "ao_ev",
    "lg_mm", "lg_max", "lg_exp", "topk", "mT_mm", "mT_ev", "pl_mm", "pl_ev", "hid_mm", "hid_ev", "hidT_ev", "eo_mm",
    "eo_ev", "eoT_mm", "eo_bd", "moe_mm",
    "la_g", "la_gev", "la_h", "la_hevA", "la_hevD", "la_qbd", "la_r", "la_w", "la_t", "la_tev",
    "la_g2", "la_p", "la_pev", "la_zm",
    "rt_h", "op_mm", "op_read", "op_ev", "w_in", "w_bd", "w1_bd", "w_used", "tok_mm", "tok_ev",
    "rq_mm", "rq_ev", "rk_ev", "rv_mm", "rv_ev", "sc_mm", "sc_max", "sc_exp", "sc_norm",
    "pT_mm", "pT_ev", "ro_mm", "ro_ev", "ry_mm",
    "f1_mm", "f1_ev", "f2mm", "h_new", "out_ready", "out_st",
    "dve_own", "act_own", "passed",
)


class Own:

    def __init__(self, eng, sem):
        self.eng, self.sem, self.n = eng, sem, 0

    def link(self, ins):
        self.n += 1
        ins.then_inc(self.sem, 1)
        self.eng.wait_ge(self.sem, self.n)

    def restart(self):
        self.eng.sem_clear(self.sem)
        self.n = 0


def build(nc, x, cst, w32, par, rows, toep, w_out, moe_w1, moe_w2, moe_b2, am, fm, keys, rec_a, rec_b, out):
    ctx = ExitStack()
    with ctx:
        def sb(name, cols, dt=F32, parts=P):
            return ctx.enter_context(nc.sbuf_tensor(name, [parts, cols], dt))[:, :]

        S = {n: ctx.enter_context(nc.semaphore(n)) for n in SEMS}
        ps = [ctx.enter_context(nc.psum_tensor(f"ps{i}", [P, 512], F32))[:, :] for i in range(8)]

        xC = sb("xC", 512)
        cstb = sb("cstb", CST_COLS)
        w32b = sb("w32b", W32_COLS)
        parb = sb("parb", len(PAR))
        rowb = sb("rowb", ROW_COLS)
        woutb = sb("woutb", C)
        w1b = sb("w1b", EXP * HID, parts=C + 1)
        w2b = sb("w2b", EXP * C)
        b2b = sb("b2b", C, parts=EXP)
        maskb = sb("maskb", NB * NOPS, I32, parts=1)
        flagb = sb("flagb", NB * NOPS, I32, parts=1)

        def cst_(n):
            return cstb[:, CST[n][0]:CST[n][1]]

        def w32_(n):
            return w32b[:, W32[n][0]:W32[n][1]]

        def par_(n):
            return parb[:, PAR.index(n):PAR.index(n) + 1]

        def row_(n):
            return rowb[:, ROWS[n][0]:ROWS[n][1]]

        ident, mask4, mask8, iota = cst_("ident"), cst_("mask4"), cst_("mask8"), cst_("iota")
        dft = cst_("dft").rearrange("p (t n) -> p t n", t=PT)

        arena = sb("arena", 20480)

        def ar(at, cols):
            return arena[:, at:at + cols]

        xnp = ar(18208, BG * 18 * 18).rearrange("p (g y x) -> p g y x", g=BG, y=18)
        xn = ar(18856, BG * N)
        offC = ar(19368, BG * N)
        dcn_bd = ar(13312, BI * KK * C).rearrange("p (b n) -> p b n", b=BI)
        xp = sb("xp", BG * 22 * 22).rearrange("p (g y x) -> p g y x", g=BG, y=22)
        off_bd = sb("off_bd", KK * BI * NOFF).rearrange("p (k b o) -> p k b o", k=KK, b=BI)
        conv_bd = sb("conv_bd", KK * BI * CH).rearrange("p (k b o) -> p k b o", k=KK, b=BI)
        gate_bd = sb("gate_bd", BI * EXP).rearrange("p (b o) -> p b o", b=BI)
        cgw = sb("cgw", P)
        base2 = sb("base2", PT * NOFF).rearrange("p (t o) -> p t o", t=PT)
        zeros = sb("zeros", P)
        x1C = sb("x1C", 512)
        small = sb("small", 512)
        T = sb("T", 512)
        t0 = sb("t0", 512)
        ln_a = sb("ln_a", 512)
        ln_b = sb("ln_b", 512)
        lnC = sb("lnC", 512)
        tC = sb("tC", 512)
        T4 = T.rearrange("p (t b c) -> p t b c", t=PT, b=B)

        GS = ar(0, 4608).rearrange("p (g t b k o) -> p g t b k o", g=BG, t=PT, b=BI, k=KK)
        hat = ar(4608, 4608).rearrange("p (t b k a q) -> p t b k a q", t=PT, b=B, k=KK, a=2)
        ST = ar(9216, 4096).rearrange("p (c t y x) -> p c t y x", c=B, t=PT, y=HH)
        SQ = ar(13312, 4096).rearrange("p (c q n) -> p c q n", c=B, q=PT)
        yx = ar(17408, 288).rearrange("p (t b o) -> p t b o", t=PT, b=B)
        Gst = ar(17696, 512).rearrange("p (g t b o) -> p g t b o", g=BG, t=PT, b=BI)

        feat = sb("feat", N)
        featT = sb("featT", PT * P).rearrange("p (t n) -> p t n", t=PT)
        F2 = ar(18432, 2 * N)
        mixed = ar(18944, 2 * N)
        outf = sb("outf", N)
        gatef = sb("gatef", N)
        scr = sb("scr", 512)
        gated = ar(19456, 512)
        gT = ar(19968, 512).rearrange("p (a t n) -> p a t n", a=2, t=PT)
        cg = sb("cg", N)

        qT, kT, V, a1, a1T, a3, a3T, res, oT = (ar(2048 * i, 2048) for i in range(9))
        toepb = sb("toepb", HEADS * 384).rearrange("p (h n) -> p h n", h=HEADS)
        ql_bd, kl_bd, bdXT, bdz, bdzT, w3_bd = (
            sb(n, 1024).rearrange("p (b h m) -> p b h m", b=B, h=HEADS)
            for n in ("ql_bd", "kl_bd", "bdXT", "bdz", "bdzT", "w3_bd"))
        res_st = scr.rearrange("p (j n) -> p j n", j=BG * PT)
        bdy, bdt, w2_bd = (a.rearrange("p (b h m) -> p b h m", b=B, h=HEADS)
                           for a in (a3[:, 0:1024], a3[:, 1024:2048], kT[:, 0:1024]))
        ql, kl, XM = (sb(n, P).rearrange("p (b m) -> p b m", b=B) for n in ("ql", "kl", "XM"))
        eye7, eye15, eye13 = (sb(n, P) for n in ("eye7", "eye15", "eye13"))
        xpool = sb("xpool", BG * LM)
        xpool_bd = sb("xpool_bd", P)
        qkv_bd = ar(16384, 3 * BI * P).rearrange("p (w b n) -> p w b n", w=3, b=BI)

        probs = sb("probs", N)
        probs_rest = sb("probs_rest", N)
        mT = sb("mT", N).rearrange("p (t e) -> p t e", t=PT)
        pooled = sb("pooled", P, parts=C + 1)
        hid_rows = scr
        hid = ln_b.rearrange("p (e b) -> p e b", e=EXP)
        eo = sb("eo", P, parts=C)
        eo_bd = sb("eo_bd", B * C).rearrange("p (b o) -> p b o", b=B)

        ZT_, ZC = sb("ZT_", 512), sb("ZC", 512)
        g_bd, w_la, gw, p_la, m_la = (ar(a, BG * P) for a in (12288, 14336, 14592, 14848, 15104))
        hs = ar(12544, BG * LHEADS * C).rearrange("p (g j o) -> p g j o", g=BG, j=LHEADS)
        q_bd = ar(13312, LHEADS * P).rearrange("p (j b o) -> p j b o", j=LHEADS, b=BI)

        hC = sb("hC", 512)
        recA = sb("recA", REC_A)
        recB = sb("recB", REC_B)
        top8 = sb("top8", 8, parts=1)
        op8 = sb("op8", 8, U32, parts=1)
        w_bd = ar(0, 512)
        rk, rv, roC = (ar(512 * (1 + i), 512) for i in range(3))
        f1 = ar(3072, 2048)
        rq_bd = f1.rearrange("p (b n) -> p b n", b=BI)
        pr = ar(5120, 4096)
        prT = ar(9216, 4096)
        rmax = sb("rmax", 16)
        rsum = sb("rsum", 16)
        keyb = off_bd.rearrange("p k b o -> p (k b o)")[0:1, 0:NB * NOPS]
        stepb, passed, cand, key = (sb(n, k, parts=1) for n, k in
                                    (("stepb", NB), ("passed_", NB), ("cand", NB), ("key", 1)))
        keyi = sb("keyi", 1, I32, parts=1)
        keyf = ar(15360, NB * NOPS)[0:1, :]
        w2c, b2c, f1t = sb("w2c", REC_B), sb("b2c", 1), sb("f1t", 1)
        w1_bd = ar(13312, BI * HID)
        outC = ln_a

        def expand16(compact):
            return compact.unsqueeze(2).to_broadcast([P, compact.shape[1], HEADS, 16])

        def mask8_for(nb):
            return mask8.unsqueeze(1).unsqueeze(3).to_broadcast([P, nb, HEADS, 16])

        def window(buf, g, y0, x0, rows):
            return buf[:, g, y0:y0 + rows, x0:x0 + WW]

        def arr3(a, k):
            return a.rearrange("p (j k) -> p j k", k=k)

        def norm_std(n):
            return small[:, 208:224] if n == 2 else small[:, 64:80]

        def settled(eng):
            eng.sem_inc(S["passed"], 1)

        def routed(eng, body):
            def places(levels, first):
                with eng.Fori(0, levels[0]) as i:
                    k = eng.value_load(keyi[0:1, 0:1], min_val=0, max_val=2 * NONE)
                    with eng.If(k < NONE):
                        n = eng.snap(first + i)
                        if len(levels) == 1:
                            body(n, k)
                        else:
                            places(levels[1:], n * levels[1])

            places(PLACES, 0)

        def each_tap(eng, body):
            with eng.Fori(0, KK // 3) as row:
                for col in range(3):
                    body(row * 3 + col)

        block = ctx.enter_context(nc.Block())

        @block.sync
        def _(sp):
            sp.dma_start(xC.rearrange("p (g n) -> p g n", g=BG),
                         x.rearrange("(g b) c n -> (b c) g n", g=BG)).then_inc(S["x_in"], 16)
            sp.dma_start(cstb[:, 0:CST_EARLY], cst[:, 0:CST_EARLY]).then_inc(S["cst_in"], 16)
            sp.dma_start(rowb, rows.partition_broadcast(P)).then_inc(S["par_in"], 16)
            sp.dma_start(parb, par.unsqueeze(0).to_broadcast([B, CH, len(PAR)])).then_inc(S["par_in"], 16)
            sp.dma_start(cstb[:, CST_EARLY:CST_COLS], cst[:, CST_EARLY:CST_COLS]).then_inc(S["late_in"], 16)
            sp.dma_start(w32b[:, W32_EARLY:W32_COLS], w32[:, W32_EARLY:W32_COLS].unsqueeze(0)
                         .to_broadcast([BI, C, W32_COLS - W32_EARLY])).then_inc(S["late_in"], 16)
            sp.dma_start(toepb, bass.AP(tensor=toep.tensor, offset=0, ap=[[1, P], [TOEP_PAD, HEADS], [1, 384]])
                         ).then_inc(S["late_in"], 16)
            sp.dma_start(woutb, w_out).then_inc(S["late_in"], 16)
            sp.dma_start(w1b.rearrange("d (e h) -> d e h", e=EXP), moe_w1).then_inc(S["late_in"], 16)
            sp.dma_start(w2b.rearrange("h (e o) -> h e o", e=EXP), moe_w2).then_inc(S["late_in"], 16)
            sp.dma_start(b2b, moe_b2).then_inc(S["late_in"], 16)
            sp.dma_start(maskb, am).then_inc(S["late_in"], 16)
            sp.dma_start(flagb, fm).then_inc(S["late_in"], 16)
            sp.wait_ge(S["off_mm"], BG)
            sp.dma_start(keyb, keys).then_inc(S["late_in"], 16)

            def fetch(last_used):
                k = sp.value_load(keyi[0:1, 0:1], min_val=0, max_val=2 * NONE)
                with sp.If(k < NONE):
                    rec = nc.s_assert_within(sp.snap(k // 4), 0, NB * NOPS - 1, skip_runtime_bounds_check_because=
                                             "a key below NONE is an active step's, so its record exists")
                    if last_used is not None:
                        sp.wait_ge(S["w_used"], last_used)
                        settled(sp)
                    sp.dma_start(recA, rec_a[bass.ds(rec, 1), :, :].to_broadcast([BI, C, REC_A])
                                 ).then_inc(S["w_in"], 16)
                    sp.dma_start(recB, rec_b[bass.ds(rec, 1), :, :].rearrange("a c n -> (a c) n")
                                 ).then_inc(S["w_in"], 16)
                with sp.Else():
                    sp.wait_ge(S["out_ready"], 1)
                    sp.dma_start(out.rearrange("(g b) c n -> (b c) g n", g=BG),
                                 outC.rearrange("p (g n) -> p g n", g=BG)).then_inc(S["out_st"], 16)

            def step(n, k):
                sp.sem_inc(S["op_read"], 1)
                sp.wait_ge(S["op_ev"], n + 2)
                settled(sp)
                fetch(n + 1)

            sp.wait_ge(S["op_ev"], 1)
            fetch(None)
            routed(sp, step)
            sp.wait_ge(S["out_st"], 16)

        @block.gpsimd
        def _(pool):
            nc.gpsimd.memset(xnp, 0.0).then_inc(S["pool_zero"], 1)
            nc.gpsimd.memset(zeros, 0.0).then_inc(S["pool_zero"], 1)
            nc.gpsimd.memset(xp, 0.0).then_inc(S["pool_zero"], 1)
            pool.wait_ge(S["pool_zero"], 3)
            nc.gpsimd.memset(pooled[C:C + 1, :], 1.0).then_inc(S["pool_zero"], 1)
            pool.wait_ge(S["pool_zero"], 4)
            pool.wait_ge(S["cst_in"], 16)
            pool.wait_ge(S["w32_in"], 16)

            def bd4(dst, src, k, o):
                m = mask4.unsqueeze(1).unsqueeze(3).to_broadcast([P, k, BI, o])
                s = src.rearrange("p (k o) -> p k o", k=k).unsqueeze(2).to_broadcast([P, k, BI, o])
                return nc.gpsimd.tensor_tensor(dst, s, m, ALU.mult)

            bd4(off_bd, w32_("off"), KK, NOFF).then_inc(S["pool_bd"], 1)
            nc.gpsimd.tensor_tensor(dcn_bd, w32_("dcn").unsqueeze(1).to_broadcast([P, BI, KK * C]),
                                    mask4.unsqueeze(2).to_broadcast([P, BI, KK * C]), ALU.mult
                                    ).then_inc(S["pool_bd"], 1)
            pool.wait_ge(S["par_in"], SMALL)
            nc.gpsimd.tensor_tensor(base2, cst_("base").rearrange("p (t o) -> p t o", t=PT),
                                    row_("b_off").unsqueeze(1).to_broadcast([P, PT, NOFF]),
                                    ALU.add).then_inc(S["pool_bd"], 1)
            bd4(conv_bd, w32_("conv"), KK, CH).then_inc(S["pool_bd"], 1)
            nc.gpsimd.tensor_scalar(cgw, cst_("mask16"), par_("cg1_w"), None, ALU.mult).then_inc(S["pool_bd"], 1)
            pool.wait_ge(S["late_in"], LATE)
            nc.gpsimd.tensor_tensor(gate_bd, w32_("gate").unsqueeze(1).to_broadcast([P, BI, EXP]),
                                    mask4.unsqueeze(2).to_broadcast([P, BI, EXP]), ALU.mult
                                    ).then_inc(S["pool_bd"], 1)
            pool.wait_ge(S["g_ev"], PT * BI)
            pool.wait_ge(S["g_evD"], PT * BI)

            def tap(k):
                for g in range(BG):
                    pool.wait_ge(S["dcn_mm"], k * BG + g + 1)
                    nc.gpsimd.tensor_copy(Gst[:, g].rearrange("p t b o -> p (t b) o"),
                                          GS[:, g].rearrange("p t b k o -> p (t b) k o")[:, :, bass.ds(k, 1), :]
                                          .rearrange("p a k o -> p a (k o)")).then_inc(S["gst"], 1)

            each_tap(pool, tap)
            pool.wait_ge(S["late_in"], LATE)
            pool.wait_ge(S["dcn_mm"], (KK + 2) * BG)
            nc.gpsimd.tensor_tensor(qkv_bd, w32_("qkv").rearrange("p (w n) -> p w n", w=3).unsqueeze(2)
                                    .to_broadcast([P, 3, BI, P]),
                                    mask4.unsqueeze(1).unsqueeze(3).to_broadcast([P, 3, BI, P]), ALU.mult
                                    ).then_inc(S["pool_bd"], 1)
            pool.wait_ge(S["lk_ev"], 1)
            nc.gpsimd.tensor_tensor(ql_bd, expand16(ql), mask8_for(B), ALU.mult).then_inc(S["ql_bd"], 1)
            pool.wait_ge(S["cr_in"], 1)
            nc.gpsimd.partition_all_reduce(small[:, 32:34], small[:, 16:18], P, bass.bass_isa.ReduceOp.max
                                           ).then_inc(S["cr_max"], 1)
            def stage_residual(bi):
                r4 = res.rearrange("p (t b n) -> p b t n", t=PT, b=BI)
                for t in range(PT):
                    ins = nc.gpsimd.tensor_copy(res_st.rearrange("p (g t) n -> p t g n", g=BG)[:, t],
                                                r4[:, bi, t].rearrange("p (g n) -> p g n", g=BG))
                ins.then_inc(S["gst"], 1)

            pool.wait_ge(S["res_ev"], 4)
            stage_residual(0)
            for bi in range(BI):
                pool.wait_ge(S["a1_sum"], bi + 1)
                v = arr3(a1[:, 512 * bi:512 * bi + 512], 16)
                nc.gpsimd.tensor_tensor(v, v, small[:, 256 + 32 * bi:288 + 32 * bi].unsqueeze(2)
                                        .to_broadcast([P, 32, 16]), ALU.mult).then_inc(S["a1_norm"], 1)
            for bi in range(1, BI):
                pool.wait_ge(S["res_mm"], BI + bi)
                stage_residual(bi)
            with pool.Fori(0, LAYERS) as l:
                pool.wait_ge(S["la_r"], l + 1)
                src = w32_("q").rearrange("p (l n) -> p l n", l=LAYERS)[:, bass.ds(l, 1), :]
                src = src.rearrange("p l (j o) -> p (l j) o", o=C).unsqueeze(2).to_broadcast([P, LHEADS, BI, C])
                nc.gpsimd.tensor_tensor(q_bd, src, mask4.unsqueeze(1).unsqueeze(3)
                                        .to_broadcast([P, LHEADS, BI, C]), ALU.mult).then_inc(S["la_qbd"], 1)

            def add_if_last(h_count):
                k = pool.value_load(keyi[0:1, 0:1], min_val=0, max_val=2 * NONE)
                with pool.If(k >= NONE):
                    pool.wait_ge(S["h_new"], h_count)
                    settled(pool)
                    nc.gpsimd.tensor_tensor(outC, tC, hC, ALU.add).then_inc(S["out_ready"], 1)

            def step(n, k):
                pool.sem_inc(S["op_read"], 1)
                pool.wait_ge(S["op_ev"], n + 2)
                settled(pool)
                add_if_last(n + 2)

            pool.wait_ge(S["ct_ev"], 4)
            pool.wait_ge(S["op_ev"], 1)
            add_if_last(1)
            routed(pool, step)

        @block.tensor
        def _(pe):
            mm = nc.tensor.matmul
            tr = nc.tensor.transpose

            def to_C(src, bank, n):
                for g in range(BG):
                    for t in range(PT):
                        c0 = (t * B + g * BI) * C
                        last = tr(ps[bank][:, (g * PT + t) * P:(g * PT + t + 1) * P], src[:, c0:c0 + P], ident)
                last.then_inc(n, 1)

            pe.wait_ge(S["xn"], 2 * BG)
            pe.wait_ge(S["pool_bd"], 1)
            for g in range(BG):
                for k in range(KK):
                    last = mm(ps[g][0:BI * NOFF, 0:N], off_bd[:, k, :, :], window(xnp, g, k // 3, k % 3, 16),
                              start=(k == 0), stop=(k == KK - 1))
                last.then_inc(S["off_mm"], 1)
            pe.wait_ge(S["off_ev"], BG)
            for t in range(PT):
                for g in range(BG):
                    c0 = (t * BG + g) * BI * NOFF
                    last = tr(ps[2][:, c0:c0 + BI * NOFF],
                              offC[0:BI * NOFF, g * N + t * P:g * N + t * P + P],
                              ident[0:BI * NOFF, 0:BI * NOFF])
            last.then_inc(S["off_mm"], 1)
            pe.wait_ge(S["pool_bd"], 2)
            for r in range(BG * PT):
                for bi in range(BI):
                    if 0 < r <= PT:
                        pe.wait_ge(S["g_ev"], (r - 1) * BI + bi + 1)
                    elif r:
                        pe.wait_ge(S["g_evD"], (r - 1 - PT) * BI + bi + 1)
                    mm(ps[4 + bi][:, 0:KK * C], xn[:, r * P:r * P + P], dcn_bd[:, bi, :],
                       start=True, stop=True).then_inc(S["g_mm"], 1)
            pe.wait_ge(S["g_evD"], PT * BI)
            pe.wait_ge(S["pool_zero"], 2)
            for g in range(BG):
                mm(ps[4 + g][:, 0:N], zeros, xn[:, 0:N], start=True, stop=False)
            pe.sem_inc(S["dcn_mm"], BG)
            pe.sem_inc(S["tr"], B)

            def transposes(k, g):
                for c in range(g * BI, g * BI + BI):
                    pe.wait_ge(S["prod"], k * B + c + 1)
                    pe.wait_ge(S["s_ev"], k * B + c + 1)
                    for q in range(PT):
                        for t in range(PT):
                            last = tr(ps[c % BI][:, (q * PT + t) * P:(q * PT + t + 1) * P],
                                      ST[:, c, t, q * 8:q * 8 + 8, :], ident)
                    last.then_inc(S["tr"], 1)

            def products(k, g):
                pe.wait_ge(S["gst"], k * BG + g + 1)
                pe.wait_ge(S["s_ev"], k * B + (g + 2) * BI)
                for q in range(PT):
                    for bi in range(BI):
                        last = mm(ps[4 + g][32 * bi:32 * bi + 32, 0:N], Gst[:, g, q, bi, :],
                                  SQ[:, g * BI + bi, q, :], start=False, stop=False, skip_group_check=True)
                last.then_inc(S["dcn_mm"], 1)

            transposes(0, 0)
            with pe.Fori(0, (KK - 1) // 2) as pair:
                for odd in range(2):
                    k = pair * 2 + odd
                    transposes(k, 1)
                    products(k, 0)
                    transposes(k + 1, 0)
                    products(k, 1)
            transposes(KK - 1, 1)
            products(KK - 1, 0)
            products(KK - 1, 1)
            for g in range(BG):
                mm(ps[4 + g][:, 0:N], zeros, xn[:, 0:N], start=False, stop=True).then_inc(S["dcn_mm"], 1)
            pe.wait_ge(S["x1_ready"], BG)
            pe.wait_ge(S["pool_bd"], 4)
            for g in range(BG):
                for k in range(KK):
                    last = mm(ps[g][64 * g:64 * g + 64, 0:N], conv_bd[:, k, :, :],
                              window(xp, g, 3 * (k // 3), 3 * (k % 3), 16), start=(k == 0), stop=(k == KK - 1))
                last.then_inc(S["conv_mm"], 1)
            pe.wait_ge(S["feat"], BG)
            for t in range(PT):
                last = tr(ps[2][:, t * P:t * P + P], feat[:, t * P:t * P + P], ident)
            last.then_inc(S["featT_mm"], 1)
            mm(ps[5][:, 0:N], cst_("swap"), feat, start=True, stop=True).then_inc(S["swap_mm"], 1)
            pe.wait_ge(S["featT_ev"], 1)
            pe.wait_ge(S["late_in"], LATE)
            for t in range(PT):
                last = mm(ps[3], featT[:, t, :], dft[:, t, 0:2 * N], start=(t == 0), stop=(t == PT - 1))
            last.then_inc(S["f2_mm"], 1)
            pe.wait_ge(S["f2_ev"], 1)
            pe.wait_ge(S["pool_bd"], 5)
            mm(ps[6][:, 0:N], cgw, F2[:, 0:N], start=True, stop=True).then_inc(S["cg_mm"], 1)
            mm(ps[4], cst_("swap"), F2, start=True, stop=True).then_inc(S["swap_mm"], 1)
            for g in range(BG):
                for t in range(PT):
                    last = tr(ps[0][:, (t * BG + g) * P:(t * BG + g + 1) * P],
                              x1C[:, g * N + t * P:g * N + t * P + P], ident)
            last.then_inc(S["toT_mm"], 1)
            pe.wait_ge(S["gated"], 2)
            for a in range(2):
                for t in range(PT):
                    last = tr(ps[7][:, (a * PT + t) * P:(a * PT + t + 1) * P],
                              gated[:, a * N + t * P:a * N + t * P + P], ident)
            last.then_inc(S["gT_mm"], 1)
            pe.wait_ge(S["gT_ev"], 1)
            for n, (a, t) in enumerate(((0, 0), (0, 1), (1, 0), (1, 1))):
                last = mm(ps[2], gT[:, a, t, :], dft[:, t, a * N:a * N + 2 * N], start=(n == 0), stop=(n == 3))
            last.then_inc(S["inv_mm"], 1)
            pe.wait_ge(S["abs"], 2)
            for n, src in enumerate((outf, gatef)):
                for t in range(PT):
                    last = tr(ps[1][:, (n * PT + t) * P:(n * PT + t + 1) * P], src[:, t * P:t * P + P], ident)
            last.then_inc(S["toT_mm"], 1)

            pe.wait_ge(S["ct_in"], 1)
            to_C(ln_b, 0, S["ct_mm"])
            pe.wait_ge(S["ct_ev"], 1)
            pe.wait_ge(S["late_in"], LATE)
            wq, wk = (w32_("qkv")[:, P * i:P * i + P] for i in range(2))
            pe.wait_ge(S["pool_bd"], 7)
            for w, bank in ((0, 0), (1, 4)):
                for bi in range(BI):
                    mm(ps[bank + bi], qkv_bd[:, w, bi, :], lnC, start=True, stop=True).then_inc(S["qk_mm"], 1)
            pe.wait_ge(S["pool_in"], 1)
            pe.wait_ge(S["q_ev"], 1)
            mm(ps[0][:, 0:P], wq, xpool_bd, start=True, stop=True)
            mm(ps[0][:, P:2 * P], wk, xpool_bd, start=True, stop=True).then_inc(S["lk_mm"], 1)
            for j in range(BG * PT):
                pe.wait_ge(S["k_ev"], j + 1)
                mm(ps[4 + j], lnC[:, j * P:j * P + P], qkv_bd[:, 2, :, :], start=True, stop=True
                   ).then_inc(S["v_mm"], 1)
            pe.wait_ge(S["ql_bd"], 1)
            pe.wait_ge(S["kl_bd"], 1)
            for b in range(B):
                last = mm(ps[0][:, 16 * b:16 * b + 16], ql_bd[:, b, :, :], kl[:, b, :], start=True, stop=True)
            last.then_inc(S["sim2_mm"], 1)
            for bi in range(BI):
                pe.wait_ge(S["v_ev"], bi + 1)
                for g in range(BG):
                    last = mm(ps[4 + bi][:, g * N:g * N + N], ql_bd[:, 2 * bi + g, :, :],
                              kT[:, 512 * bi + N * g:512 * bi + N * g + N], start=True, stop=True)
                last.then_inc(S["sim3_mm"], 1)
            for bi in range(BI):
                pe.wait_ge(S["a3_exp"], bi + 1)
                for j in range(4):
                    last = tr(ps[4 + bi][:, j * P:j * P + P], a3[:, 512 * bi + j * P:512 * bi + j * P + P], ident)
                last.then_inc(S["a3T_mm"], 1)
            for bi in range(BI):
                pe.wait_ge(S["a3T_ev"], bi + 1)
                for g in range(BG):
                    b = 2 * bi + g
                    for t in range(PT):
                        c0 = 512 * bi + (g * PT + t) * P
                        last = mm(ps[2 + b // 4][:, (b % 4) * P:(b % 4) * P + P], a3T[:, c0:c0 + P],
                                  V[:, c0:c0 + P], start=(t == 0), stop=(t == PT - 1))
            last.then_inc(S["w3_mm"], 1)
            pe.wait_ge(S["x_bd"], 1)
            for b in range(B):
                last = tr(ps[b // 4][:, (b % 4) * P:(b % 4) * P + P], bdz[:, b, :, :], ident)
            last.then_inc(S["xT_mm"], 1)
            for bi in range(BI):
                for g in range(BG):
                    for t in range(PT):
                        c0 = 512 * bi + g * N + t * P
                        last = mm(ps[4 + bi][:, (g * PT + t) * P:(g * PT + t + 1) * P], qT[:, c0:c0 + P],
                                  kl_bd[:, 2 * bi + g, :, :], start=True, stop=True)
                last.then_inc(S["sim1_mm"], 1)
            pe.wait_ge(S["late_in"], LATE)
            pe.wait_ge(S["w3_ev"], 1)
            pe.wait_ge(S["xT_ev"], 2)
            Vb = V.rearrange("p (b t n) -> p b t n", b=B, t=PT)
            for t in range(PT):
                for h in range(HEADS):
                    for s in range(PT):
                        col = (1 - t + s) * P
                        last = mm(ps[2 * t + h // 4][:, (h % 4) * P:(h % 4) * P + P], toepb[:, h, col:col + P],
                                  Vb[:, :, s, h * DH:h * DH + DH], start=(s == 0), stop=(s == PT - 1))
                    if h % 4 == 3:
                        last.then_inc(S["res_mm"], 1)
            pe.wait_ge(S["res_ev"], 2)
            pe.wait_ge(S["a1_sub"], BI)

            def product(bank, half, lhs, rhs):
                for j in range(4):
                    b = half * 4 + j
                    last = mm(ps[bank + half][:, j * P:j * P + P], lhs[:, b, :, :], rhs[:, b, :, :],
                              start=True, stop=True)
                last.then_inc(S["pi_mm"], 1)

            def pinv_step(it, meanwhile, last_one):
                for half in range(2):
                    pe.wait_ge(S["z_new"], it * 2 + 1 + half)
                    product(0, half, bdXT, bdz)
                meanwhile(it)
                for half in range(2):
                    pe.wait_ge(S["t_ready"], it * 6 + 1 + half)
                    pe.wait_ge(S["y_ev"], it * 2 + 1 + half)
                    product(2, half, bdy, bdt)
                for half in range(2):
                    pe.wait_ge(S["t_ready"], it * 6 + 3 + half)
                    product(0, half, bdy, bdt)
                if not last_one:
                    for half in range(2):
                        pe.wait_ge(S["t_ready"], it * 6 + 5 + half)
                        pe.wait_ge(S["zT_new"], it * 2 + 1 + half)
                        product(6, half, bdzT, bdt)
                for half in range(2):
                    if last_one:
                        pe.wait_ge(S["t_ready"], it * 6 + 5 + half)
                        pe.wait_ge(S["zT_new"], it * 2 + 1 + half)
                    product(2, half, bdt, bdzT)

            def turn_residual(it):
                pe.wait_ge(S["gst"], it + KK * BG)
                pe.wait_ge(S["res_ev"], it + 3)
                for j in range(BG * PT):
                    last = mm(ps[4][:, j * P:j * P + P], res_st[:, j, :], cst_("flip"), start=True, stop=True)
                last.then_inc(S["res_mm"], 1)

            def transpose_a1(it):
                for bi in range(BI):
                    pe.wait_ge(S["a1_norm"], bi + 1)
                    pe.wait_ge(S["res_ev"], 2 * BI)
                    for j in range(4):
                        last = tr(ps[4 + bi][:, j * P:j * P + P], a1[:, 512 * bi + j * P:512 * bi + j * P + P],
                                  ident)
                    last.then_inc(S["a1T_mm"], 1)

            pinv_step(0, lambda it: pe.wait_ge(S["res_ev"], 4), False)
            with pe.Fori(1, PINV - 1) as it:
                pinv_step(it, turn_residual, False)
            pinv_step(PINV - 1, transpose_a1, True)
            pe.wait_ge(S["zT_new"], 2 * PINV + 2)
            for b in range(B):
                last = mm(ps[b // 4][:, (b % 4) * P:(b % 4) * P + P], bdzT[:, b, :, :], w3_bd[:, b, :, :],
                          start=True, stop=True)
            last.then_inc(S["w2_mm"], 1)
            for bi in range(BI):
                pe.wait_ge(S["w2_ev"] if bi < 2 else S["w2_evD"], 1)
                pe.wait_ge(S["a1T_ev"], BI)
                for g in range(BG):
                    b = 2 * bi + g
                    last = mm(ps[4 + bi][:, g * N:g * N + N], w2_bd[:, b, :, :], a1T[:, N * b:N * b + N],
                              start=True, stop=True)
                last.then_inc(S["oT_mm"], 1)
            pe.wait_ge(S["late_in"], LATE)
            for bi in range(BI):
                pe.wait_ge(S["oT_ev"], bi + 1)
                last = mm(ps[0][32 * bi:32 * bi + 32, :], woutb, oT[:, 512 * bi:512 * bi + 512],
                          start=True, stop=True)
            last.then_inc(S["ao_mm"], 1)
            pe.wait_ge(S["ao_ev"], 1)
            for g in range(BG):
                for t in range(PT):
                    last = tr(ps[1][:, (t * BG + g) * P:(t * BG + g + 1) * P],
                              lnC[:, g * N + t * P:g * N + t * P + P], ident)
            last.then_inc(S["ao_mm"], 1)

            pe.wait_ge(S["ct_in"], 2)
            to_C(t0, 3, S["ct_mm"])
            pe.wait_ge(S["ct_ev"], 2)
            pe.wait_ge(S["pool_bd"], 6)
            for g in range(BG):
                last = mm(ps[2][64 * g:64 * g + 64, 0:N], gate_bd, lnC[:, g * N:g * N + N], start=True, stop=True)
            last.then_inc(S["lg_mm"], 1)
            pe.wait_ge(S["topk"], 1)
            for t in range(PT):
                last = tr(ps[3][:, t * P:t * P + P], probs[:, t * P:t * P + P], ident)
            last.then_inc(S["mT_mm"], 1)
            pe.wait_ge(S["mT_ev"], 1)
            for b in range(B):
                for t in range(PT):
                    j = t * B + b
                    last = mm(ps[4][0:C, 16 * b:16 * b + 16], t0[:, j * C:j * C + C], mT[:, t, 16 * b:16 * b + 16],
                              start=(t == 0), stop=(t == PT - 1))
            last.then_inc(S["pl_mm"], 1)
            pe.wait_ge(S["pl_ev"], 1)
            pe.wait_ge(S["late_in"], LATE)
            pe.wait_ge(S["pool_zero"], 4)
            for e in range(EXP):
                q, c = e % 4, e // 4
                last = mm(ps[5][32 * q:32 * q + B, HID * c:HID * c + HID], pooled[:, B * e:B * e + B],
                          w1b[:, HID * e:HID * e + HID], start=True, stop=True)
            last.then_inc(S["hid_mm"], 1)
            pe.wait_ge(S["hid_ev"], 1)
            for c in range(4):
                last = tr(ps[6][:, c * P:c * P + P], hid_rows[:, c * P:c * P + P], ident)
            last.then_inc(S["hid_mm"], 1)
            pe.wait_ge(S["hidT_ev"], 1)
            for e in range(EXP):
                last = mm(ps[4][0:C, B * e:B * e + B], w2b[:, C * e:C * e + C], hid[:, e, 0:B],
                          start=True, stop=True)
            last.then_inc(S["eo_mm"], 1)
            mm(ps[7][:, 0:C], cst_("rep16")[0:EXP, :], b2b, start=True, stop=False)
            pe.wait_ge(S["eo_ev"], 1)
            mm(ps[7][:, 0:C], eo, ident[0:C, 0:C], start=False, stop=True).then_inc(S["eoT_mm"], 1)
            pe.wait_ge(S["eo_bd"], 1)
            for t in range(PT):
                last = mm(ps[0][:, t * N:t * N + N], probs[:, t * P:t * P + P], eo_bd, start=True, stop=True)
            last.then_inc(S["moe_mm"], 1)

            pe.wait_ge(S["ct_in"], 3)
            for g in range(BG):
                for t in range(PT):
                    c0 = (t * B + g * BI) * C
                    last = mm(ps[2][:, g * P:g * P + P], ZT_[:, c0:c0 + P], ZT_[:, c0:c0 + P],
                              start=(t == 0), stop=(t == PT - 1))
            last.then_inc(S["la_g"], 1)
            to_C(ZT_, 1, S["ct_mm"])
            VT = w32_("v").rearrange("p (l n) -> p l n", l=LAYERS)
            pe.sem_inc(S["la_r"], 1)
            hs2 = hs.rearrange("p g j o -> p j g o")

            def layer(l, last_one):
                pe.wait_ge(S["la_gev"], l + 1)
                for g in range(BG):
                    mm(ps[3 + g][:, 0:N], g_bd[:, g * P:g * P + P], VT[:, bass.ds(l, 1), :],
                       start=True, stop=True).then_inc(S["la_h"], 1)
                mm(ps[2][:, 0:BG * C], ident, cst_("eye32").unsqueeze(1).to_broadcast([P, BG, C]),
                   start=True, stop=False)
                pe.wait_ge(S["la_hevA"], l + 1)
                pe.wait_ge(S["la_hevD"], l + 1)
                pe.wait_ge(S["la_qbd"], l + 1)
                for j in range(LHEADS):
                    last = mm(ps[2][:, 0:BG * C], q_bd[:, j, :, :], hs2[:, j, :, :],
                              start=False, stop=(j == LHEADS - 1))
                last.then_inc(S["la_r"], 1)
                pe.wait_ge(S["la_w"], l + 1)
                if last_one:
                    pe.wait_ge(S["la_pev"], l + 1)
                    for g in range(BG):
                        gg = slice(g * P, g * P + P)
                        last = mm(ps[5][:, gg], p_la[:, gg], w_la[:, gg], start=True, stop=True)
                    last.then_inc(S["la_p"], 1)
                    return
                for g in range(BG):
                    gg = slice(g * P, g * P + P)
                    last = mm(ps[5][:, gg], g_bd[:, gg], w_la[:, gg], start=True, stop=True)
                last.then_inc(S["la_t"], 1)
                pe.wait_ge(S["la_pev"], l + 1)
                for g in range(BG):
                    gg = slice(g * P, g * P + P)
                    last = mm(ps[7][:, gg], w_la[:, gg], p_la[:, gg], start=True, stop=True)
                last.then_inc(S["la_p"], 1)
                pe.wait_ge(S["la_tev"], l + 1)
                for g in range(BG):
                    gg = slice(g * P, g * P + P)
                    last = mm(ps[6][:, gg], w_la[:, gg], gw[:, gg], start=True, stop=True)
                last.then_inc(S["la_g2"], 1)

            with pe.Fori(0, LAYERS - 1) as l:
                layer(l, False)
            layer(LAYERS - 1, True)
            pe.wait_ge(S["la_pev"], LAYERS + 1)
            pe.wait_ge(S["ct_ev"], 3)
            for t in range(PT):
                for g in range(BG):
                    c0 = (t * B + g * BI) * C
                    last = mm(ps[0][:, c0:c0 + P], ZC[:, g * N + t * P:g * N + t * P + P],
                              m_la[:, g * P:g * P + P], start=True, stop=True)
            last.then_inc(S["la_zm"], 1)

            pe.wait_ge(S["ct_in"], 4)
            to_C(ln_b, 1, S["ct_mm"])
            to_C(T, 0, S["ct_mm"])
            pe.wait_ge(S["ct_ev"], 4)
            pe.wait_ge(S["op_ev"], 1)

            def step(n, k):
                pe.sem_inc(S["op_read"], 1)
                fl = pe.snap(k % 4)
                ffn = pe.snap(k % 2)
                with pe.If(fl >= 2):
                    wq, wk, wv, wo = (w_bd[:, P * i:P * i + P] for i in range(4))
                    pe.wait_ge(S["h_new"], n + 1)
                    pe.wait_ge(S["w_bd"], n + 1)
                    mm(ps[7], wq, hC, start=True, stop=True).then_inc(S["rq_mm"], 1)
                    mm(ps[6], wk, hC, start=True, stop=True).then_inc(S["rq_mm"], 1)
                    for g in range(BG):
                        for t in range(PT):
                            last = mm(ps[5][:, (g * PT + t) * P:(g * PT + t + 1) * P],
                                      hC[:, g * N + t * P:g * N + t * P + P], wv, start=True, stop=True)
                    last.then_inc(S["rv_mm"], 1)
                    pe.wait_ge(S["rk_ev"], n + 1)
                    for b in range(B + LAG):
                        if b < B:
                            g, bi = divmod(b, BI)
                            if b < BI:
                                pe.wait_ge(S["rq_ev"], n * BI + b + 1)
                            elif b == 5:
                                pe.wait_ge(S["rv_ev"], n + 1)
                            for t in range(PT):
                                last = mm(ps[b][:, t * N:t * N + N], rq_bd[:, bi, g * N + t * P:g * N + t * P + P],
                                          rk[:, g * N:g * N + N], start=True, stop=True)
                            last.then_inc(S["sc_mm"], 1)
                        if b >= LAG:
                            a = b - LAG
                            pe.wait_ge(S["sc_norm"], n * B + a + 1)
                            for t in range(PT):
                                for u in range(PT):
                                    last = tr(ps[a][:, (u * PT + t) * P:(u * PT + t + 1) * P],
                                              pr[:, a * 512 + t * N + u * P:a * 512 + t * N + u * P + P], ident)
                            last.then_inc(S["pT_mm"], 1)
                    for g in range(BG):
                        pe.wait_ge(S["pT_ev"], n * B + (g + 1) * BI)
                        for u in range(PT):
                            for bi in range(BI):
                                last = mm(ps[g][32 * bi:32 * bi + 32, 0:N],
                                          rv[:, (g * PT + u) * P + 32 * bi:(g * PT + u) * P + 32 * bi + 32],
                                          prT[:, (g * BI + bi) * 512 + u * N:(g * BI + bi) * 512 + u * N + N],
                                          start=(u == 0), stop=(u == PT - 1), skip_group_check=True)
                    last.then_inc(S["ro_mm"], 1)
                    pe.wait_ge(S["ro_ev"], n + 1)
                    mm(ps[2], wo, roC, start=True, stop=True).then_inc(S["ry_mm"], 1)
                with pe.Else():
                    pe.sem_inc(S["rq_mm"], 2)
                    pe.sem_inc(S["rv_mm"], 1)
                    pe.sem_inc(S["sc_mm"], B)
                    pe.sem_inc(S["pT_mm"], B)
                    pe.sem_inc(S["ro_mm"], 1)
                    pe.sem_inc(S["ry_mm"], 1)
                with pe.If(ffn != 0):
                    pe.wait_ge(S["w1_bd"], n + 1)
                    pe.wait_ge(S["h_new"], n + 1)
                    pe.wait_ge(S["rt_h"], n + 1)
                    mm(ps[0][:, 0:1], w1_bd[:, 0:HID], hC[:, 0:1], start=True, stop=True).then_inc(S["tok_mm"], 1)
                    for bi in range(BI):
                        mm(ps[4 + bi], w1_bd[:, HID * bi:HID * bi + HID], hC, start=True, stop=True
                           ).then_inc(S["f1_mm"], 1)
                        if bi == 0:
                            pe.wait_ge(S["tok_ev"], n + 1)
                            mm(ps[0][0:1, 0:C], f1t, w2c[:, 0:C], start=True, stop=False)
                            mm(ps[0][0:1, 0:C], b2c[0:C, :], ident[0:C, 0:C], start=False, stop=True
                               ).then_inc(S["op_mm"], 1)
                    for bi in range(BI):
                        pe.wait_ge(S["f1_ev"], n * BI + bi + 1)
                        last = mm(ps[1][32 * bi:32 * bi + 32, :], w2c[:, 0:C], f1[:, 512 * bi:512 * bi + 512],
                                  start=True, stop=True)
                    last.then_inc(S["f2mm"], 1)
                with pe.Else():
                    pe.sem_inc(S["f1_mm"], BI)
                    pe.sem_inc(S["f2mm"], 1)
                    pe.sem_inc(S["tok_mm"], 1)
                    pe.wait_ge(S["rt_h"], n + 1)
                    settled(pe)
                    tr(ps[0][0:1, 0:C], hC[0:C, 0:1], ident[0:C, 0:C]).then_inc(S["op_mm"], 1)
                pe.wait_ge(S["op_ev"], n + 2)
                settled(pe)

            routed(pe, step)

        @block.scalar
        def _(act):
            own = Own(act, S["act_own"])
            af = nc.scalar.activation

            def half_of(a, half):
                return a[:, 4 * half:4 * half + 4].rearrange("p b h m -> p (b h m)")

            def ln_std(n):
                act.wait_ge(S["var"], n + 2)
                af(norm_std(n), small[:, 48:64], ACT.Sqrt).then_inc(S["std"], 1)

            def evac_C(bank, dst, n):
                act.wait_ge(S["ct_mm"], n)
                af(dst, ps[bank], ACT.Copy).then_inc(S["ct_ev"], 1)

            act.dma_start(w32b[:, 0:W32_EARLY], w32[:, 0:W32_EARLY].unsqueeze(0)
                          .to_broadcast([BI, C, W32_EARLY])).then_inc(S["w32_in"], 16)
            act.wait_ge(S["var"], 1)
            af(small[:, 4:6], small[:, 2:4], ACT.Sqrt).then_inc(S["std"], 1)
            act.wait_ge(S["var"], 2)
            af(small[:, 10:12], small[:, 8:10], ACT.Sqrt).then_inc(S["std"], 1)
            act.wait_ge(S["bn_ready"], 1)
            for n in range(PT * BI):
                act.wait_ge(S["g_mm"], n + 1)
                af(GS[:, 0, n // BI, n % BI].rearrange("p k o -> p (k o)"), ps[4 + n % BI][:, 0:KK * C],
                   ACT.Copy).then_inc(S["g_ev"], 1)
            for t in range(PT):
                act.wait_ge(S["diff"], t + 1)
                v = hat[:, t].rearrange("p b k a q -> p (b k a q)")
                own.link(af(v, v, ACT.Abs))
                af(v, v, ACT.Relu, bias=1.0, scale=-1.0).then_inc(S["hat"], 1)
            act.sem_inc(S["s_ev"], BI)

            def tap(k):
                for c in range(B):
                    act.wait_ge(S["tr"], k * B + B + c + 1)
                    act.wait_ge(S["dcn_mm"], k * BG + c // BI + 1)
                    af(SQ[:, c].rearrange("p q n -> p (q n)"), ps[c % BI], ACT.Copy).then_inc(S["s_ev"], 1)

            each_tap(act, tap)
            for g in range(BG):
                act.wait_ge(S["conv_mm"], g + 1)
                hh = slice(64 * g, 64 * g + 64)
                af(feat[hh, :], ps[g][hh, 0:N], ACT.Gelu, bias=small[hh, 13:14], scale=small[hh, 12:13]
                   ).then_inc(S["feat"], 1)
            act.wait_ge(S["featT_mm"], 1)
            af(featT.rearrange("p t n -> p (t n)"), ps[2][:, 0:PT * P], ACT.Copy).then_inc(S["featT_ev"], 1)
            act.wait_ge(S["f2_mm"], 1)
            af(F2, ps[3], ACT.Copy).then_inc(S["f2_ev"], 1)
            act.wait_ge(S["cg_mm"], 1)
            own.link(af(cg, ps[6][:, 0:N], ACT.Gelu, bias=small[:, 15:16], scale=small[:, 14:15]))
            af(cg, cg, ACT.Sigmoid, bias=par_("cg2_b"), scale=par_("cg2_w")).then_inc(S["cg_act"], 1)
            act.wait_ge(S["l2_sum"], 1)
            af(small[:, 18:20], small[:, 16:18], ACT.Sqrt).then_inc(S["l2_std"], 1)
            act.wait_ge(S["gT_mm"], 1)
            af(gT.rearrange("p a t n -> p (a t n)"), ps[7], ACT.Copy).then_inc(S["gT_ev"], 1)
            act.wait_ge(S["sm2_in"], 1)
            af(small[:, 28:32], small[:, 28:32], ACT.Exp).then_inc(S["sm2_exp"], 1)
            act.wait_ge(S["sum_sq"], 1)
            af(outf, outf, ACT.Sqrt).then_inc(S["abs"], 1)
            act.wait_ge(S["inv_mm"], 1)
            af(gated, ps[2], ACT.Square).then_inc(S["inv_sq"], 1)
            act.wait_ge(S["sum_sq"], 2)
            af(gatef, gatef, ACT.Sqrt, scale=1.0 / (N * N)).then_inc(S["abs"], 1)

            ln_std(1)
            ln_std(2)
            act.wait_ge(S["ct_mm"], 1)
            act.wait_ge(S["late_in"], LATE)
            af(lnC, ps[0], ACT.Identity, bias=w32_("ln")[:, 1:2], scale=w32_("ln")[:, 0:1]).then_inc(S["ct_ev"], 1)
            for bi in range(BI):
                act.wait_ge(S["qk_mm"], bi + 1)
                af(qT[:, 512 * bi:512 * bi + 512], ps[bi], ACT.Copy, scale=DH ** -0.5).then_inc(S["q_ev"], 1)
            for j in range(BG * PT):
                act.wait_ge(S["v_mm"], j + 1)
                af(V.rearrange("p (b j n) -> p b j n", b=BI, j=BG * PT)[:, :, j, :],
                   ps[4 + j].rearrange("p (b n) -> p b n", b=BI), ACT.Copy).then_inc(S["v_ev"], 1)
            act.wait_ge(S["a2_sub"], 1)
            af(XM, XM, ACT.Exp).then_inc(S["a2_exp"], 1)
            for bi in range(BI):
                act.wait_ge(S["a3_max"], bi + 1)
                for g in range(BG):
                    b = 2 * bi + g
                    last = af(a3[:, N * b:N * b + N], ps[4 + bi][:, g * N:g * N + N], ACT.Exp,
                              bias=small[:, 80 + b:81 + b], accum_out=small[:, 88 + b:89 + b])
                last.then_inc(S["a3_exp"], 1)
            for bi in range(BI):
                act.wait_ge(S["a3T_mm"], bi + 1)
                af(a3T[:, 512 * bi:512 * bi + 512], ps[4 + bi], ACT.Copy).then_inc(S["a3T_ev"], 1)
            act.wait_ge(S["xT_mm"], 1)
            for half in range(2):
                af(half_of(bdXT, half), ps[half], ACT.Copy).then_inc(S["xT_ev"], 1)
            rr4 = res.rearrange("p (t b h e) -> p t h b e", t=PT, b=B, h=HEADS)

            def residual(n):
                act.wait_ge(S["res_mm"], n + 1)
                af(rr4[:, n // 2, 4 * (n % 2):4 * (n % 2) + 4],
                   ps[n].rearrange("p (h b e) -> p h b e", h=4, b=B), ACT.Copy).then_inc(S["res_ev"], 1)

            for bi in range(BI):
                act.wait_ge(S["a1_sub"], bi + 1)
                v = a1[:, 512 * bi:512 * bi + 512]
                af(v, v, ACT.Exp).then_inc(S["a1_exp"], 1)
                if bi == 1:
                    act.wait_ge(S["cr_in"], 2)
                    c = small[:, 34:35]
                    for half in range(2):
                        af(half_of(bdzT, half), half_of(bdz, half), ACT.Copy, scale=c).then_inc(S["zT_new"], 1)
                        act.wait_ge(S["zT_new"], half + 1)
                        af(half_of(bdz, half), half_of(bdXT, half), ACT.Copy, scale=c).then_inc(S["z_new"], 1)
                    for n in range(3):
                        residual(n)
            residual(3)

            def pinv_step(it, meanwhile, last_one):
                done = it * 10
                for half in range(2):
                    act.wait_ge(S["t_ready"], it * 6 + 1 + half)
                    af(half_of(bdy, half), ps[half], ACT.Copy).then_inc(S["y_ev"], 1)
                meanwhile(it)
                if not last_one:
                    for half in range(2):
                        act.wait_ge(S["pi_mm"], done + 7 + half)
                        af(half_of(bdz, half), ps[6 + half], ACT.Copy).then_inc(S["z_new"], 1)
                    done += 2
                for half in range(2):
                    act.wait_ge(S["pi_mm"], done + 7 + half)
                    af(half_of(bdzT, half), ps[2 + half], ACT.Copy).then_inc(S["zT_new"], 1)

            def residual_turned(it):
                act.wait_ge(S["res_mm"], it + 4)
                af(oT.rearrange("p (b n) -> p b n", b=BI)[:, bass.ds(it - 1, 1), :], ps[4].unsqueeze(1),
                   ACT.Copy).then_inc(S["res_ev"], 1)

            def a1_transposed(it):
                for bi in range(BI):
                    act.wait_ge(S["a1T_mm"], bi + 1)
                    af(a1T[:, 512 * bi:512 * bi + 512], ps[4 + bi], ACT.Copy).then_inc(S["a1T_ev"], 1)

            pinv_step(0, lambda it: None, False)
            with act.Fori(1, PINV - 1) as it:
                pinv_step(it, residual_turned, False)
            pinv_step(PINV - 1, a1_transposed, True)
            act.wait_ge(S["w2_mm"], 1)
            af(half_of(w2_bd, 0), ps[0], ACT.Copy).then_inc(S["w2_ev"], 1)
            act.wait_ge(S["ao_mm"], 1)
            af(lnC, ps[0], ACT.Copy).then_inc(S["ao_ev"], 1)

            ln_std(3)
            evac_C(3, lnC, 2)
            act.wait_ge(S["lg_max"], 1)
            af(probs, probs, ACT.Exp, bias=small[:, 105:106], accum_out=small[:, 106:107]).then_inc(S["lg_exp"], 1)
            act.wait_ge(S["hid_mm"], 1)
            af(hid_rows, ps[5], ACT.Gelu).then_inc(S["hid_ev"], 1)

            ln_std(4)
            evac_C(1, ZC, 3)

            def layer(l, last_one):
                act.wait_ge(S["la_h"], 2 * l + 1)
                af(hs[:, 0].rearrange("p j o -> p (j o)"), ps[3][:, 0:N], ACT.Copy).then_inc(S["la_hevA"], 1)
                if last_one:
                    return
                act.wait_ge(S["la_t"], l + 1)
                af(gw, ps[5][:, 0:BG * P], ACT.Copy).then_inc(S["la_tev"], 1)
                act.wait_ge(S["la_p"], l + 1)
                af(p_la, ps[7][:, 0:BG * P], ACT.Copy).then_inc(S["la_pev"], 1)

            with act.Fori(0, LAYERS - 1) as l:
                layer(l, False)
            layer(LAYERS - 1, True)
            ln_std(5)
            act.wait_ge(S["ct_mm"], 4)
            af(hC, ps[1], ACT.Copy).then_inc(S["h_new"], 1)
            evac_C(0, tC, 5)

            act.wait_ge(S["op_ev"], 1)

            def step(n, k):
                act.sem_inc(S["op_read"], 1)
                fl = act.snap(k % 4)
                ffn = act.snap(k % 2)
                with act.If(fl >= 2):
                    act.wait_ge(S["rq_mm"], n * 2 + 2)
                    af(rk, ps[6], ACT.Copy).then_inc(S["rk_ev"], 1)
                    act.wait_ge(S["rv_mm"], n + 1)
                    af(rv, ps[5], ACT.Copy).then_inc(S["rv_ev"], 1)
                    for b in range(B + LAG):
                        if b < B:
                            act.wait_ge(S["sc_max"], n * B + b + 1)
                            for t in range(PT):
                                last = af(pr[:, b * 512 + t * N:b * 512 + t * N + N], ps[b][:, t * N:t * N + N],
                                          ACT.Exp, bias=rmax[:, 2 * b + t:2 * b + t + 1],
                                          accum_out=rsum[:, 2 * b + t:2 * b + t + 1])
                            last.then_inc(S["sc_exp"], 1)
                        if b >= LAG:
                            a = b - LAG
                            act.wait_ge(S["pT_mm"], n * B + a + 1)
                            af(prT[:, a * 512:a * 512 + 512], ps[a], ACT.Copy).then_inc(S["pT_ev"], 1)
                with act.Else():
                    act.sem_inc(S["rk_ev"], 1)
                    act.sem_inc(S["rv_ev"], 1)
                    act.sem_inc(S["sc_exp"], B)
                    act.sem_inc(S["pT_ev"], B)
                with act.If(ffn != 0):
                    act.wait_ge(S["w1_bd"], n + 1)
                    for bi in range(BI):
                        act.wait_ge(S["f1_mm"], n * BI + bi + 1)
                        af(f1[:, 512 * bi:512 * bi + 512], ps[4 + bi], ACT.Relu, bias=w2c[:, C:C + 1]
                           ).then_inc(S["f1_ev"], 1)
                with act.Else():
                    act.sem_inc(S["f1_ev"], BI)
                act.wait_ge(S["op_ev"], n + 2)
                settled(act)

            routed(act, step)

        @block.vector
        def _(dve):
            own = Own(dve, S["dve_own"])
            link = own.link
            v_ = nc.vector
            tt_, ts_, stt = v_.tensor_tensor, v_.tensor_scalar, v_.scalar_tensor_tensor

            bc16 = lambda a: a.unsqueeze(2).to_broadcast([P, 16, C])

            def centre(src, dst, eps):
                s3, d3, c3 = arr3(src, C), arr3(dst, C), arr3(ln_a, C)
                total, var, sums = small[:, 32:48], small[:, 48:64], small[:, 128:144]
                link(v_.tensor_reduce(total, s3, AX.X, ALU.add))
                link(stt(c3, bc16(total), -1.0 / C, s3, ALU.mult, ALU.add))
                link(tt_(d3, c3, c3, ALU.mult))
                link(v_.tensor_reduce(sums, d3, AX.X, ALU.add))
                ts_(var, sums, 1.0 / C, eps, ALU.mult, ALU.add).then_inc(S["var"], 1)

            def scale_of(n):
                dve.wait_ge(S["std"], n + 2)
                std = norm_std(n)
                link(v_.reciprocal(std, std))
                return std

            def layernorm(src, dst, eps, n):
                centre(src, dst, eps)
                return tt_(arr3(dst, C), arr3(ln_a, C), bc16(scale_of(n)), ALU.mult)

            dve.wait_ge(S["x_in"], 16)
            stats = scr[:, 0:12].rearrange("p (g s) -> p g s", g=BG)
            mv = scr[:, 16:20].rearrange("p (g s) -> p g s", g=BG)
            for g in range(BG):
                link(v_.bn_stats(stats[:, g, :], xC[:, g * N:g * N + N]))
            for g in range(BG):
                link(v_.bn_aggr(mv[:, g, :], stats[:, g, :]))
            ts_(small[:, 2:4], mv[:, :, 1], 1e-5, None, ALU.add).then_inc(S["var"], 1)
            dve.wait_ge(S["std"], 1)
            link(v_.reciprocal(small[:, 4:6], small[:, 4:6]))
            dve.wait_ge(S["pool_zero"], 1)
            for g in range(BG):
                src = xC[:, g * N:g * N + N]
                ts_(xnp[:, g, 1:17, 1:17], src.rearrange("p (y x) -> p y x", y=HH), mv[:, g, 0:1],
                    small[:, 4 + g:5 + g], ALU.subtract, ALU.mult).then_inc(S["xn"], 1)
                ts_(xn[:, g * N:g * N + N], src, mv[:, g, 0:1], small[:, 4 + g:5 + g], ALU.subtract, ALU.mult
                    ).then_inc(S["xn"], 1)
            dve.wait_ge(S["par_in"], SMALL)
            link(ts_(small[:, 8:9], par_("bn_v"), 1e-5, None, ALU.add))
            ts_(small[:, 9:10], par_("cgbn_v"), 1e-5, None, ALU.add).then_inc(S["var"], 1)
            dve.wait_ge(S["std"], 2)
            link(v_.reciprocal(small[:, 10:12], small[:, 10:12]))
            link(tt_(small[:, 12:13], par_("bn_g"), small[:, 10:11], ALU.mult))
            link(tt_(small[:, 14:15], par_("cgbn_g"), small[:, 11:12], ALU.mult))
            link(tt_(small[:, 6:7], par_("bn_m"), small[:, 12:13], ALU.mult))
            link(tt_(small[:, 13:14], par_("bn_b"), small[:, 6:7], ALU.subtract))
            link(tt_(small[:, 7:8], par_("cg1_b"), par_("cgbn_m"), ALU.subtract))
            link(tt_(small[:, 7:8], small[:, 7:8], small[:, 14:15], ALU.mult))
            tt_(small[:, 15:16], small[:, 7:8], par_("cgbn_b"), ALU.add).then_inc(S["bn_ready"], 1)
            for g in range(BG):
                dve.wait_ge(S["off_mm"], g + 1)
                v_.tensor_copy(offC[0:BI * NOFF, g * N:g * N + N], ps[g][0:BI * NOFF, 0:N]
                               ).then_inc(S["off_ev"], 1)
            dve.wait_ge(S["off_mm"], BG + 1)
            dve.wait_ge(S["pool_bd"], 3)
            link(tt_(yx, ps[2][:, 0:288].rearrange("p (t b o) -> p t b o", t=PT, b=B),
                     base2.unsqueeze(2).to_broadcast([P, PT, B, NOFF]), ALU.add))
            for t in range(PT):
                tt_(hat[:, t].rearrange("p b k a q -> p (b k a) q"),
                    yx[:, t].rearrange("p b o -> p (b o)").unsqueeze(2).to_broadcast([P, B * NOFF, 16]),
                    iota.unsqueeze(1).to_broadcast([P, B * NOFF, 16]), ALU.subtract).then_inc(S["diff"], 1)
            for n in range(PT * BI):
                dve.wait_ge(S["g_mm"], PT * BI + n + 1)
                v_.tensor_copy(GS[:, 1, n // BI, n % BI].rearrange("p k o -> p (k o)"),
                               ps[4 + n % BI][:, 0:KK * C]).then_inc(S["g_evD"], 1)
            dve.wait_ge(S["hat"], PT)

            def tap(k):
                for c in range(B):
                    dve.wait_ge(S["tr"], k * B + c + 1)
                    hy = hat[:, :, c, bass.ds(k, 1), 0, :].rearrange("p t k q -> p t (k q)")
                    hx = hat[:, :, c, bass.ds(k, 1), 1, :].rearrange("p t k q -> p t (k q)")
                    tt_(ST[:, c], hy.unsqueeze(3).to_broadcast([P, PT, 16, 16]),
                        hx.unsqueeze(2).to_broadcast([P, PT, 16, 16]), ALU.mult).then_inc(S["prod"], 1)

            each_tap(dve, tap)
            dve.wait_ge(S["dcn_mm"], (KK + 2) * BG)
            for g in range(BG):
                link(tt_(x1C[:, g * N:g * N + N], xC[:, g * N:g * N + N], ps[4 + g][:, 0:N], ALU.add))
                dve.wait_ge(S["pool_zero"], 3)
                v_.tensor_copy(xp[:, g, 3:19, 3:19], x1C[:, g * N:g * N + N].rearrange("p (y x) -> p y x", y=HH)
                               ).then_inc(S["x1_ready"], 1)

            Fp, fp = ps[4], ps[5][:, 0:N]
            dve.wait_ge(S["f2_ev"], 1)
            sm = small
            link(v_.tensor_tensor_reduce(scr, F2, F2, 1.0, 0.0, ALU.mult, ALU.add, sm[:, 16:17]))
            dve.wait_ge(S["swap_mm"], 2)
            link(v_.tensor_copy(mixed, Fp))
            link(v_.tensor_tensor_reduce(scr, mixed, mixed, 1.0, 0.0, ALU.mult, ALU.add, sm[:, 17:18]))
            link(v_.tensor_copy(sm[:, 20:21], sm[:, 16:17]))
            link(v_.tensor_tensor_reduce(scr, F2, mixed, 1.0, 0.0, ALU.mult, ALU.add, sm[:, 21:22]))
            link(v_.tensor_tensor_reduce(scr[:, 0:N], F2[:, N:2 * N], mixed[:, 0:N], 1.0, 0.0, ALU.mult, ALU.add,
                                         sm[:, 22:23]))
            link(v_.tensor_tensor_reduce(scr[:, 0:N], F2[:, 0:N], mixed[:, N:2 * N], 1.0, 0.0, ALU.mult, ALU.add,
                                         sm[:, 23:24]))
            dve.wait_ge(S["cg_act"], 1)
            for a in range(2):
                tt_(gated[:, a * N:a * N + N], F2[:, a * N:a * N + N], cg, ALU.mult).then_inc(S["gated"], 1)
            link(tt_(sm[:, 23:24], sm[:, 22:23], sm[:, 23:24], ALU.subtract))
            link(v_.memset(sm[:, 22:23], 0.0))
            ts_(sm[:, 16:18], sm[:, 16:18], 1e-6, None, ALU.add).then_inc(S["l2_sum"], 1)
            dve.wait_ge(S["l2_std"], 1)
            link(v_.reciprocal(sm[:, 18:20], sm[:, 18:20]))
            link(ts_(sm[:, 24:28], sm[:, 20:24], sm[:, 18:19], par_("tau"), ALU.mult, ALU.mult))
            pairs = sm[:, 24:28].rearrange("p (r s) -> p r s", r=2)
            link(tt_(pairs, pairs, sm[:, 18:20].unsqueeze(1).to_broadcast([P, 2, 2]), ALU.mult))
            link(v_.tensor_reduce(sm[:, 20:22], pairs, AX.X, ALU.max))
            ex = sm[:, 28:32].rearrange("p (r s) -> p r s", r=2)
            tt_(ex, pairs, sm[:, 20:22].unsqueeze(2).to_broadcast([P, 2, 2]), ALU.subtract).then_inc(S["sm2_in"], 1)
            dve.wait_ge(S["sm2_exp"], 1)
            link(v_.tensor_reduce(sm[:, 20:22], ex, AX.X, ALU.add))
            link(v_.reciprocal(sm[:, 20:22], sm[:, 20:22]))
            link(tt_(ex, ex, sm[:, 20:22].unsqueeze(2).to_broadcast([P, 2, 2]), ALU.mult))
            for a in range(2):
                m = mixed[:, a * N:a * N + N]
                link(ts_(m, fp, sm[:, 29 + 2 * a:30 + 2 * a], None, ALU.mult))
                link(stt(m, feat, sm[:, 28 + 2 * a:29 + 2 * a], m, ALU.mult, ALU.add))
            link(tt_(mixed, mixed, mixed, ALU.mult))
            tt_(outf, mixed[:, 0:N], mixed[:, N:2 * N], ALU.add).then_inc(S["sum_sq"], 1)
            dve.wait_ge(S["toT_mm"], 1)
            link(v_.tensor_copy(T, ps[0]))
            dve.wait_ge(S["inv_sq"], 1)
            tt_(gatef, gated[:, 0:N], gated[:, N:2 * N], ALU.add).then_inc(S["sum_sq"], 1)
            dve.wait_ge(S["toT_mm"], 2)
            for n in range(2):
                dst = T4[:, :, :, n * CH:n * CH + CH]
                link(tt_(dst, dst, ps[1][:, n * N:n * N + N].rearrange("p (t b c) -> p t b c", t=PT, b=B), ALU.add))

            eps = 1e-5
            centre(T, t0, eps)
            r = scale_of(1)
            w = small[:, 48:64]
            link(stt(w, small[:, 128:144], 1.0 / C, r, ALU.mult, ALU.mult))
            link(tt_(w, w, r, ALU.mult))
            ts_(w, w, eps, None, ALU.add).then_inc(S["var"], 1)
            link(tt_(arr3(t0, C), arr3(ln_a, C), bc16(r), ALU.mult))
            tt_(arr3(ln_b, C), arr3(t0, C), bc16(scale_of(2)), ALU.mult).then_inc(S["ct_in"], 1)
            dve.wait_ge(S["ct_ev"], 1)
            link(v_.tensor_reduce(xpool, arr3(lnC, 16), AX.X, ALU.add))
            link(ts_(xpool, xpool, 1.0 / LM, None, ALU.mult))
            tt_(xpool_bd.rearrange("p (b n) -> p b n", b=BI), xpool.unsqueeze(1).to_broadcast([P, BI, BG * LM]),
                mask4.unsqueeze(2).to_broadcast([P, BI, BG * LM]), ALU.mult).then_inc(S["pool_in"], 1)
            for bi in range(BI):
                dve.wait_ge(S["qk_mm"], BI + bi + 1)
                v_.tensor_copy(kT[:, 512 * bi:512 * bi + 512], ps[4 + bi]).then_inc(S["k_ev"], 1)
            dve.wait_ge(S["lk_mm"], 1)
            flat = lambda a: a.rearrange("p b m -> p (b m)")
            ts_(flat(ql), ps[0][:, 0:P], DH ** -0.5, None, ALU.mult).then_inc(S["lk_ev"], 1)
            link(v_.tensor_copy(flat(kl), ps[0][:, P:2 * P]))
            tt_(kl_bd, expand16(kl), mask8_for(B), ALU.mult).then_inc(S["kl_bd"], 1)
            dve.wait_ge(S["sim2_mm"], 1)
            s2 = ps[0][:, 0:P].rearrange("p (b m) -> p b m", b=B)
            mx, sm8 = small[:, 108:116], small[:, 116:124]
            bc8 = lambda a: a.unsqueeze(2).to_broadcast([P, B, LM])
            link(v_.tensor_reduce(mx, s2, AX.X, ALU.max))
            tt_(XM, s2, bc8(mx), ALU.subtract).then_inc(S["a2_sub"], 1)
            for bi in range(BI):
                dve.wait_ge(S["sim3_mm"], bi + 1)
                v_.tensor_reduce(small[:, 80 + 2 * bi:82 + 2 * bi], arr3(ps[4 + bi], N), AX.X, ALU.max,
                                 negate=True).then_inc(S["a3_max"], 1)
            dve.wait_ge(S["a2_exp"], 1)
            link(v_.tensor_reduce(sm8, XM, AX.X, ALU.add))
            link(v_.reciprocal(sm8, sm8))
            link(tt_(XM, XM, bc8(sm8), ALU.mult))
            tt_(bdz, expand16(XM), mask8_for(B), ALU.mult).then_inc(S["x_bd"], 1)
            dve.wait_ge(S["w3_mm"], 1)
            link(v_.reciprocal(small[:, 96:104], small[:, 88:96]))
            mr = small[:, 128:192].rearrange("p (b h) -> p b h", b=B)
            link(tt_(mr, mask8.unsqueeze(1).to_broadcast([P, B, HEADS]),
                     small[:, 96:104].unsqueeze(2).to_broadcast([P, B, HEADS]), ALU.mult))
            for n in range(2):
                ins = tt_(w3_bd[:, 4 * n:4 * n + 4], ps[2 + n].rearrange("p (b h e) -> p b h e", b=4, h=HEADS),
                          mr[:, 4 * n:4 * n + 4].unsqueeze(3).to_broadcast([P, 4, HEADS, DH]), ALU.mult)
                if n:
                    ins.then_inc(S["w3_ev"], 1)
                else:
                    link(ins)
            dve.wait_ge(S["xT_ev"], 2)
            link(v_.tensor_reduce(mx, XM, AX.X, ALU.add, apply_absolute_value=True))
            link(v_.tensor_reduce(sm8, bdXT.rearrange("p b h m -> p b (h m)"), AX.X, ALU.add,
                                  apply_absolute_value=True))
            v_.tensor_reduce(small[:, 16:18], small[:, 108:124].rearrange("p (a b) -> p a b", a=2), AX.X, ALU.max
                             ).then_inc(S["cr_in"], 1)
            mx1 = small[:, 384:512]
            for bi in range(BI):
                if bi == 1:
                    dve.wait_ge(S["cr_max"], 1)
                    link(tt_(small[:, 34:35], small[:, 32:33], small[:, 33:34], ALU.mult))
                    v_.reciprocal(small[:, 34:35], small[:, 34:35]).then_inc(S["cr_in"], 1)
                dve.wait_ge(S["sim1_mm"], bi + 1)
                m = mx1[:, 32 * bi:32 * bi + 32]
                link(v_.tensor_reduce(m, arr3(ps[4 + bi], 16), AX.X, ALU.max))
                tt_(arr3(a1[:, 512 * bi:512 * bi + 512], 16), arr3(ps[4 + bi], 16),
                    m.unsqueeze(2).to_broadcast([P, 32, 16]), ALU.subtract).then_inc(S["a1_sub"], 1)
            for e, k in ((eye7, 7.0), (eye15, 15.0), (eye13, 3.25)):
                ins = ts_(e, ident, k, None, ALU.mult)
            link(ins)

            def pinv_step(it):
                for n, (k, eye) in enumerate(((-1.0, eye7), (-1.0, eye15), (-0.25, eye13))):
                    for half in range(2):
                        dve.wait_ge(S["pi_mm"], it * 10 + 1 + 2 * n + half)
                        stt(bdt[:, 4 * half:4 * half + 4].rearrange("p b h m -> p b (h m)"),
                            ps[2 * (n % 2) + half].rearrange("p (b m) -> p b m", b=4), k,
                            eye.unsqueeze(1).to_broadcast([P, 4, P]), ALU.mult, ALU.add
                            ).then_inc(S["t_ready"], 1)

            pinv_step(0)
            for bi in range(BI):
                dve.wait_ge(S["a1_exp"], bi + 1)
                r = small[:, 256 + 32 * bi:288 + 32 * bi]
                link(v_.tensor_reduce(r, arr3(a1[:, 512 * bi:512 * bi + 512], 16), AX.X, ALU.add))
                v_.reciprocal(r, r).then_inc(S["a1_sum"], 1)
            link(tt_(T, T, t0, ALU.add))
            link(tt_(arr3(T, C), arr3(T, C), row_("b_out").unsqueeze(1).to_broadcast([P, 16, C]), ALU.add))
            own.restart()
            with dve.Fori(1, PINV) as it:
                pinv_step(it)
            own.restart()
            dve.wait_ge(S["w2_mm"], 1)
            v_.tensor_copy(w2_bd[:, 4:8], ps[1].rearrange("p (b h e) -> p b h e", b=4, h=HEADS)
                           ).then_inc(S["w2_evD"], 1)
            dve.wait_ge(S["res_ev"], 2 * BI)
            for bi in range(BI):
                dve.wait_ge(S["oT_mm"], bi + 1)
                v = oT[:, 512 * bi:512 * bi + 512]
                tt_(v, v, ps[4 + bi], ALU.add).then_inc(S["oT_ev"], 1)
            dve.wait_ge(S["ao_mm"], 1)
            link(v_.memset(ps[5], 0.0))
            dve.wait_ge(S["ao_mm"], 2)
            link(tt_(T, T, ps[1], ALU.add))

            layernorm(T, t0, 1e-5, 3).then_inc(S["ct_in"], 1)
            dve.wait_ge(S["lg_mm"], 1)
            link(ts_(probs, ps[2][:, 0:N], par_("gate_b"), None, ALU.add))
            v_.tensor_reduce(small[:, 105:106], probs, AX.X, ALU.max, negate=True).then_inc(S["lg_max"], 1)
            dve.wait_ge(S["lg_exp"], 1)
            link(v_.reciprocal(small[:, 107:108], small[:, 106:107]))
            link(ts_(probs, probs, small[:, 107:108], None, ALU.mult))
            link(v_.max(small[:, 192:200], probs))
            link(v_.match_replace(probs_rest, small[:, 192:200], probs, 0.0))
            tt_(probs, probs, probs_rest, ALU.subtract).then_inc(S["topk"], 1)
            dve.wait_ge(S["mT_mm"], 1)
            v_.tensor_copy(mT.rearrange("p t e -> p (t e)"), ps[3][:, 0:N]).then_inc(S["mT_ev"], 1)
            dve.wait_ge(S["pl_mm"], 1)
            v_.tensor_copy(pooled[0:C, :].rearrange("d (e b) -> d e b", e=EXP),
                           ps[4][0:C, 0:P].rearrange("d (b e) -> d e b", b=B)).then_inc(S["pl_ev"], 1)
            link(v_.tensor_copy(stepb, keyb.rearrange("p (s o) -> p s o", o=NOPS)[:, :, 0]))
            link(stt(keyf, maskb, 2.0, flagb, ALU.mult, ALU.add))
            link(tt_(keyb, keyb, keyf, ALU.add))
            link(ts_(keyf, keyf, 0.0, float(NONE), ALU.is_equal, ALU.mult))
            link(tt_(keyb, keyb, keyf, ALU.add))
            link(v_.memset(passed, 0.0))
            dve.wait_ge(S["hid_mm"], 2)
            v_.tensor_copy(hid.rearrange("p e b -> p (e b)"), ps[6]).then_inc(S["hidT_ev"], 1)
            dve.wait_ge(S["eo_mm"], 1)
            v_.tensor_copy(eo.rearrange("o (b e) -> o e b", b=B),
                           ps[4][0:C, 0:P].rearrange("o (e b) -> o e b", e=EXP)).then_inc(S["eo_ev"], 1)
            dve.wait_ge(S["eoT_mm"], 1)
            tt_(eo_bd, ps[7][:, 0:C].unsqueeze(1).to_broadcast([P, B, C]),
                mask8.unsqueeze(2).to_broadcast([P, B, C]), ALU.mult).then_inc(S["eo_bd"], 1)
            dve.wait_ge(S["moe_mm"], 1)
            link(tt_(T, T, ps[0], ALU.add))

            layernorm(T, ZT_, 1e-5, 4).then_inc(S["ct_in"], 1)
            own.restart()
            dve.wait_ge(S["oT_mm"], BI)
            v_.tensor_copy(p_la.rearrange("p (g n) -> p g n", g=BG), ident.unsqueeze(1).to_broadcast([P, BG, P])
                           ).then_inc(S["la_pev"], 1)
            m4 = mask4.unsqueeze(1).unsqueeze(3)
            bd_view = lambda a: a.rearrange("p (g b o) -> p g b o", g=BG, b=BI)
            dve.wait_ge(S["la_g"], 1)
            for g in range(BG):
                last = stt(bd_view(g_bd)[:, g], bd_view(ps[2][:, 0:BG * P])[:, g], 1.0 / (N * LHEADS),
                           mask4.unsqueeze(2).to_broadcast([P, BI, C]), ALU.mult, ALU.mult)
            last.then_inc(S["la_gev"], 1)

            def layer(l, last_one):
                dve.wait_ge(S["la_h"], 2 * l + 2)
                v_.tensor_copy(hs[:, 1].rearrange("p j o -> p (j o)"), ps[4][:, 0:N]).then_inc(S["la_hevD"], 1)
                dve.wait_ge(S["la_r"], l + 2)
                tt_(bd_view(w_la), ps[2][:, 0:BG * C].rearrange("p (g o) -> p g o", g=BG).unsqueeze(2)
                    .to_broadcast([P, BG, BI, C]), m4.to_broadcast([P, BG, BI, C]), ALU.mult).then_inc(S["la_w"], 1)
                if last_one:
                    dve.wait_ge(S["la_p"], LAYERS)
                    v_.tensor_copy(m_la, ps[5][:, 0:BG * P]).then_inc(S["la_pev"], 1)
                    return
                dve.wait_ge(S["la_g2"], l + 1)
                v_.tensor_copy(g_bd, ps[6][:, 0:BG * P]).then_inc(S["la_gev"], 1)

            with dve.Fori(0, LAYERS - 1) as l:
                layer(l, False)
            layer(LAYERS - 1, True)
            dve.wait_ge(S["la_zm"], 1)
            link(tt_(T, T, ps[0], ALU.add))

            layernorm(T, ln_b, 1e-5, 5).then_inc(S["ct_in"], 1)
            dve.wait_ge(S["ct_in"], 4)

            def next_op(row):
                link(v_.max(top8, row))
                link(v_.max_index(op8, top8, row))
                op = dve.value_load(op8[0:1, 0:1], min_val=0, max_val=NOPS - 1)
                link(tt_(cand, keyb.rearrange("p (s o) -> p s o", o=NOPS)[:, :, bass.ds(op, 1)]
                         .rearrange("p s o -> p (s o)"), passed, ALU.add))
                link(v_.tensor_reduce(key, cand, AX.X, ALU.min))
                link(v_.tensor_copy(keyi, key))
                own.restart()
                dve.sem_inc(S["op_ev"], 1)

            next_op(ln_b[0:1, 0:NOPS])

            def step(n, k):
                fl = dve.snap(k % 4)
                ffn = dve.snap(k % 2)
                dve.wait_ge(S["h_new"], n + 1)
                dve.wait_ge(S["w_in"], (n + 1) * 32)
                with dve.If(fl >= 2):
                    tt_(w_bd.rearrange("p (w b o) -> p w b o", w=4, b=BI),
                        recA[:, HID:HID + 4 * C].rearrange("p (w o) -> p w o", w=4).unsqueeze(2)
                        .to_broadcast([P, 4, BI, C]), m4.to_broadcast([P, 4, BI, C]), ALU.mult
                        ).then_inc(S["w_bd"], 1)
                with dve.Else():
                    dve.sem_inc(S["w_bd"], 1)
                v_.tensor_copy(w2c, recB)
                v_.tensor_copy(b2c, recA[:, REC_A - 1:REC_A])
                tt_(w1_bd.rearrange("p (b h) -> p b h", b=BI),
                    recA[:, 0:HID].unsqueeze(1).to_broadcast([P, BI, HID]),
                    mask4.unsqueeze(2).to_broadcast([P, BI, HID]), ALU.mult).then_inc(S["w1_bd"], 1)
                link(ts_(passed, stepb, key, float(NONE), ALU.is_le, ALU.mult))
                dve.wait_ge(S["w1_bd"], n + 1)
                dve.sem_inc(S["w_used"], 1)
                with dve.If(fl >= 2):
                    dve.wait_ge(S["rq_mm"], 2 * n + 1)
                    for bi in range(BI):
                        ts_(rq_bd[:, bi, :], ps[7], mask4[:, bi:bi + 1], C ** -0.5, ALU.mult, ALU.mult
                            ).then_inc(S["rq_ev"], 1)
                    for b in range(B + 1):
                        if b < B:
                            dve.wait_ge(S["sc_mm"], n * B + b + 1)
                            v_.tensor_reduce(rmax[:, 2 * b:2 * b + 2], arr3(ps[b], N), AX.X, ALU.max,
                                             negate=True).then_inc(S["sc_max"], 1)
                        if b:
                            a = b - 1
                            dve.wait_ge(S["sc_exp"], n * B + a + 1)
                            r = rsum[:, 2 * a:2 * a + 2]
                            link(v_.reciprocal(r, r))
                            pb3 = arr3(pr[:, a * 512:a * 512 + 512], N)
                            tt_(pb3, pb3, r.unsqueeze(2).to_broadcast([P, 2, N]), ALU.mult).then_inc(S["sc_norm"], 1)
                    dve.wait_ge(S["ro_mm"], n + 1)
                    link(v_.tensor_copy(roC[:, 0:N], ps[0][:, 0:N]))
                    v_.tensor_copy(roC[:, N:2 * N], ps[1][:, 0:N]).then_inc(S["ro_ev"], 1)
                    dve.wait_ge(S["ry_mm"], n + 1)
                    v_.tensor_copy(hC, ps[2]).then_inc(S["rt_h"], 1)
                    dve.wait_ge(S["rt_h"], n + 1)
                    settled(dve)
                    own.restart()
                with dve.Else():
                    dve.sem_inc(S["rq_ev"], BI)
                    dve.sem_inc(S["sc_max"], B)
                    dve.sem_inc(S["sc_norm"], B)
                    dve.sem_inc(S["ro_ev"], 1)
                    dve.sem_inc(S["rt_h"], 1)
                    own.restart()
                with dve.If(ffn != 0):
                    dve.wait_ge(S["tok_mm"], n + 1)
                    ts_(f1t, ps[0][:, 0:1], w2c[:, C:C + 1], 0.0, ALU.add, ALU.max).then_inc(S["tok_ev"], 1)
                with dve.Else():
                    dve.sem_inc(S["tok_ev"], 1)
                dve.wait_ge(S["op_mm"], n + 1)
                dve.wait_ge(S["op_read"], 4 * n + 4)
                settled(dve)
                next_op(ps[0][0:1, 0:NOPS])
                with dve.If(ffn != 0):
                    dve.wait_ge(S["f2mm"], n + 1)
                    ts_(hC, ps[1], b2c, None, ALU.add).then_inc(S["h_new"], 1)
                with dve.Else():
                    dve.sem_inc(S["h_new"], 1)

            routed(dve, step)


def constants():
    c = np.zeros((P, CST_COLS), np.float32)
    p = np.arange(P)

    def put(n, a):
        c[:, CST[n][0]:CST[n][1]] = a.reshape(P, -1)

    put("ident", np.eye(P))
    put("flip", np.eye(P)[::-1])
    put("mask4", p[:, None] // 32 == np.arange(4))
    put("mask8", p[:, None] // 16 == np.arange(8))
    put("iota", np.broadcast_to(np.arange(16), (P, 16)))
    put("rep16", p[:, None] == p % EXP)
    put("mask16", p[:, None] // 16 == p[None, :] // 16)
    put("swap", (p[:, None] ^ 1) == p[None, :])
    put("eye32", p[:, None] % 32 == np.arange(C))
    k = np.arange(KK)
    t = np.arange(PT)
    y = t[None, :, None] * 8 + p[:, None, None] // 16 + k // 3 - 1
    xx = p[:, None, None] % 16 + k % 3 - 1 + 0 * t[None, :, None]
    put("base", np.stack([y, xx], -1))
    n = np.arange(N)
    ang = (np.outer(n // 16, n // 16) + np.outer(n % 16, n % 16)) % 16 * (2 * np.pi / 16)
    co, si = np.cos(ang), np.sin(ang)
    d = np.concatenate([co, -si, -co], 1).reshape(PT, P, 3 * N).transpose(1, 0, 2)
    put("dft", d)
    return c


def kernel(x, **w):
    from concourse import bacc
    from concourse.bass_utils import run_bass_kernel_spmd

    w = {k: np.asarray(v) for k, v in w.items()}

    def taps(a):
        return a.transpose(1, 2, 3, 0).reshape(C, -1)

    def words(mask):
        return np.pad(mask.view(np.uint8).reshape(1, -1, 1), ((0, 0), (0, 0), (0, 3))).view(np.int32)[:, :, 0]

    arrays = {
        "x": np.ascontiguousarray(np.asarray(x).reshape(B, C, N)),
        "cst": constants(),
        "w32": np.concatenate([
            taps(w["L0_conv_w_off"]), taps(w["L0_conv_w_dcn"]), taps(w["L1_conv_conv_w"]), w["L2_attn_w_qkv"],
            w["L2_ffn_gate_w"].T, np.stack([w["L2_attn_ln_w"], w["L2_attn_ln_b"]], 1),
            w["L3_attn_v_matrix"][:, :, 0].transpose(3, 0, 1, 2).reshape(C, -1),
            w["L3_attn_q_matrix"][:, :, 0].transpose(3, 0, 1, 2).reshape(C, -1)], 1),
        "par": np.stack([
            w["L1_conv_bn1_g"], w["L1_conv_bn1_b"], w["L1_conv_bn1_m"], w["L1_conv_bn1_v"],
            w["L1_conv_cg2_w"].reshape(CH), w["L1_conv_cg2_b"], w["L1_conv_cg1_w"].reshape(CH)]
            + [np.broadcast_to(w["L1_conv_" + n], (CH,)) for n in ("cg1_b", "cgbn_g", "cgbn_b", "cgbn_m", "cgbn_v")]
            + [np.repeat(w["L1_conv_tau"].reshape(-1), 2), w["L2_ffn_gate_b"]], 1),
        "rows": np.concatenate([w["L0_conv_b_off"], w["L2_attn_b_out"]]),
        "toep": np.pad(w["L2_attn_res_w"].reshape(HEADS, KRES),
                       ((0, 0), (2 * P - KRES // 2 - 1, TOEP_PAD - 2 * P + 1 - KRES + KRES // 2))),
        "w_out": w["L2_attn_w_out"],
        "moe_w1": np.ascontiguousarray(w["L2_ffn_weight1"].transpose(1, 0, 2)),
        "moe_w2": np.ascontiguousarray(w["L2_ffn_weight2"][:, :HID].transpose(1, 0, 2)),
        "moe_b2": w["L2_ffn_weight2"][:, HID],
        "am": words(w["L3_ffn_attn_mask"]),
        "fm": words(w["L3_ffn_ffn_mask"]),
        "keys": 4 * np.arange(NB * NOPS, dtype=np.float32).reshape(1, -1),
        "rec_a": np.concatenate([w["L3_ffn_ffn_w1"], w["L3_ffn_wq"], w["L3_ffn_wk"], w["L3_ffn_wv"], w["L3_ffn_wo"],
                                 w["L3_ffn_ffn_b2"][..., None]], -1).reshape(NB * NOPS, C, REC_A),
        "rec_b": np.concatenate([w["L3_ffn_ffn_w2"], w["L3_ffn_ffn_b1"][..., None]], -1
                                ).reshape(NB * NOPS, HID, REC_B),
    }
    arrays = {k: np.ascontiguousarray(a) for k, a in arrays.items()}
    nc = bacc.Bacc("TRN2", target_bir_lowering=False, num_devices=1)
    args = [nc.dram_tensor(k, a.shape, mybir.dt.from_np(a.dtype), kind="ExternalInput").ap()
            for k, a in arrays.items()]
    out = nc.dram_tensor("out", (B, C, N), F32, kind="ExternalOutput").ap()
    build(nc, *args, out)
    r = run_bass_kernel_spmd(nc, [arrays], core_ids=[0])
    return r.results[0]["out"].reshape(B, C, HH, WW)
```
